# Optimizing a Trainium2 kernel written in Bass

```python
import numpy as np
import jax
import jax.numpy as jnp

def _softmax(x, axis=-1):
    return jax.nn.softmax(x, axis=axis)

def _gelu(x):
    return jax.nn.gelu(x, approximate=True)

def _silu(x):
    return jax.nn.silu(x)

def _sigmoid(x):
    return jax.nn.sigmoid(x)

def _layernorm(x, axis=-1, eps=1e-05):
    m = jnp.mean(x, axis=axis, keepdims=True)
    v = jnp.var(x, axis=axis, keepdims=True)
    return (x - m) / jnp.sqrt(v + eps)

def _scatter_add(tgt, idx, src, axis=0):
    return tgt.at[idx].add(src)

def _segment_sum(src, seg, n):
    return jax.ops.segment_sum(src, seg, n)
kernel_name = 'mk_gnn_preln_d4_gnn_r16_f1f02d'

def setup_inputs(seed: int=0):
    np.random.seed(seed)
    _w = jnp.asarray

    def _rec_inputs():
        import jax
        import jax.numpy as jnp
        _gk = jax.random.key(seed)
        x = 3.202e-06 + 0.05001 * jax.random.normal(jax.random.fold_in(_gk, 1), (6250, 128), jnp.float32)
        src = jax.random.randint(jax.random.fold_in(_gk, 2), (100000,), 0, 6250, jnp.int32)
        dst = jax.random.randint(jax.random.fold_in(_gk, 3), (100000,), 0, 6250, jnp.int32)
        _o = jnp.argsort(dst, stable=True)
        src = src[_o]
        dst = dst[_o]
        edge_attr_128 = 9.41057e-06 + 1 * jax.random.normal(jax.random.fold_in(_gk, 12), (100000, 128), jnp.float32)
        edge_type_2 = jax.random.randint(jax.random.fold_in(_gk, 14), (100000,), 0, 2, jnp.int32)
        edge_type_200 = jax.random.randint(jax.random.fold_in(_gk, 15), (100000,), 0, 200, jnp.int32)
        return (x, src, dst, edge_attr_128, edge_type_2, edge_type_200)
    x, src, dst, edge_attr_128, edge_type_2, edge_type_200 = _rec_inputs()

    def _L0_gnn_setup():
        import jax, jax.numpy as jnp
        import numpy as np
        N_ENT = 6250
        N_REL = 200
        N_EDGE = 40000
        D = 128

        def _wgc_layer(h, W, rel_w, heads, rels, tails):
            msg = rel_w[rels][:, None] * h[tails]
            agg = jax.ops.segment_sum(msg, heads, num_segments=N_ENT) + h
            return jnp.tanh(agg @ W)
        key = jax.random.key(seed)
        ks = jax.random.split(key, 12)
        return {'heads': jax.random.randint(ks[0], (N_EDGE,), 0, N_ENT, dtype=jnp.int32), 'rels': jax.random.randint(ks[1], (N_EDGE,), 0, N_REL, dtype=jnp.int32), 'tails': jax.random.randint(ks[2], (N_EDGE,), 0, N_ENT, dtype=jnp.int32), 'em_entity': jax.random.normal(ks[3], (N_ENT, D), jnp.float32) * 0.05, 'W1': jax.random.normal(ks[4], (D, D), jnp.float32) * 0.05, 'W2': jax.random.normal(ks[5], (D, D), jnp.float32) * 0.05, 'W3': jax.random.normal(ks[6], (D, D), jnp.float32) * 0.05, 're_attention_weight': jax.random.normal(ks[7], (N_REL,), jnp.float32), 'u': jax.random.normal(ks[8], (3 * D,), jnp.float32) * 0.05, 'en_weight': jax.random.normal(ks[9], (D, D), jnp.float32) * 0.05, 're_weight': jax.random.normal(ks[10], (D, D), jnp.float32) * 0.05, 're_specific_attention': jax.random.normal(ks[11], (D,), jnp.float32) * 0.05}
    _L0_gnn_all = _L0_gnn_setup()
    _L0_gnn_in = {k: v for k, v in _L0_gnn_all.items() if k in ('W1', 'W2', 'W3', 're_attention_weight', 'u', 'en_weight', 're_weight', 're_specific_attention')}
    del _L0_gnn_all

    def _L1_gnn_setup():
        import jax, jax.numpy as jnp
        import numpy as np
        N, E, DIN, H, C = (6250, 100000, 128, 8, 16)
        NEG_SLOPE = 0.2
        key = jax.random.key(seed)
        k1, k2, k3, k4, k5, k6 = jax.random.split(key, 6)
        x = jax.random.normal(k1, (N, DIN), dtype=jnp.float32)
        src = jax.random.randint(k2, (E,), 0, N, dtype=jnp.int64)
        dst = jax.random.randint(k3, (E,), 0, N, dtype=jnp.int64)
        dst = jnp.where(src == dst, (dst + 1) % N, dst)
        edge_index = jnp.stack([src, dst], axis=0)
        W = jax.random.normal(k4, (DIN, H * C), dtype=jnp.float32) * (1.0 / np.sqrt(DIN))
        att_src = jax.random.normal(k5, (H, C), dtype=jnp.float32) * (1.0 / np.sqrt(C))
        att_dst = jax.random.normal(k6, (H, C), dtype=jnp.float32) * (1.0 / np.sqrt(C))
        bias = jnp.zeros((H * C,), dtype=jnp.float32)
        return {'x': x, 'edge_index': edge_index, 'W': W, 'att_src': att_src, 'att_dst': att_dst, 'bias': bias}
    _L1_gnn_all = _L1_gnn_setup()
    _L1_gnn_in = {k: v for k, v in _L1_gnn_all.items() if k in ('W', 'att_src', 'att_dst', 'bias')}
    del _L1_gnn_all

    def _L2_gnn_setup():
        import jax, jax.numpy as jnp
        import numpy as np
        N_NODES = 6250
        N_EDGES = 100000
        HIDDEN = 128
        key = jax.random.key(seed)
        ks = jax.random.split(key, 7)
        s = 1.0 / np.sqrt(HIDDEN)
        return {'x': jax.random.normal(ks[0], (N_NODES, HIDDEN), dtype=jnp.float32), 'edge_index': jax.random.randint(ks[1], (2, N_EDGES), 0, N_NODES, dtype=jnp.int64), 'edge_attr': jax.random.normal(ks[2], (N_EDGES, HIDDEN), dtype=jnp.float32), 'w_self_W': jax.random.normal(ks[3], (HIDDEN, HIDDEN), dtype=jnp.float32) * s, 'w_self_b': jax.random.normal(ks[4], (HIDDEN,), dtype=jnp.float32) * s, 'w_nei_W': jax.random.normal(ks[5], (HIDDEN, HIDDEN), dtype=jnp.float32) * s, 'w_edge_W': jax.random.normal(ks[6], (HIDDEN, HIDDEN), dtype=jnp.float32) * s}
    _L2_gnn_all = _L2_gnn_setup()
    _L2_gnn_in = {k: v for k, v in _L2_gnn_all.items() if k in ('w_self_W', 'w_self_b', 'w_nei_W', 'w_edge_W')}
    del _L2_gnn_all

    def _L3_gnn_setup():
        import jax, jax.numpy as jnp
        import numpy as np
        IN_DIM = 128
        OUT_DIM = 128
        N_NODES = 625
        N_EDGES = 40000
        key = jax.random.key(seed)
        ks = jax.random.split(key, 9)
        X = jax.random.normal(ks[0], (N_NODES, IN_DIM), dtype=jnp.float32)
        edge_index = jax.random.randint(ks[1], (2, N_EDGES), 0, N_NODES, dtype=jnp.int64)
        edge_types = jax.random.randint(ks[2], (N_EDGES,), 0, 2, dtype=jnp.int64)
        s = 1.0 / np.sqrt(IN_DIM)
        W_data = jax.random.uniform(ks[3], (OUT_DIM, IN_DIM), minval=-s, maxval=s, dtype=jnp.float32)
        b_data = jax.random.uniform(ks[4], (OUT_DIM,), minval=-s, maxval=s, dtype=jnp.float32)
        W_control = jax.random.uniform(ks[5], (OUT_DIM, IN_DIM), minval=-s, maxval=s, dtype=jnp.float32)
        b_control = jax.random.uniform(ks[6], (OUT_DIM,), minval=-s, maxval=s, dtype=jnp.float32)
        W_self = jax.random.uniform(ks[7], (OUT_DIM, IN_DIM), minval=-s, maxval=s, dtype=jnp.float32)
        b_self = jax.random.uniform(ks[8], (OUT_DIM,), minval=-s, maxval=s, dtype=jnp.float32)
        return {'X': X, 'edge_index': edge_index, 'edge_types': edge_types, 'W_data': W_data, 'b_data': b_data, 'W_control': W_control, 'b_control': b_control, 'W_self': W_self, 'b_self': b_self}
    _L3_gnn_all = _L3_gnn_setup()
    _L3_gnn_in = {k: v for k, v in _L3_gnn_all.items() if k in ('W_data', 'b_data', 'W_control', 'b_control', 'W_self', 'b_self')}
    del _L3_gnn_all
    return {'x': x, 'src': src, 'dst': dst, 'edge_attr_128': edge_attr_128, 'edge_type_2': edge_type_2, 'edge_type_200': edge_type_200, 'L0_gnn_W1': _L0_gnn_in['W1'], 'L0_gnn_W2': _L0_gnn_in['W2'], 'L0_gnn_W3': _L0_gnn_in['W3'], 'L0_gnn_re_attention_weight': _L0_gnn_in['re_attention_weight'], 'L0_gnn_u': _L0_gnn_in['u'], 'L0_gnn_en_weight': _L0_gnn_in['en_weight'], 'L0_gnn_re_weight': _L0_gnn_in['re_weight'], 'L0_gnn_re_specific_attention': _L0_gnn_in['re_specific_attention'], 'L1_gnn_W': _L1_gnn_in['W'], 'L1_gnn_att_src': _L1_gnn_in['att_src'], 'L1_gnn_att_dst': _L1_gnn_in['att_dst'], 'L1_gnn_bias': _L1_gnn_in['bias'], 'L2_gnn_w_self_W': _L2_gnn_in['w_self_W'], 'L2_gnn_w_self_b': _L2_gnn_in['w_self_b'], 'L2_gnn_w_nei_W': _L2_gnn_in['w_nei_W'], 'L2_gnn_w_edge_W': _L2_gnn_in['w_edge_W'], 'L3_gnn_W_data': _L3_gnn_in['W_data'], 'L3_gnn_b_data': _L3_gnn_in['b_data'], 'L3_gnn_W_control': _L3_gnn_in['W_control'], 'L3_gnn_b_control': _L3_gnn_in['b_control'], 'L3_gnn_W_self': _L3_gnn_in['W_self'], 'L3_gnn_b_self': _L3_gnn_in['b_self']}

def reference(x, src, dst, edge_attr_128, edge_type_2, edge_type_200, L0_gnn_W1, L0_gnn_W2, L0_gnn_W3, L0_gnn_re_attention_weight, L0_gnn_u, L0_gnn_en_weight, L0_gnn_re_weight, L0_gnn_re_specific_attention, L1_gnn_W, L1_gnn_att_src, L1_gnn_att_dst, L1_gnn_bias, L2_gnn_w_self_W, L2_gnn_w_self_b, L2_gnn_w_nei_W, L2_gnn_w_edge_W, L3_gnn_W_data, L3_gnn_b_data, L3_gnn_W_control, L3_gnn_b_control, L3_gnn_W_self, L3_gnn_b_self):
    import jax
    import jax.numpy as jnp

    def _L0_gnn_ref(heads, rels, tails, em_entity, W1, W2, W3, re_attention_weight, u, en_weight, re_weight, re_specific_attention):
        import jax, jax.numpy as jnp
        import numpy as np
        N_ENT = 6250
        N_REL = 200
        N_EDGE = 40000
        D = 128

        def _wgc_layer(h, W, rel_w, heads, rels, tails):
            msg = rel_w[rels][:, None] * h[tails]
            agg = jax.ops.segment_sum(msg, heads, num_segments=N_ENT) + h
            return jnp.tanh(agg @ W)
        x = _wgc_layer(em_entity, W1, re_attention_weight, heads, rels, tails)
        x = _wgc_layer(x, W2, re_attention_weight, heads, rels, tails)
        x = _wgc_layer(x, W3, re_attention_weight, heads, rels, tails)
        u1, u2, u3 = (u[:D], u[D:2 * D], u[2 * D:])
        xh = x @ en_weight.T
        rel_term = jnp.dot(re_weight @ re_specific_attention, u2)
        e = jax.nn.leaky_relu(xh[heads] @ u1 + xh[tails] @ u3 + rel_term)
        alpha = jax.nn.softmax(e)
        out = jax.ops.segment_sum(alpha[:, None] * x[tails], heads, num_segments=N_ENT)
        return out

    def _L1_gnn_ref(x, edge_index, W, att_src, att_dst, bias):
        import jax, jax.numpy as jnp
        import numpy as np
        N, E, DIN, H, C = (6250, 100000, 128, 8, 16)
        NEG_SLOPE = 0.2
        n = x.shape[0]
        h = (x @ W).reshape(n, H, C)
        a_src = jnp.einsum('nhc,hc->nh', h, att_src)
        a_dst = jnp.einsum('nhc,hc->nh', h, att_dst)
        loop = jnp.arange(n, dtype=edge_index.dtype)
        src = jnp.concatenate([edge_index[0], loop])
        dst = jnp.concatenate([edge_index[1], loop])
        e = jax.nn.leaky_relu(a_src[src] + a_dst[dst], NEG_SLOPE)
        m = jax.ops.segment_max(e, dst, num_segments=n)
        m = jnp.where(jnp.isfinite(m), m, 0.0)
        ex = jnp.exp(e - m[dst])
        denom = jax.ops.segment_sum(ex, dst, num_segments=n)
        alpha = ex / denom[dst]
        msg = h[src] * alpha[:, :, None]
        out = jax.ops.segment_sum(msg, dst, num_segments=n)
        return out.reshape(n, H * C) + bias

    def _L2_gnn_ref(x, edge_index, edge_attr, w_self_W, w_self_b, w_nei_W, w_edge_W):
        import jax, jax.numpy as jnp
        import numpy as np
        N_NODES = 6250
        N_EDGES = 100000
        HIDDEN = 128
        src, dst = (edge_index[0], edge_index[1])
        n = x.shape[0]
        x_nei = x @ w_nei_W.T
        msg = x_nei[src] + edge_attr @ w_edge_W.T
        out = jax.ops.segment_sum(msg, dst, num_segments=n)
        deg = jax.ops.segment_sum(jnp.ones_like(dst, dtype=x.dtype), dst, num_segments=n)
        deg = jnp.maximum(deg, 1.0)[:, None]
        return jax.nn.relu(x @ w_self_W.T + w_self_b + out / deg)

    def _L3_gnn_ref(X, edge_index, edge_types, W_data, b_data, W_control, b_control, W_self, b_self):
        import jax, jax.numpy as jnp
        import numpy as np
        IN_DIM = 128
        OUT_DIM = 128
        N_NODES = 625
        N_EDGES = 40000
        src, dst = (edge_index[0], edge_index[1])
        Xs = X[src]
        m_data = Xs @ W_data.T + b_data
        m_ctrl = Xs @ W_control.T + b_control
        msg = jnp.where((edge_types == 0)[:, None], m_data, m_ctrl)
        agg = jax.ops.segment_sum(msg, dst, num_segments=X.shape[0])
        out = agg + (X @ W_self.T + b_self)
        return jax.nn.relu(out)
    edge_index = jnp.stack([src, dst])
    h = jnp.maximum(_layernorm(x, axis=-1), 0.0)
    x = x + _L0_gnn_ref(src, edge_type_200, dst, h, L0_gnn_W1, L0_gnn_W2, L0_gnn_W3, L0_gnn_re_attention_weight, L0_gnn_u, L0_gnn_en_weight, L0_gnn_re_weight, L0_gnn_re_specific_attention)
    h = jnp.maximum(_layernorm(x, axis=-1), 0.0)
    x = x + _L1_gnn_ref(h, edge_index, L1_gnn_W, L1_gnn_att_src, L1_gnn_att_dst, L1_gnn_bias)
    h = jnp.maximum(_layernorm(x, axis=-1), 0.0)
    x = x + _L2_gnn_ref(h, edge_index, edge_attr_128, L2_gnn_w_self_W, L2_gnn_w_self_b, L2_gnn_w_nei_W, L2_gnn_w_edge_W)
    h = jnp.maximum(_layernorm(x, axis=-1), 0.0)
    x = x + _L3_gnn_ref(h, edge_index, edge_type_2, L3_gnn_W_data, L3_gnn_b_data, L3_gnn_W_control, L3_gnn_b_control, L3_gnn_W_self, L3_gnn_b_self)
    return x

_drawn_inputs = setup_inputs


def setup_inputs(seed=0):
    import zlib

    import numpy as np

    out = dict(_drawn_inputs(seed))
    spreads = {'L1_gnn_bias': (0.0, 0.1)}
    factors = {'L0_gnn_W1': 64.0,
     'L0_gnn_W2': 64.0,
     'L0_gnn_W3': 64.0,
     'L0_gnn_re_attention_weight': 64.0,
     'L0_gnn_u': 64.0,
     'L0_gnn_en_weight': 64.0,
     'L0_gnn_re_weight': 8.0,
     'L0_gnn_re_specific_attention': 64.0,
     'L3_gnn_b_self': 6.62}
    for name, (base, spread) in spreads.items():
        noise = np.random.default_rng([zlib.crc32(name.encode()), seed]).standard_normal(out[name].shape)
        drawn = base * np.exp(spread * noise) if base else spread * noise
        out[name] = jnp.asarray(drawn.astype(out[name].dtype))
    for name, factor in factors.items():
        out[name] = (out[name] * factor).astype(out[name].dtype)
    return out
```

```python
from contextlib import ExitStack

import concourse.bass as bass
from concourse import mybir

ALU = mybir.AluOpType
ACT = mybir.ActivationFunctionType
F32 = mybir.dt.float32
BF16 = mybir.dt.bfloat16
I32 = mybir.dt.int32
I16 = mybir.dt.int16
AX_X = mybir.AxisListType.X
RMAX = bass.bass_isa.ReduceOp.max
RADD = bass.bass_isa.ReduceOp.add

N = 6250
D = 128
E = 100000
NREL = 200
EP, EC = 125, 800
NT = 49
NP = NT * 128
NW = 25
WN = 256
NTL = E // 128 + NW
NTB = 7
TG, TJ = 16, 51
BIG = 1.0e30
PAD = 256 << 21
LAST = E - 128


class Queues:

    def __init__(self, sems):
        self.names = ("v", "a", "t", "p", "s")
        self.items = {n: [] for n in self.names}
        self.sem = dict(sems)
        self.count = {n: 0 for n in self.names}
        self.seen = {n: {} for n in self.names}
        self.dcount = {}

    def wait(self, eng, *tokens):
        for tok in tokens:
            if tok is None:
                continue
            if isinstance(tok, list):
                self.wait(eng, *tok)
                continue
            sem, value = tok
            key = id(sem)
            if self.seen[eng].get(key, 0) >= value:
                continue
            self.seen[eng][key] = value
            self.items[eng].append(lambda e, s=sem, v=value: e.wait_ge(s, v))

    def op(self, eng, fn, *tokens):
        self.wait(eng, *tokens)
        self.count[eng] += 1
        sem = self.sem[eng]
        self.items[eng].append(lambda e: fn(e).then_inc(sem, 1))
        return (sem, self.count[eng])

    def quiet(self, eng, fn, *tokens):
        self.wait(eng, *tokens)
        self.items[eng].append(fn)

    def dma(self, eng, sem, fn, *tokens):
        self.wait(eng, *tokens)
        self.dcount[id(sem)] = self.dcount.get(id(sem), 0) + 16
        self.items[eng].append(lambda e: fn(e).then_inc(sem, 16))
        return (sem, self.dcount[id(sem)])

    def now(self, eng):
        return (self.sem[eng], self.count[eng])


def program(nc, x, src, dst, edge_attr_128, edge_type_2, edge_type_200,
            W1, W2, W3, relw, u, en_w, re_w, re_att,
            gW, att_src, att_dst, gbias,
            w_self_W, w_self_b, w_nei_W, w_edge_W,
            W_data, b_data, W_control, b_control, W_self, b_self, out, stop_at=99):
    ctx = ExitStack()
    with ctx:
        def sb(name, shape, dt=F32):
            return ctx.enter_context(nc.sbuf_tensor(name, shape, dt))

        def sem(name):
            return ctx.enter_context(nc.semaphore(name))

        def dram(name, shape, dt=F32):
            return nc.dram_tensor(name, shape, dt).ap()

        XS = sb("XS", [128, NT, D])
        HN = sb("HN", [128, NT, 144])
        RA = sb("RA", [128, 6528])
        RB = sb("RB", [128, NW * 290])
        RC = sb("RC", [128, 6528])
        RING = sb("RING", [128, 34, 145])
        GR = RING[:, :, :].rearrange("p a b -> p (a b)")
        IDX0 = sb("IDX0", [128, NTB * 128], I32)
        KEY0 = sb("KEY0", [128, NTB * 128])
        WE0 = sb("WE0", [128, NTB * 128])
        SC1 = sb("SC1", [128, NTB * 128])
        SC2 = sb("SC2", [128, NTB * 128])
        IDX1 = sb("IDX1", [128, NTB * 128], I32)
        KEY1 = sb("KEY1", [128, NTB * 128])
        OH = sb("OH", [128, 4, WN])
        OHB = sb("OHB", [128, 4, WN], BF16)
        OHT = sb("OHT", [128, 4, WN], BF16)
        WTAB0 = sb("WTAB0", [1, NTB * 128], I16)
        WTAB1 = sb("WTAB1", [1, NTB * 128], I16)
        IOTA = sb("IOTA", [128, WN])
        IOTAB = sb("IOTAB", [128, WN], BF16)
        IOI = sb("IOI", [128, WN], I32)
        IDENT = sb("IDENT", [128, 128])
        IDENTB = sb("IDENTB", [128, 128], BF16)
        TRI = sb("TRI", [128, 128])
        ONES = sb("ONES", [128, 128])
        BD = sb("BD", [128, 8])
        WT = sb("WT", [128, 12, 128])
        RHS1 = sb("RHS1", [128, 144])
        ADC = sb("ADC", [128, 16])
        COLS = sb("COLS", [128, 16])
        RELB = sb("RELB", [128, NREL])
        BIAS1 = sb("BIAS1", [128, D])
        ROWS = sb("ROWS", [1, 512])
        AD3 = sb("AD3", [128, 50, 24], BF16)
        ST = sb("ST", [128, 640])
        SI = sb("SI", [128, 64], I32)
        RDEG = sb("RDEG", [128, NT])

        PS = [ctx.enter_context(nc.psum_tensor(f"PS{i}", [128, 512], F32)) for i in range(8)]

        TAB = [dram(f"TAB{i}", (NP, D)) for i in range(3)]
        TABQ = dram("TABQ", (NP, 132))
        TABG = dram("TABG", (NP, 136))
        TAB2 = dram("TABN", (NP, D))
        TAB3 = dram("TABM", (2 * NP, D))
        SPA = dram("SPA", (128, NTL, 132))
        SPB = dram("SPB", (128, NTL, 136))
        REC0 = dram("REC0", (NTB * 128 * 128, 1), I32)
        REC1 = dram("REC1", (E + 128, 1), I32)
        RECA = dram("RECA", (E, 2), I32)
        RECB = dram("RECB", (E, 2), I32)
        EA = dram("EA", (E, D))
        TW0 = dram("TW0", (NTB, 128), I16)
        TW1 = dram("TW1", (NTB, 128), I16)
        TBT = dram("TBT", (2, NTB, 128), I32)
        KFD = dram("KFD", (128, NTB * 128))
        I3D = dram("I3D", (128, NTB * 128), I32)
        ATTD = dram("ATTD", (128, NW * WN))

        q = Queues({n: sem(f"e_{n}") for n in ("v", "a", "t", "p", "s")})
        s_in = [sem(f"in{i}") for i in range(40)]
        s_g = [sem(f"g{i}") for i in range(34)]
        s_h = [sem(f"h{i}") for i in range(16)]
        s_m = [sem(f"m{i}") for i in range(24)]
        s_r0, s_r1 = sem("r0"), sem("r1")
        s_fin = sem("fin")
        s_join = sem("join")

        def V(fn, *w):
            return q.op("v", fn, *w)

        def A(fn, *w):
            return q.op("a", fn, *w)

        def T(fn, *w):
            return q.op("t", fn, *w)

        def P(fn, *w):
            return q.op("p", fn, *w)

        def vv():
            return q.now("v")

        def VC(fn, *w):
            return q.op("v", fn, q.now("v"), *w)

        def load(i, dst_ap, src_ap, *w, eng="s"):
            return q.dma(eng, s_in[i], lambda e: e.dma_start(dst_ap, src_ap), *w)

        def affine(t_, op, fill, pattern, cm, base, *w):
            return P(lambda e: e.affine_select(out=t_, in_=t_, compare_op=op, fill=fill, base=base,
                                               pattern=pattern, channel_multiplier=cm), *w)

        c0 = P(lambda e: e.memset(IDENT[:, :], 0.0))
        c1 = P(lambda e: e.memset(TRI[:, :], 0.0))
        c_ones = P(lambda e: e.memset(ONES[:, :], 1.0))
        c2 = P(lambda e: e.memset(BD[:, :], 1.0))
        c_id = affine(IDENT[:, :], ALU.not_equal, 1.0, [[-1, 128]], 1, 0, c2)
        c_tri = affine(TRI[:, :], ALU.is_ge, 1.0, [[-1, 128]], 1, 0, c2)
        c3 = affine(BD[:, :], ALU.is_ge, 0.0, [[-16, 8]], 1, 0, c2)
        c_bd = affine(BD[:, :], ALU.is_ge, 0.0, [[16, 8]], -1, 15, c3)
        c4 = P(lambda e: e.iota(IOI[:, :], pattern=[[1, WN]], base=0, channel_multiplier=0))
        c_tt = P(lambda e: e.iota(SI[:, 0:NTB], pattern=[[128, NTB]], base=0, channel_multiplier=1))
        c5 = P(lambda e: e.tensor_copy(IOTA[:, :], IOI[:, :]), c4)
        c_io = P(lambda e: e.tensor_copy(IOTAB[:, :], IOI[:, :]), c4)
        c_idb = P(lambda e: e.tensor_copy(IDENTB[:, :], IDENT[:, :]), c_id)

        def edges(ap):
            return ap.rearrange("(p c) -> p c", c=EC)

        def slot(k, dt=I32):
            v = RA[0:EP, k * EC:(k + 1) * EC]
            return v if dt is F32 else v.bitcast(dt)

        def slotb(k, dt=I32):
            v = RC[0:EP, k * EC:(k + 1) * EC]
            return v if dt is F32 else v.bitcast(dt)

        l_src = load(0, slot(0), edges(src))
        l_dst = load(1, slot(1), edges(dst))
        l_nx = load(2, slotb(0)[0:124, :], dst[1:1 + 124 * EC].rearrange("(p c) -> p c", c=EC), eng="a")
        l_nx1 = load(3, slotb(0)[124:125, 0:EC - 1], dst[1 + 124 * EC:E].rearrange("(p c) -> p c", p=1), eng="a")
        l_nx2 = load(4, slotb(0)[124:125, EC - 1:EC], dst[E - 1:E].rearrange("(p c) -> p c", p=1), eng="a")
        l_t200 = load(5, slot(2), edges(edge_type_200))
        l_t2 = load(6, slot(3), edges(edge_type_2))
        m_x = P(lambda e: e.memset(XS[:, NT - 1, :], 0.0))
        l_x = load(7, XS[:, 0:NT - 1, :], x[0:48 * 128, :].rearrange("(t p) d -> p t d", p=128))
        l_x2 = load(8, XS[0:N - 48 * 128, NT - 1, :], x[48 * 128:N, :], m_x)

        names = [W1, W2, W3, en_w, re_w, gW, w_self_W, w_nei_W, w_edge_W, W_data, W_control, W_self]
        l_w = [load(9 + i, WT[:, i, :], a, eng="a") for i, a in enumerate(names)]
        (iW1, iW2, iW3, iEN, iRE, iGW, iSS, iNE, iED, iDA, iCO, iSE) = range(12)
        l_u = [load(i, COLS[:, k:k + 1], u[k * 128:(k + 1) * 128].rearrange("(p k) -> p k", k=1), eng="a")
               for k, i in enumerate((21, 35, 36))]
        l_ra = load(22, COLS[:, 3:4], re_att.rearrange("(p k) -> p k", k=1), eng="a")
        l_as = load(23, COLS[:, 4:5], att_src.rearrange("h (c k) -> (h c) k", k=1), eng="a")
        l_ad = load(24, COLS[:, 5:6], att_dst.rearrange("h (c k) -> (h c) k", k=1), eng="a")
        l_rel = load(25, RELB[:, :], relw.rearrange("(a n) -> a n", a=1).to_broadcast([128, NREL]), eng="a")
        l_gb = load(26, BIAS1[:, :], gbias.rearrange("(a n) -> a n", a=1).to_broadcast([128, D]), eng="a")
        l_b1 = load(27, ROWS[:, 0:128], w_self_b.rearrange("(a n) -> a n", a=1), eng="a")
        l_b2 = load(28, ROWS[:, 128:256], b_data.rearrange("(a n) -> a n", a=1), eng="a")
        l_b3 = load(29, ROWS[:, 256:384], b_control.rearrange("(a n) -> a n", a=1), eng="a")
        l_b4 = load(30, ROWS[:, 384:512], b_self.rearrange("(a n) -> a n", a=1), eng="a")

        m_pad = P(lambda e: e.memset(SC2[:, :].bitcast(I32), PAD))
        pads = []
        for b in range(NTB):
            def put(b=b):
                return q.dma("s", s_m[0], lambda e: e.dma_start(
                    REC0[b * 16384:(b + 1) * 16384, :].rearrange("(p l) o -> p (l o)", l=128),
                    SC2[:, 0:128].bitcast(I32)), m_pad)
            pads.append(put())
        d_pad = pads[-1]
        m_pad1 = P(lambda e: e.memset(SC2[0:1, 128:256].bitcast(I32), 8191 << 14), m_pad)
        d_pad1 = q.dma("s", s_m[1], lambda e: e.dma_start(
            REC1[E:E + 128, :].rearrange("(a l) o -> a (l o)", a=1), SC2[0:1, 128:256].bitcast(I32)), m_pad1)

        def cst(eng, *toks):
            q.wait(eng, *toks)

        def place(key, nb, padded, msk, scn, pos, posi, w0, tot_out, work, base_out=None):
            cnt, offs, tmp, tot = (work[:, 32 * k:32 * k + nb] for k in range(4))
            cum = work[:, 128:128 + nb]
            cols = []
            V(lambda e: e.memset(work[:, :], 0.0))
            for b in range(nb):
                def count(b=b):
                    return V(lambda e: e.tensor_scalar(msk[b % 2], key, float(b), None, ALU.is_equal, ALU.add,
                                                       accum_out=cnt[0:EP, b:b + 1]),
                             w0, q.now("v"))
                last = count()
            m1 = T(lambda e: e.matmul(PS[0][:, 0:nb], TRI[0:EP, :], cnt[0:EP, :], start=True, stop=True),
                   last, c_tri, c_idb)
            m2 = T(lambda e: e.matmul(PS[1][:, 0:nb], ONES[0:EP, :], cnt[0:EP, :], start=True, stop=True))
            V(lambda e: e.tensor_copy(tot, PS[1][:, 0:nb]), m2)
            VC(lambda e: e.tensor_copy(tmp, tot))
            if padded:
                ti = SI[:, 8:8 + nb]
                VC(lambda e: e.tensor_scalar(ti, tot, 127.0, None, ALU.add))
                VC(lambda e: e.tensor_scalar(ti, ti, 7, None, ALU.arith_shift_right))
                VC(lambda e: e.tensor_copy(tmp, ti))
            VC(lambda e: e.tensor_tensor_scan(cum, ONES[:, 0:nb], tmp, 0.0, ALU.mult, ALU.add))
            mul = 128.0 if padded else 1.0
            VC(lambda e: e.tensor_tensor(tmp, cum, tmp, ALU.subtract))
            VC(lambda e: e.tensor_scalar(tmp, tmp, mul, -1.0, ALU.mult, ALU.add))
            VC(lambda e: e.tensor_tensor(offs, tmp, PS[0][:, 0:nb], ALU.add), m1)
            for b in range(nb):
                def one(b=b):
                    k = b % 2
                    V(lambda e: e.tensor_scalar(msk[k].bitcast(I32), key, float(b), None, ALU.is_equal), q.now("v"))
                    VC(lambda e: e.tensor_tensor_scan(scn, work2[0:EP, :], msk[k].bitcast(I32),
                                                      offs[0:EP, b:b + 1], ALU.mult, ALU.add))
                    return VC(lambda e: e.copy_predicated(pos, msk[k].bitcast(I32), scn))
                one()
            return VC(lambda e: e.tensor_copy(posi, pos)), cum, tot

        work2 = RING[:, 0:6, :].rearrange("p a b -> p (a b)")[:, 0:EC]
        ringf = RING[:, 6:34, :].rearrange("p a b -> p (a b)")

        def rs(k):
            return ringf[0:EP, k * EC:(k + 1) * EC]

        V(lambda e: e.memset(work2, 1.0))
        wk, ws_, pos0 = rs(0), rs(1), rs(2)
        msk = [slotb(1, F32), slotb(2, F32)]
        wi = slotb(3)
        t_win = VC(lambda e: e.tensor_scalar(wi, slot(0), 8, None, ALU.arith_shift_right), l_src)
        t_key = VC(lambda e: e.tensor_copy(wk, wi))
        work0 = ST[:, 0:160]
        VC(lambda e: e.memset(pos0, 0.0))
        posi0 = slotb(4)
        t_pos0, cum0, tot0 = place(wk, NW, True, msk, ws_, pos0, posi0, [c_ones, t_key], None, work0)
        v0 = slotb(5)
        VC(lambda e: e.tensor_scalar(v0, slot(0), 255, 21, ALU.bitwise_and, ALU.logical_shift_left))
        VC(lambda e: e.tensor_scalar(wi, slot(1), 8, None, ALU.logical_shift_left), l_dst)
        VC(lambda e: e.tensor_tensor(v0, v0, wi, ALU.bitwise_or))
        t_v0 = VC(lambda e: e.tensor_tensor(v0, v0, slot(2), ALU.bitwise_or), l_t200)
        v1 = slot(4)
        VC(lambda e: e.tensor_scalar(wi, slot(3), 0.0, None, ALU.not_equal), l_t2)
        VC(lambda e: e.tensor_scalar(v1, slot(1), 14, None, ALU.logical_shift_left))
        VC(lambda e: e.tensor_tensor(v1, v1, wi, ALU.bitwise_or))
        VC(lambda e: e.tensor_scalar(wi, slot(0), 1, None, ALU.logical_shift_left))
        t_v1 = VC(lambda e: e.tensor_tensor(v1, v1, wi, ALU.bitwise_or))
        d_v1 = q.dma("s", s_m[2], lambda e: e.dma_start(
            REC1[0:E, :].rearrange("(p c) o -> p (c o)", c=EC), v1), t_v1)
        fl = SI[0:EP, 40:41]
        FLG = SI[:, 41:42]
        VC(lambda e: e.tensor_tensor(wi, slotb(0), slot(1), ALU.is_lt), l_nx, l_nx1, l_nx2)
        VC(lambda e: e.memset(ST[:, 620:621], 0.0))
        t_fl = VC(lambda e: e.tensor_reduce(ST[0:EP, 620:621], wi, AX_X, ALU.max))
        t_fa = P(lambda e: e.partition_all_reduce(ST[:, 621:622], ST[:, 620:621], 128, RMAX), t_fl)
        t_flag = VC(lambda e: e.tensor_copy(FLG, ST[:, 621:622]), t_fa)

        flag_regs = {}

        def general():
            outer_sem, outer_cnt = q.sem, q.count
            outer_seen = q.seen
            q.sem = {n: g_sem[n] for n in q.names}
            q.count = {n: 0 for n in q.names}
            q.seen = {n: {} for n in q.names}
            saved = q.items
            q.items = {n: [] for n in q.names}
            bufs = [RECA, RECB]
            eid = rs(4).bitcast(I32)
            vp = RB[0:EP, 0:2 * EC].bitcast(I32).rearrange("p (c k) -> p c k", k=2)
            kf, sc, ps_ = rs(0), rs(1), rs(2)
            ki = rs(3).bitcast(I32)
            mk = [RB[0:EP, 2 * EC:3 * EC], RB[0:EP, 3 * EC:4 * EC]]
            pi = RB[0:EP, 4 * EC:5 * EC].bitcast(I32)
            wrk = ST[:, 160:320]
            P(lambda e: e.iota(eid, pattern=[[1, EC]], base=0, channel_multiplier=EC), t_pos0)
            V(lambda e: e.tensor_copy(vp[:, :, 0], v1), q.now("p"))
            ld = VC(lambda e: e.tensor_copy(vp[:, :, 1], eid))
            done = None
            for r, (sh, nb) in enumerate(((14, 16), (18, 16), (22, NW))):
                if r:
                    ld = q.dma("s", g_m[0], lambda e, r=r: e.dma_start(
                        vp, bufs[(r - 1) % 2].rearrange("(p c) k -> p c k", c=EC)), done)
                VC(lambda e, sh=sh: e.tensor_scalar(ki, vp[:, :, 0], sh, None, ALU.arith_shift_right), ld)
                if nb == 16:
                    VC(lambda e: e.tensor_scalar(ki, ki, 15, None, ALU.bitwise_and))
                tk = VC(lambda e: e.tensor_copy(kf, ki))
                VC(lambda e: e.memset(ps_, 0.0))
                tp, _, _ = place(kf, nb, False, mk, sc, ps_, pi, [tk, ld], None, wrk)
                for c in range(EC):
                    done = q.dma("p", g_m[1], lambda e, c=c, r=r: e.indirect_dma_start(
                        bufs[r % 2], bass.IndirectOffsetOnAxis(ap=pi[:, c:c + 1], axis=0), vp[:, c, :], None), tp, ld)
            ld = q.dma("s", g_m[0], lambda e: e.dma_start(vp, bufs[0].rearrange("(p c) k -> p c k", c=EC)), done)
            VC(lambda e: e.tensor_copy(ki, vp[:, :, 0]), ld)
            t1 = VC(lambda e: e.tensor_copy(pi, vp[:, :, 1]))
            w1 = q.dma("s", g_m[2], lambda e: e.dma_start(
                REC1[0:E, :].rearrange("(p c) o -> p (c o)", c=EC), ki), t1, d_v1)
            G = RB[0:EP, 5 * EC:5 * EC + 16 * 128].rearrange("p (a d) -> p a d", d=128)
            EAV = EA.rearrange("(p c) d -> p c d", c=EC)
            prev = [None] * 2
            for b in range(EC // 8):
                h = b % 2
                for k in range(8):
                    c = b * 8 + k
                    ga = q.dma("p", g_g[h], lambda e, c=c, k=k, h=h: e.indirect_dma_start(
                        G[:, h * 8 + k, :], None, edge_attr_128,
                        bass.IndirectOffsetOnAxis(ap=pi[:, c:c + 1], axis=0)), prev[h], t1)
                prev[h] = q.dma("s", g_w[h], lambda e, b=b, h=h: e.dma_start(
                    EAV[:, b * 8:b * 8 + 8, :], G[:, h * 8:h * 8 + 8, :]), ga)
            q.wait("s", prev[0], prev[1], w1)
            ends = {n: q.now(n) for n in q.names if q.count[n]}
            for n in q.names:
                for m, tok in ends.items():
                    q.wait(n, tok)
            branch = q.items
            q.items, q.sem, q.count, q.seen = saved, outer_sem, outer_cnt, outer_seen
            return branch

        g_sem = {n: sem(f"ge_{n}") for n in ("v", "a", "t", "p", "s")}
        g_m = [sem(f"gm{i}") for i in range(3)]
        g_g = [sem(f"gg{i}") for i in range(2)]
        g_w = [sem(f"gw{i}") for i in range(2)]
        branch = general()
        for n in ("v", "t", "p", "s"):
            q.wait(n, t_flag, t_pos0, d_v1 if n == "s" else None)

            def enter(e, n=n):
                r = e.alloc_register(f"flag_{n}")
                e.load([r], FLG[0:1, 0:1])
                flag_regs[n] = r
                with e.If_ne(r, 0):
                    for it in branch[n]:
                        it(e)
                e.sem_inc(s_join, 1)
                e.wait_ge(s_join, 4)
            q.items[n].append(enter)

        sct = {}
        for c in range(EC):
            def put(c=c):
                return q.dma("p", s_g[16 + c % 16], lambda e: e.indirect_dma_start(
                    REC0, bass.IndirectOffsetOnAxis(ap=posi0[:, c:c + 1], axis=0), v0[:, c:c + 1], None),
                    t_pos0, t_v0, d_pad, sct.get(c - 16))
            sct[c] = put()
        t_sc = [sct[c] for c in range(EC - 16, EC)]

        tf = ST[:, 320:327]
        VC(lambda e: e.tensor_copy(tf, SI[:, 0:NTB]), c_tt, c_idb)

        def windows(cum, wout):
            VC(lambda e: e.memset(wout, 0.0))
            for b in range(1, NW):
                VC(lambda e, b=b: e.scalar_tensor_tensor(out=wout, in0=tf, scalar=cum[:, b - 1:b], in1=wout,
                                                         op0=ALU.is_ge, op1=ALU.add))

        W0F, W1F = ST[:, 328:335], ST[:, 336:343]
        windows(cum0, W0F)
        I16A = sb("I16A", [128, 16], I16)
        t_w0 = VC(lambda e: e.tensor_copy(I16A[:, 0:NTB], W0F))
        def ident_store(dst_ap, src_ap, s_, *w):
            return q.dma("s", s_, lambda e: e.dma_start(dst_ap.rearrange("b p -> p b"), src_ap,
                                                        allow_slow_non_contiguous=True), *w)
        d_w0 = ident_store(TW0, I16A[:, 0:NTB], s_m[3], t_w0)
        l_w0 = q.dma("s", s_m[4], lambda e: e.dma_start(WTAB0[0:1, :], TW0.rearrange("b p -> (b p)").rearrange("(a n) -> a n", a=1)), d_w0)

        cnt1 = ST[:, 352:352 + NW]
        tot1, nt1, cum1, st1, sh1 = (ST[:, 384 + 32 * k:384 + 32 * k + NW] for k in range(5))
        VC(lambda e: e.tensor_scalar(wi, slot(1), 8, None, ALU.arith_shift_right))
        VC(lambda e: e.tensor_copy(wk, wi))
        VC(lambda e: e.memset(cnt1, 0.0))
        for b in range(NW):
            t_c1 = VC(lambda e, b=b: e.tensor_scalar(msk[0], wk, float(b), None, ALU.is_equal, ALU.add,
                                                     accum_out=cnt1[0:EP, b:b + 1]))
        m3 = T(lambda e: e.matmul(PS[2][:, 0:NW], ONES[0:EP, :], cnt1[0:EP, :], start=True, stop=True), t_c1)
        VC(lambda e: e.tensor_copy(tot1, PS[2][:, 0:NW]), m3)
        ti = SI[:, 8:8 + NW]
        VC(lambda e: e.tensor_scalar(ti, tot1, 127.0, None, ALU.add))
        VC(lambda e: e.tensor_scalar(ti, ti, 7, None, ALU.arith_shift_right))
        VC(lambda e: e.tensor_copy(nt1, ti))
        VC(lambda e: e.tensor_tensor_scan(cum1, ONES[:, 0:NW], nt1, 0.0, ALU.mult, ALU.add))
        VC(lambda e: e.tensor_tensor_scan(st1, ONES[:, 0:NW], tot1, 0.0, ALU.mult, ALU.add))
        windows(cum1, W1F)
        VC(lambda e: e.scalar_tensor_tensor(out=sh1, in0=cum1, scalar=-128.0, in1=st1, op0=ALU.mult, op1=ALU.add))
        VC(lambda e: e.tensor_copy(nt1, sh1))
        VC(lambda e: e.tensor_tensor(nt1[:, 1:NW], sh1[:, 1:NW], sh1[:, 0:NW - 1], ALU.subtract))
        BTF, tm = ST[:, 544:551], ST[:, 552:559]
        VC(lambda e: e.tensor_scalar(BTF, tf, 128.0, None, ALU.mult))
        for b in range(1, NW):
            VC(lambda e, b=b: e.tensor_scalar(tm, tf, cum1[:, b - 1:b], nt1[:, b - 1:b], ALU.is_ge, ALU.mult))
            VC(lambda e: e.tensor_tensor(BTF, BTF, tm, ALU.add))
        BTA, DT, FT, W256 = ST[:, 560:567], ST[:, 568:575], ST[:, 576:583], ST[:, 584:591]
        VC(lambda e: e.tensor_scalar(BTF, BTF, float(E), None, ALU.min))
        VC(lambda e: e.tensor_scalar(BTA, BTF, float(LAST), None, ALU.min))
        VC(lambda e: e.tensor_tensor(DT, BTF, BTA, ALU.subtract))
        VC(lambda e: e.tensor_scalar(FT, DT, 0.0, None, ALU.is_gt))
        VC(lambda e: e.tensor_scalar(W256, W1F, 256.0, None, ALU.mult))
        VC(lambda e: e.tensor_copy(I16A[:, 8:8 + NTB], W1F))
        VC(lambda e: e.tensor_copy(SI[:, 44:44 + NTB], BTF))
        t_tb = VC(lambda e: e.tensor_copy(SI[:, 52:52 + NTB], BTA))
        d1 = ident_store(TW1, I16A[:, 8:8 + NTB], s_m[5], t_tb)
        d2 = ident_store(TBT[0], SI[:, 44:44 + NTB], s_m[6], t_tb)
        d3 = ident_store(TBT[1], SI[:, 52:52 + NTB], s_m[7], t_tb)
        l_w1 = q.dma("s", s_m[8], lambda e: e.dma_start(WTAB1[0:1, :], TW1.rearrange("b p -> (b p)").rearrange("(a n) -> a n", a=1)), d1)
        q.wait("s", d2, d3)

        RR = RC[:, 0:NTB * 128].rearrange("p (b l) -> p b l", l=128)
        RRI = RR.bitcast(I32)
        t_rr = None
        v_before_rr = q.now("v")
        sregs = {}

        def dyn_rows(t):
            def go(e):
                if t % 8 == 0:
                    if "r" not in sregs:
                        sregs["r"] = [e.alloc_register(f"bt{i}") for i in range(8)]
                    e.load(sregs["r"], TBT[0].rearrange("b p -> (b p)").rearrange("(a n) -> a n", a=1)[0:1, t:t + 8])
                v = e.snap(sregs["r"][t % 8], min_val=0, max_val=E)
                return e.dma_start(RRI[t % 128:t % 128 + 1, t // 128, :],
                                   REC1[bass.ds(v, 128), :].rearrange("(a l) o -> a (l o)", a=1))
            return go

        m_rr = VC(lambda e: e.memset(RR, 0.0))
        q.wait("s", m_rr, d_pad1, d_v1)
        for t in range(NTL):
            t_rr = q.dma("s", s_r1, dyn_rows(t))
        RL = RC[:, NTB * 128:NTB * 128 + 128].bitcast(I32)
        RLF = RC[:, NTB * 128 + 128:NTB * 128 + 256]
        t_rl = q.dma("s", s_m[9], lambda e: e.dma_start(
            RL, REC1[LAST:E, :].rearrange("(a l) o -> a (l o)", a=1).to_broadcast([128, 128])), m_rr)

        KR = [HN[:, 0:49, :].rearrange("p a b -> p (a b)")[:, k * 896:(k + 1) * 896].rearrange("p (b l) -> p b l", l=128) for k in range(5)]
        DI1 = HN[:, :, :].rearrange("p a b -> p (a b)")[:, 5 * 896:6 * 896].bitcast(I32).rearrange("p (b l) -> p b l", l=128)

        def decode(DI, dst_f, srci, sh, mask, *w):
            if mask is None:
                VC(lambda e: e.tensor_scalar(DI, srci, sh, None, ALU.arith_shift_right), *w)
            else:
                VC(lambda e: e.tensor_scalar(DI, srci, sh, mask, ALU.arith_shift_right, ALU.bitwise_and), *w)
            return VC(lambda e: e.tensor_copy(dst_f, DI))

        def columns(dst_t, src_rows, tok, banks, prev_evac):
            last = prev_evac
            for half, (a, b) in enumerate(((0, 4), (4, NTB))):
                bank = PS[banks[half]]
                for k in range(a, b):
                    mt = T(lambda e, k=k, a=a, bank=bank: e.transpose(
                        bank[:, (k - a) * 128:(k - a + 1) * 128], src_rows[:, k, :], IDENT[:, :]),
                        tok, prev_evac, c_id)
                last = V(lambda e, a=a, b=b, bank=bank: e.tensor_copy(
                    dst_t[:, a * 128:b * 128], bank[:, 0:(b - a) * 128]), mt)
            return last

        decode(DI1, KR[0], RRI, 14, None, t_rr)
        decode(DI1, KR[1], RRI, 1, 8191)
        decode(DI1, KR[2], RRI, 0, 16383)
        KA = KR[3]
        VC(lambda e: e.tensor_copy(KR[4], KR[0]))
        for b in range(NTB):
            VC(lambda e, b=b: e.tensor_scalar(KR[4][:, b, :], KR[0][:, b, :], W256[:, b:b + 1], None, ALU.subtract))
        VC(lambda e: e.tensor_scalar(RL, RL, 14, None, ALU.arith_shift_right), t_rl)
        VC(lambda e: e.tensor_copy(RLF, RL))
        for b in range(NTB):
            lm = ST[:, 0:128]
            VC(lambda e, b=b: e.tensor_scalar(lm, IOTA[:, 0:128], DT[:, b:b + 1], -1.0e4, ALU.is_lt, ALU.mult), t_pos0, c_io)
            VC(lambda e: e.tensor_tensor(lm, lm, RLF, ALU.add))
            VC(lambda e, b=b: e.tensor_scalar(lm, lm, W256[:, b:b + 1], None, ALU.subtract))
            VC(lambda e, b=b: e.tensor_tensor(lm, lm, KR[4][:, b, :], ALU.subtract))
            VC(lambda e, b=b: e.scalar_tensor_tensor(out=KA[:, b, :], in0=lm, scalar=FT[:, b:b + 1],
                                                     in1=KR[4][:, b, :], op0=ALU.mult, op1=ALU.add))
        t_dec = vv()
        KEYA = SC1
        e1 = columns(KEYA, KA, t_dec, (0, 1), None)
        e1 = columns(KEY1, KR[4], t_dec, (2, 3), None)
        e1 = columns(WE0, KR[0], t_dec, (0, 1), e1)
        d_kf = q.dma("s", s_in[31], lambda e: e.dma_start(KFD, WE0[:, :]), e1)
        e1 = columns(IDX1, KR[1], t_dec, (2, 3), e1)
        t_i3 = columns(IDX0, KR[2], t_dec, (0, 1), e1)
        d_i3 = q.dma("s", s_in[32], lambda e: e.dma_start(I3D, IDX0[:, :]), t_i3)
        cst("v", c_io)

        wregs = {}

        def window(e, n, tab, t):
            key = n
            if key not in wregs:
                wregs[key] = [e.alloc_register(f"w_{n}_{i}") for i in range(8)]
            if t % 8 == 0:
                e.load(wregs[key], tab[0:1, t:t + 8])
            return e.snap(wregs[key][t % 8], min_val=0, max_val=NW - 1)

        def sum_pass(acc, tab, fetch, key, wgt, ready, extra=None):
            mm = {}
            ad = {}
            oh = {}
            for t in range(NTL + 2):
                if t < NTL:
                    def onehot(t=t):
                        if wgt is None:
                            return V(lambda e: e.tensor_scalar(OH[:, t % 4, :], IOTA[:, :], key[:, t:t + 1], None,
                                                               ALU.is_equal), mm.get(t - 4), ready)
                        return V(lambda e: e.tensor_scalar(OH[:, t % 4, :], IOTA[:, :], key[:, t:t + 1],
                                                           wgt[:, t:t + 1], ALU.is_equal, ALU.mult),
                                 mm.get(t - 4), ready, wtok.get(t))
                    wtok = {}
                    if extra is not None:
                        wtok[t] = extra(t)
                    oh[t] = onehot()
                    rows, tok = fetch(t)

                    def mult(t=t, rows=rows, tok=tok):
                        return T(lambda e: e.matmul(PS[t % 4][:, 0:WN], rows, OH[:, t % 4, :], start=True, stop=True),
                                 oh[t], tok, ad.get(t - 4), ready)
                    mm[t] = mult()
                if t >= 2:
                    def add(t=t - 2):
                        def go(e):
                            w = window(e, "v", tab, t)
                            sl = acc[:, bass.ds(w * WN, WN)]
                            return e.tensor_tensor(sl, sl, PS[t % 4][:, 0:WN], ALU.add)
                        return V(go, mm[t], ad.get(t - 1), ready)
                    ad[t - 2] = add()
            return ad[NTL - 1], mm

        GD = GR[:, 0:32 * 128].rearrange("p (a d) -> p a d", d=128)

        def gatherer(table, idx, ready, used, nslots=16):
            def fetch(t):
                s = t % nslots
                tok = q.dma("p", s_g[s], lambda e: e.indirect_dma_start(
                    GD[:, s, :], None, table, bass.IndirectOffsetOnAxis(ap=idx[:, t:t + 1], axis=0)),
                    ready, used().get(t - nslots))
                return GD[:, s, :], tok
            return fetch

        def run_gather(acc, tab, table, idx, key, wgt, ready, extra=None):
            holder = {}
            mmref = {}

            def used():
                return mmref

            f = gatherer(table, idx, ready, used)
            def fetch(t):
                return f(t)
            return sum_pass2(acc, tab, fetch, key, wgt, ready, extra, mmref)

        def sum_pass2(acc, tab, fetch, key, wgt, ready, extra, mm):
            ad, oh = {}, {}
            for t in range(NTL + 2):
                if t < NTL:
                    def tile(t=t):
                        wt = extra(t) if extra is not None else None
                        if wgt is None:
                            oh[t] = V(lambda e: e.tensor_scalar(OH[:, t % 4, :], IOTA[:, :], key[:, t:t + 1], None,
                                                                ALU.is_equal), mm.get(t - 4), ready)
                        else:
                            oh[t] = V(lambda e: e.tensor_scalar(OH[:, t % 4, :], IOTA[:, :], key[:, t:t + 1],
                                                                wgt[:, t:t + 1], ALU.is_equal, ALU.mult),
                                      mm.get(t - 4), ready, wt)
                        rows, tok = fetch(t)
                        mm[t] = T(lambda e: e.matmul(PS[t % 4][:, 0:WN], rows, OH[:, t % 4, :],
                                                     start=True, stop=True),
                                  oh[t], tok, ad.get(t - 4), ready)
                    tile()
                if t >= 2:
                    def add(t=t - 2):
                        def go(e):
                            w = window(e, "v", tab, t)
                            sl = acc[:, bass.ds(w * WN, WN)]
                            return e.tensor_tensor(sl, sl, PS[t % 4][:, 0:WN], ALU.add)
                        return V(go, mm[t], ad.get(t - 1), ready)
                    ad[t - 2] = add()
            return ad[NTL - 1]

        ATT = RB[:, 0:NW * WN]
        m_att = V(lambda e: e.memset(ATT, 0.0), vv())
        aregs = {}
        amm = {}
        toks_attr = {}
        AB = 8

        def attr_sp(e):
            r = e.alloc_register("flag_attr")
            e.load([r], FLG[0:1, 0:1])
            rr = [e.alloc_register(f"ba{i}") for i in range(8)]
            for which in (0, 1):
                with (e.If_eq(r, 0) if which == 0 else e.Else()):
                    table = edge_attr_128 if which == 0 else EA
                    for t in range(NTL):
                        s = t % 16
                        if t >= 16:
                            e.wait_ge(*amm[t - 16])
                        if t % 8 == 0:
                            e.load(rr, TBT[1].rearrange("b p -> (b p)").rearrange("(a n) -> a n", a=1)[0:1, t:t + 8])
                        v = e.snap(rr[t % 8], min_val=0, max_val=LAST)
                        e.dma_start(GD[:, s, :], table[bass.ds(v, 128), :]).then_inc(s_h[s], 16)

        q.wait("s", t_i3)
        q.items["s"].append(attr_sp)

        def attr_fetch(t):
            s = t % 16
            q.dcount[id(s_h[s])] = q.dcount.get(id(s_h[s]), 0) + 16
            return GD[:, s, :], (s_h[s], q.dcount[id(s_h[s])])

        t_att = sum_pass2(ATT, WTAB1, attr_fetch, KEYA, None, [m_att, l_w1, t_i3, c_io], None, amm)
        d_att = q.dma("s", s_m[10], lambda e: e.dma_start(ATTD, ATT), t_att)

        def layernorm(*w):
            bs, mv, sd, rd = (ST[:, 0:6 * NT], ST[:, 6 * NT:8 * NT], ST[:, 8 * NT:9 * NT], ST[:, 9 * NT:10 * NT])
            first = vv()
            for t in range(NT):
                V(lambda e, t=t: e.bn_stats(bs[:, 6 * t:6 * t + 6], XS[:, t, :]), first, *w)
            s1 = vv()
            for t in range(NT):
                V(lambda e, t=t: e.bn_aggr(mv[:, 2 * t:2 * t + 2], bs[:, 6 * t:6 * t + 6]), s1)
            mvv = mv.rearrange("p (t k) -> p t k", k=2)
            VC(lambda e: e.tensor_scalar(sd, mvv[:, :, 1], 1.0e-5, None, ALU.add))
            a1 = A(lambda e: e.activation(sd, sd, ACT.Sqrt), vv())
            VC(lambda e: e.reciprocal(rd, sd), a1)
            s2 = vv()
            toks = []
            for t in range(NT):
                toks.append(V(lambda e, t=t: e.tensor_scalar(HN[:, t, 0:128], XS[:, t, :], mvv[:, t, 0:1],
                                                             rd[:, t:t + 1], ALU.subtract, ALU.mult), s2, *w))
            return toks

        def transposed(dst_t, toks, *w):
            outs = []
            ev = {}
            for g in range(13):
                k0, k1 = 4 * g, min(4 * g + 4, NT)
                bank = PS[4 + g % 3]
                for k in range(k0, k1):
                    mt = T(lambda e, k=k, k0=k0, bank=bank: e.transpose(
                        bank[:, (k - k0) * 128:(k - k0 + 1) * 128], HN[:, k, 0:128], IDENT[:, :]),
                        toks[k], ev.get(g - 3))
                ev[g] = A(lambda e, k0=k0, k1=k1, bank=bank: e.activation(
                    dst_t[:, k0 * 128:k1 * 128], bank[:, 0:(k1 - k0) * 128], ACT.Relu), mt, *w)
                outs.append(ev[g])
            return outs

        def rows_out(table, src_v, toks_of, s_, eng="s", width=None):
            tv = table.rearrange("(t p) d -> p t d", p=128)
            tok = None
            for g in range(7):
                tok = q.dma(eng, s_, lambda e, g=g: e.dma_start(tv[:, 7 * g:7 * g + 7, :], src_v[:, 7 * g:7 * g + 7, :]),
                            toks_of(7 * g + 6))
            return tok

        hn = layernorm(l_x, l_x2, t_i3)
        ACC = RA[:, 0:NW * WN]
        z0 = V(lambda e: e.memset(RA[:, NP:NW * WN], 0.0), t_c1)
        ht = transposed(ACC, hn, t_c1, t_v1, d_v1)
        HF = HN[:, :, 0:128]
        rl = {}
        for g in range(7):
            rl[g] = A(lambda e, g=g: e.activation(HF[:, 7 * g:7 * g + 7, :], HF[:, 7 * g:7 * g + 7, :], ACT.Relu),
                      q.now("t"))
        d_tab = rows_out(TAB[0], HF, lambda t: rl[t // 7], s_m[11])

        R0 = RC[:, 0:NTB * 128].rearrange("p (b l) -> p b l", l=128)
        l_r0 = q.dma("s", s_m[12], lambda e: e.dma_start(
            R0.bitcast(I32), REC0.rearrange("(b p l) o -> p b (l o)", p=128, l=128)), t_sc, t_dec)
        K0 = [RC[:, (k + 1) * 896:(k + 2) * 896].rearrange("p (b l) -> p b l", l=128) for k in range(3)]
        DI0 = RC[:, 4 * 896:5 * 896].bitcast(I32).rearrange("p (b l) -> p b l", l=128)
        decode(DI0, K0[0], R0.bitcast(I32), 21, None, l_r0, t_sc)
        decode(DI0, K0[1], R0.bitcast(I32), 8, 8191)
        decode(DI0, K0[2], R0.bitcast(I32), 0, 255)
        t_d0 = vv()
        TYP = SC1
        cst("v", d_kf, d_i3)
        e0 = columns(KEY0, K0[0], t_d0, (0, 1), t_att)
        e0 = columns(IDX0, K0[1], t_d0, (2, 3), t_att)
        e0 = columns(TYP, K0[2], t_d0, (0, 1), e0)
        t_e0 = e0

        wsel_s = RC[:, 5 * 896:5 * 896 + 2 * NREL]

        def wsel(t):
            return V(lambda e: e.scalar_tensor_tensor(
                out=wsel_s[:, (t % 2) * NREL:(t % 2 + 1) * NREL], in0=IOTA[:, 0:NREL], scalar=TYP[:, t:t + 1], in1=RELB[:, :],
                op0=ALU.is_equal, op1=ALU.mult, accum_out=WE0[:, t:t + 1]), l_rel, t_e0, ws_prev.get(t - 2))
        ws_prev = {}

        def wsel_first(t):
            if t == 0:
                ws_prev[0] = wsel(0)
            if t + 1 < NTL:
                ws_prev[t + 1] = wsel(t + 1)
            return ws_prev[t]

        acc_tok = [ht, z0]
        tabs = [TAB[0], TAB[1], TAB[2], TABQ]
        for layer, iw in enumerate((iW1, iW2, iW3)):
            done = run_gather(ACC, WTAB0, tabs[layer], IDX0, KEY0, WE0,
                              [d_tab, l_w0, t_e0, *([] if layer else [*ht, z0])],
                              extra=wsel_first if layer == 0 else None)
            ev, mt = {}, {}
            for g in range(13):
                k0, k1 = 4 * g, min(4 * g + 4, NT)
                bank = PS[4 + g % 3]
                for k in range(k0, k1):
                    mt[g] = T(lambda e, k=k, k0=k0, bank=bank, iw=iw: e.matmul(
                        bank[:, (k - k0) * 128:(k - k0 + 1) * 128], ACC[:, k * 128:(k + 1) * 128], WT[:, iw, :],
                        start=True, stop=True), done, ev.get(g - 3), l_w[iw])
                ev[g] = A(lambda e, k0=k0, k1=k1, bank=bank: e.activation(
                    HN[:, k0:k1, 0:128], bank[:, 0:(k1 - k0) * 128].rearrange("p (a b) -> p a b", b=128), ACT.Tanh),
                    mt[g], d_tab)
            if layer < 2:
                d_tab = rows_out(tabs[layer + 1], HF, lambda t: ev[t // 4], s_m[13 + layer])
            ev2 = {}
            for g in range(13):
                c0_, c1_ = 512 * g, min(512 * g + 512, NW * WN)
                bank = PS[g % 4]
                m = T(lambda e, c0_=c0_, c1_=c1_, bank=bank, iw=iw: e.matmul(
                    bank[:, 0:c1_ - c0_], WT[:, iw, :], ACC[:, c0_:c1_], start=True, stop=True), ev2.get(g - 4))
                ev2[g] = A(lambda e, c0_=c0_, c1_=c1_, bank=bank: e.activation(
                    ACC[:, c0_:c1_], bank[:, 0:c1_ - c0_], ACT.Tanh), m)
            acc_tok = [ev2[12]]
            cst("v", ev2[12])
            hn_ev = ev

        if stop_at == 0:
            pass

        m = T(lambda e: e.matmul(PS[4][:, 0:1], WT[:, iEN, :], COLS[:, 0:1], start=True, stop=True), l_u, l_w[iEN], hn_ev[12])
        m = T(lambda e: e.matmul(PS[4][:, 1:2], WT[:, iEN, :], COLS[:, 2:3], start=True, stop=True))
        m = T(lambda e: e.transpose(PS[4][:, 128:256], WT[:, iRE, :], IDENT[:, :]), l_w[iRE])
        V(lambda e: e.tensor_copy(COLS[:, 6:8], PS[4][:, 0:2]), m)
        RET = ST[:, 500:628]
        VC(lambda e: e.tensor_copy(RET, PS[4][:, 128:256]))
        m = T(lambda e: e.matmul(PS[5][:, 0:1], RET, COLS[:, 3:4], start=True, stop=True), vv(), l_ra)
        VC(lambda e: e.tensor_tensor(COLS[:, 8:9], PS[5][:, 0:1], COLS[:, 1:2], ALU.mult), m)
        m = T(lambda e: e.matmul(PS[5][:, 1:2], ONES[:, :], COLS[:, 8:9], start=True, stop=True), vv())
        VC(lambda e: e.tensor_copy(COLS[:, 9:10], PS[5][:, 1:2]), m)
        V1B = OH[:, 0, 0:128]
        t_v1b = VC(lambda e: e.tensor_copy(V1B, COLS[:, 6:7].to_broadcast([128, 128])), done)
        for t in range(NT):
            m = T(lambda e, t=t: e.matmul(PS[6][:, t:t + 1], ACC[:, t * 128:(t + 1) * 128], COLS[:, 7:8],
                                          start=True, stop=True), acc_tok, t_v1b)
        t_q = VC(lambda e: e.tensor_copy(HN[:, :, 128:129], PS[6][:, 0:NT].unsqueeze(2)), m)
        t_q2 = VC(lambda e: e.memset(HN[:, :, 129:132], 0.0))
        d_q = rows_out(TABQ, HN[:, :, 0:132], lambda t: [t_q2, hn_ev[12]], s_m[15])
        PB = RB[:, 0:NW * WN]
        ev2 = {}
        for g in range(13):
            c0_, c1_ = 512 * g, min(512 * g + 512, NW * WN)
            bank = PS[g % 4]
            m = T(lambda e, c0_=c0_, c1_=c1_, bank=bank: e.matmul(
                bank[:, 0:c1_ - c0_], V1B, ACC[:, c0_:c1_], start=True, stop=True), ev2.get(g - 4))
            ev2[g] = A(lambda e, c0_=c0_, c1_=c1_, bank=bank: e.activation(
                PB[:, c0_:c1_], bank[:, 0:c1_ - c0_], ACT.Copy), m, d_att)
        t_pb = ev2[12]
        t_accfree = m

        def two_phase_a(table, wd, idx, gs, nring, spill, ready, per_tile, per_group, s_sp):
            RG = GR[:, 0:nring * wd].rearrange("p (a d) -> p a d", d=wd)
            free = {}
            t0 = 0
            groups = []
            while t0 < NTL:
                t1 = min(t0 + gs, (t0 // TJ + 1) * TJ if gs == 17 else NTL, NTL)
                groups.append((t0, t1))
                t0 = t1
            ngr = nring // gs
            toks = {}
            lasts = []
            for gi, (a, b) in enumerate(groups):
                base = (gi % ngr) * gs
                for t in range(a, b):
                    s = base + t - a
                    toks[t] = q.dma("p", s_g[s], lambda e, s=s, t=t: e.indirect_dma_start(
                        RG[:, s, :], None, table, bass.IndirectOffsetOnAxis(ap=idx[:, t:t + 1], axis=0)),
                        ready, free.get(gi - ngr))
                    per_tile(t)
                gt = [toks[t] for t in range(a, b)]
                d = q.dma("s", s_sp[gi % ngr], lambda e, a=a, b=b, base=base: e.dma_start(
                    spill[:, a:b, :], RG[:, base:base + b - a, :]), gt)
                free[gi] = [d, per_group(gi, a, b, RG[:, base:base + b - a, :], gt)]
                lasts.append(d)
            return lasts[-ngr:]

        S0 = SC1
        QE = SC2
        junk = RC[:, 0:2 * WN].rearrange("p (a b) -> p a b", b=WN)
        pe_t = {}

        def pe_tile(t):
            def go(e):
                w = window(e, "v", WTAB0, t)
                return e.scalar_tensor_tensor(out=junk[:, t % 2, :], in0=IOTA[:, :], scalar=KEY0[:, t:t + 1],
                                              in1=PB[:, bass.ds(w * WN, WN)], op0=ALU.is_equal, op1=ALU.mult,
                                              accum_out=S0[:, t:t + 1])
            pe_t[t] = V(go, t_pb, pe_t.get(t - 2), done)

        def q_group(gi, a, b, rows, gt):
            return A(lambda e: e.activation(QE[:, a:b], rows[:, :, 128], ACT.Copy), gt)

        sp0 = two_phase_a(TABQ, 132, IDX0, 13, 26, SPA, [d_q, done], pe_tile, q_group, [s_m[16], s_m[17]])
        inv = WE0
        NL = slice(0, NTL)
        VC(lambda e: e.tensor_tensor(S0[:, NL], S0[:, NL], QE[:, NL], ALU.add), q.now("a"))
        VC(lambda e: e.tensor_scalar(S0[:, NL], S0[:, NL], COLS[:, 9:10], None, ALU.add))
        VC(lambda e: e.scalar_tensor_tensor(out=QE[:, NL], in0=S0[:, NL], scalar=0.01, in1=S0[:, NL],
                                            op0=ALU.mult, op1=ALU.max))
        VC(lambda e: e.tensor_scalar(inv[:, NL], KEY0[:, NL], 255.5, -BIG, ALU.is_gt, ALU.mult))
        VC(lambda e: e.tensor_tensor(QE[:, NL], QE[:, NL], inv[:, NL], ALU.add))
        VC(lambda e: e.tensor_reduce(COLS[:, 10:11], QE[:, NL], AX_X, ALU.max))
        t_mx = P(lambda e: e.partition_all_reduce(COLS[:, 11:12], COLS[:, 10:11], 128, RMAX), vv())
        VC(lambda e: e.tensor_scalar(QE[:, NL], QE[:, NL], COLS[:, 11:12], None, ALU.subtract), t_mx)
        t_ex = A(lambda e: e.activation(S0[:, NL], QE[:, NL], ACT.Exp, accum_out=COLS[:, 12:13]), vv())
        t_z = P(lambda e: e.partition_all_reduce(COLS[:, 13:14], COLS[:, 12:13], 128, RADD), t_ex)
        VC(lambda e: e.reciprocal(COLS[:, 14:15], COLS[:, 13:14]), t_z)
        t_al = VC(lambda e: e.tensor_scalar(S0[:, NL], S0[:, NL], COLS[:, 14:15], None, ALU.mult))
        z1 = VC(lambda e: e.memset(ACC, 0.0), t_accfree, d_q)

        def replay(spill, wd, gs, nring, rw, ready, used, s_base):
            RG = GR[:, 0:nring * rw].rearrange("p (a d) -> p a d", d=rw)
            ngr = nring // gs
            st = {"gi": -1, "b": 0}
            groups = []
            t0 = 0
            while t0 < NTL:
                t1 = min(t0 + gs, NTL)
                groups.append((t0, t1))
                t0 = t1
            tokg = {}

            def issue(gi):
                if gi >= len(groups) or gi in tokg:
                    return
                a, b = groups[gi]
                base = (gi % ngr) * gs
                w = used().get(groups[gi - ngr][1] - 1) if gi >= ngr else None
                tokg[gi] = q.dma("s", s_base[gi % ngr], lambda e: e.dma_start(
                    RG[:, base:base + b - a, 0:wd], spill[:, a:b, :]), ready, w)

            def fetch(t):
                gi = t // gs
                issue(gi)
                base = (gi % ngr) * gs
                return RG[:, base + t % gs, :], tokg[gi], gi, RG, base
            return fetch, tokg

        mmr = {}
        f0, _ = replay(SPA, 132, 13, 26, 132, [sp0, q.now("a")], lambda: mmr, [s_m[18], s_m[19]])

        def fetch0(t):
            r, tok, *_ = f0(t)
            return r[:, 0:128], tok

        d_l0 = sum_pass2(ACC, WTAB0, fetch0, KEY0, S0, [z1, t_al], None, mmr)

        def add_transposed(src_t, tok):
            evt = {}
            for g in range(13):
                k0, k1 = 4 * g, min(4 * g + 4, NT)
                bank = PS[4 + g % 3]
                for k in range(k0, k1):
                    mt_ = T(lambda e, k=k, k0=k0, bank=bank: e.transpose(
                        bank[:, (k - k0) * 128:(k - k0 + 1) * 128], src_t[:, k * 128:(k + 1) * 128], IDENT[:, :]),
                        tok, evt.get(g - 3))
                evt[g] = V(lambda e, k0=k0, k1=k1, bank=bank: e.tensor_tensor(
                    XS[:, k0:k1, :], XS[:, k0:k1, :], bank[:, 0:(k1 - k0) * 128].rearrange("p (a b) -> p a b", b=128),
                    ALU.add), mt_, vv())
            return evt[12]
        t_x1 = add_transposed(ACC, d_l0)

        hn = layernorm(t_x1)
        ht = transposed(ACC, hn, t_x1)
        V(lambda e: e.tensor_scalar(ADC[:, 0:8], BD[:, :], COLS[:, 4:5], None, ALU.mult), l_as, c_bd, c_idb)
        t_adc = V(lambda e: e.tensor_scalar(ADC[:, 8:16], BD[:, :], COLS[:, 5:6], None, ALU.mult), l_ad)
        m = T(lambda e: e.transpose(PS[0][:, 0:128], WT[:, iGW, :], IDENT[:, :]), l_w[iGW], d_l0)
        t_ = VC(lambda e: e.tensor_copy(RET, PS[0][:, 0:128]), m)
        m = T(lambda e: e.matmul(PS[1][:, 0:16], RET, ADC[:, :], start=True, stop=True), t_, t_adc)
        V(lambda e: e.tensor_copy(RHS1[:, 128:144], PS[1][:, 0:16]), m)
        t_rhs = V(lambda e: e.tensor_copy(RHS1[:, 0:128], WT[:, iGW, :]))
        ev = {}
        for g in range(17):
            k0, k1 = 3 * g, min(3 * g + 3, NT)
            if k0 >= NT:
                break
            bank = PS[g % 4]
            for k in range(k0, k1):
                mt_ = T(lambda e, k=k, k0=k0, bank=bank: e.matmul(
                    bank[:, (k - k0) * 144:(k - k0 + 1) * 144], ACC[:, k * 128:(k + 1) * 128], RHS1[:, :],
                    start=True, stop=True), ht, t_rhs, ev.get(g - 4))
            ev[g] = A(lambda e, k0=k0, k1=k1, bank=bank: e.activation(
                HN[:, k0:k1, :], bank[:, 0:(k1 - k0) * 144].rearrange("p (a b) -> p a b", b=144), ACT.Copy), mt_)
        t_hw = ev[max(ev)]
        d_g = rows_out(TABG, HN[:, :, 0:136], lambda t: ev[t // 3], s_m[11])
        AR = ST[:, 0:NT * 8].rearrange("p (t h) -> p t h", h=8)
        AF = RC[:, 0:NT * 8].rearrange("p (t h) -> p t h", h=8)
        V(lambda e: e.memset(AD3[:, :, :], 0.0), t_rhs)
        VC(lambda e: e.tensor_copy(AR, HN[:, :, 136:144]), t_hw)
        for k in range(3):
            part = AD3[:, 0:NT, 8 * k:8 * k + 8]
            VC(lambda e, part=part: e.tensor_copy(part, AR))
            if k < 2:
                VC(lambda e, part=part: e.tensor_copy(AF, part))
                VC(lambda e: e.tensor_tensor(AR, AR, AF, ALU.subtract))
        t_ad3 = vv()
        EE = RA[:, :].rearrange("p (j g h) -> p j g h", g=TG, h=8)
        AE = RB[:, 0:6528].rearrange("p (j g h) -> p j g h", g=TG, h=8)
        z2 = VC(lambda e: e.memset(RA[:, :], 0.0), [ev[k] for k in ev])
        z3 = VC(lambda e: e.memset(RB[:, 0:6528], 0.0))
        ohb, tr, oht, lk, evd = {}, {}, {}, {}, {}
        pend = []

        def lk_tile(t):
            gi = t // 17
            j0 = t % TJ
            ohb[t] = V(lambda e: e.tensor_scalar(OHB[:, t % 4, :], IOTAB[:, :], KEY1[:, t:t + 1], None, ALU.is_equal),
                       tr.get(t - 4), z3)
            pb = PS[4 + t % 4][:, 0:128].bitcast(BF16)
            for h in range(2):
                tr[t] = T(lambda e, h=h: e.transpose(pb[:, h * 128:h * 128 + 128],
                                                     OHB[:, t % 4, h * 128:(h + 1) * 128], IDENTB[:, :]),
                          ohb[t], oht.get(t - 4), c_idb)
            oht[t] = A(lambda e: e.activation(OHT[:, t % 4, :], pb, ACT.Copy),
                       tr[t], lk.get(t - 4))
            pend.append(t)
            if len(pend) > 2 or t == NTL - 1:
                while len(pend) > (0 if t == NTL - 1 else 2):
                    look(pend.pop(0))

        def look(t):
            gi = grp_of[t]
            c = (t - grp_start[t]) * 24
            bank = PS[gi % 3]

            def go(e, h):
                w = window(e, "t", WTAB1, t) if h == 0 else wlast["v"]
                wlast["v"] = w
                return e.matmul(bank[:, c:c + 24], OHT[:, t % 4, h * 128:(h + 1) * 128],
                                AD3[:, bass.ds(w * 2 + h, 1), :].rearrange("p a b -> p (a b)"),
                                start=(h == 0), stop=(h == 1))
            T(lambda e: go(e, 0), oht[t], t_ad3, evd.get(gi - 3))
            lk[t] = T(lambda e: go(e, 1))
            if t == grp_end[t]:
                a, b = grp_start[t], t + 1
                tg, j = a // TJ, a % TJ
                pv = bank[:, 0:24 * (b - a)].rearrange("p (t k h) -> p t h k", k=3, h=8)
                evd[gi] = V(lambda e: e.tensor_reduce(AE[:, j:j + b - a, tg, :], pv, AX_X, ALU.add), lk[t], z3)

        wlast = {}
        grp_of, grp_start, grp_end = {}, {}, {}
        t0, gi = 0, 0
        while t0 < NTL:
            t1 = min(t0 + 17, (t0 // TJ + 1) * TJ, NTL)
            for t in range(t0, t1):
                grp_of[t], grp_start[t], grp_end[t] = gi, t0, t1 - 1
            t0, gi = t1, gi + 1

        def as_group(gi, a, b, rows, gt):
            tg, j = a // TJ, a % TJ
            return A(lambda e: e.activation(EE[:, j:j + b - a, tg, :], rows[:, :, 128:136], ACT.Copy), gt, z2)

        cst("v", t_x1)
        sp1 = two_phase_a(TABG, 136, IDX1, 17, 34, SPB, [d_g, t_i3, d_l0], lk_tile, as_group, [s_m[20], s_m[21]])
        VC(lambda e: e.tensor_tensor(RA[:, :], RA[:, :], RB[:, 0:6528], ALU.add), q.now("a"))
        VC(lambda e: e.scalar_tensor_tensor(out=RA[:, :], in0=RA[:, :], scalar=0.2, in1=RA[:, :],
                                            op0=ALU.mult, op1=ALU.max))
        IN = SC1[:, 0:TG * TJ]
        VC(lambda e: e.memset(SC1[:, NTL:TG * TJ], -BIG))
        VC(lambda e: e.tensor_scalar(IN[:, 0:NTL], KEY1[:, 0:NTL], 255.5, -BIG, ALU.is_gt, ALU.mult))
        VC(lambda e: e.tensor_scalar(SC2[:, 0:NTL], KEY1[:, 0:NTL], -0.5, -BIG, ALU.is_lt, ALU.mult))
        VC(lambda e: e.tensor_tensor(IN[:, 0:NTL], IN[:, 0:NTL], SC2[:, 0:NTL], ALU.add))
        for g in range(TG):
            V(lambda e, g=g: e.tensor_tensor(EE[:, :, g, :], EE[:, :, g, :],
                                             IN[:, g * TJ:(g + 1) * TJ].unsqueeze(2).to_broadcast([128, TJ, 8]),
                                             ALU.add), *( [vv()] if g == 0 else []))
        t_e = vv()
        RK8 = RC[:, :].rearrange("p (j g h) -> p j g h", g=TG, h=8)
        l_kf = q.dma("s", s_in[33], lambda e: e.dma_start(SC2[:, :], KFD), d_kf, vv())
        VC(lambda e: e.memset(SC2[:, NTL:TG * TJ], 8191.0), l_kf)
        s_ = vv()
        for g in range(TG):
            V(lambda e, g=g: e.tensor_copy(RK8[:, :, g, :],
                                           SC2[:, g * TJ:(g + 1) * TJ].unsqueeze(2).to_broadcast([128, TJ, 8])), s_)
        t_k8 = vv()
        ROWE = RB[:, 0:6528]

        def blocks(dst_t, src_t, tok, act, out_tok=None):
            evb, mb = {}, {}
            for g in range(13):
                j0, j1 = 4 * g, min(4 * g + 4, TJ)
                bank = PS[g % 4]
                for j in range(j0, j1):
                    mb[g] = T(lambda e, j=j, j0=j0, bank=bank: e.transpose(
                        bank[:, (j - j0) * 128:(j - j0 + 1) * 128], src_t[:, j * 128:(j + 1) * 128], IDENT[:, :]),
                        tok, evb.get(g - 4))
                evb[g] = act(g, j0, j1, bank, mb[g], mb)
            return evb[12]

        def copy_to(dst_t):
            def f(g, j0, j1, bank, mtok, _):
                return A(lambda e: e.activation(dst_t[:, j0 * 128:j1 * 128], bank[:, 0:(j1 - j0) * 128], ACT.Copy),
                         mtok)
            return f
        t_re = blocks(ROWE, RA, t_e, copy_to(ROWE))
        t_rk = blocks(RC, RC, [t_k8, t_re], copy_to(RC))
        VC(lambda e: e.tensor_copy(COLS[:, 0:1], RC[:, 0:1]), t_rk)
        VC(lambda e: e.tensor_copy(COLS[:, 1:2], RC[:, 6527:6528]))
        BN = HX = None
        BND = GR[:, 0:3264].bitcast(BF16)
        VC(lambda e: e.tensor_tensor(BND[:, 1:6528], RC[:, 1:6528], RC[:, 0:6527], ALU.not_equal), sp1)
        VC(lambda e: e.memset(BND[:, 0:1], 0.0))
        VC(lambda e: e.tensor_scalar(BND, BND, -BIG, None, ALU.mult))
        VC(lambda e: e.tensor_reduce(COLS[:, 2:3], BND, AX_X, ALU.min))
        VC(lambda e: e.tensor_tensor_scan(ROWE, BND, ROWE, -BIG, ALU.add, ALU.max), t_re)
        VC(lambda e: e.tensor_copy(COLS[:, 3:4], ROWE[:, 6527:6528]))

        L1R = ST[0:1, 0:512]

        def row_of(k, col, tok):
            return T(lambda e: e.matmul(PS[4][0:1, 128 * k:128 * k + 128], COLS[:, col:col + 1], IDENT[:, :],
                                        start=True, stop=True), tok)
        for k, col in enumerate((0, 1, 2, 3)):
            m = row_of(k, col, vv())
        VC(lambda e: e.tensor_copy(L1R.rearrange("p (k h g) -> p k g h", h=8, g=TG),
                                   PS[4][0:1, :].rearrange("p (k g h) -> p k g h", g=TG, h=8)), m)
        KF, KL, BR, FR = (L1R[:, 128 * k:128 * k + 128].rearrange("p (h g) -> p h g", g=TG) for k in range(4))
        XR = ST[0:1, 512:640]
        NE = XR.rearrange("p (h g) -> p h g", g=TG)
        CR = RC[0:1, 0:128]
        C3 = CR.rearrange("p (h g) -> p h g", g=TG)
        TR2 = RC[0:1, 128:256]
        T3 = TR2.rearrange("p (h g) -> p h g", g=TG)
        FC = RC[0:1, 256:384]
        FC3 = FC.rearrange("p (h g) -> p h g", g=TG)
        CO = RC[0:1, 384:512]

        VC(lambda e: e.memset(XR, -BIG))
        VC(lambda e: e.tensor_tensor(NE[:, :, 1:TG], KF[:, :, 1:TG], KL[:, :, 0:TG - 1], ALU.not_equal))
        VC(lambda e: e.tensor_scalar(NE[:, :, 1:TG], NE[:, :, 1:TG], -BIG, None, ALU.mult))

        def carry(forward, vals3):
            VC(lambda e: e.memset(TR2, -BIG))
            if forward:
                VC(lambda e: e.tensor_tensor(T3[:, :, 1:TG], NE[:, :, 1:TG], BR[:, :, 1:TG], ALU.add))
                VC(lambda e: e.tensor_tensor_scan(FC, TR2, vals3, -BIG, ALU.add, ALU.max))
                VC(lambda e: e.memset(CR, -BIG))
                VC(lambda e: e.tensor_tensor(C3[:, :, 1:TG], FC3[:, :, 0:TG - 1], NE[:, :, 1:TG], ALU.add))
            else:
                VC(lambda e: e.tensor_tensor(T3[:, :, 0:TG - 1], NE[:, :, 1:TG], BR[:, :, 0:TG - 1], ALU.add))
                VC(lambda e: e.tensor_tensor_scan(FC[:, ::-1], TR2[:, ::-1], vals3[:, ::-1], -BIG, ALU.add, ALU.max))
                VC(lambda e: e.memset(CR, -BIG))
                VC(lambda e: e.tensor_tensor(C3[:, :, 0:TG - 1], FC3[:, :, 1:TG], NE[:, :, 1:TG], ALU.add))
            VC(lambda e: e.tensor_copy(CO.rearrange("p (g h) -> p h g", h=8), C3))
            m_ = T(lambda e: e.matmul(PS[5][:, 0:1], CO, ONES[0:1, 0:1], start=True, stop=True), vv())
            return VC(lambda e: e.tensor_copy(COLS[:, 4:5], PS[5][:, 0:1]), m_)

        carry(True, L1R[:, 384:512])
        VC(lambda e: e.tensor_tensor_scan(ROWE, BND, ROWE, COLS[:, 4:5], ALU.add, ALU.max))
        B2 = BND
        VC(lambda e: e.tensor_tensor_scan(RC[:, 6527:0:-1] if False else RC[:, 512:513], BND[:, 0:1], ROWE[:, 6527:6528],
                                          -BIG, ALU.add, ALU.max))
        def back(init):
            VC(lambda e: e.tensor_tensor(ROWE[:, 6527:6528], ROWE[:, 6527:6528], init, ALU.max)
               if init is not None else e.tensor_copy(COLS[:, 5:6], ROWE[:, 6527:6528]))
            VC(lambda e: e.tensor_copy(COLS[:, 5:6], ROWE[:, 6527:6528]))
            VC(lambda e: e.tensor_tensor_scan(ROWE[:, 0:6527][:, ::-1], BND[:, 1:6528][:, ::-1],
                                              ROWE[:, 0:6527][:, ::-1], COLS[:, 5:6], ALU.add, ALU.max))
        back(None)
        m = T(lambda e: e.matmul(PS[4][0:1, 0:128], ROWE[:, 0:1], IDENT[:, :], start=True, stop=True), vv())
        VC(lambda e: e.tensor_copy(FR, PS[4][0:1, 0:128].rearrange("p (g h) -> p h g", h=8)), m)
        carry(False, L1R[:, 384:512])
        back(COLS[:, 4:5])
        t_rows = vv()
        def fin(g, j0, j1, bank, mtok, _):
            ct = A(lambda e: e.activation(RC[:, j0 * 128:j1 * 128], bank[:, 0:(j1 - j0) * 128], ACT.Copy), mtok, t_rows)
            vt = V(lambda e: e.tensor_tensor(RA[:, j0 * 128:j1 * 128], RA[:, j0 * 128:j1 * 128],
                                             RC[:, j0 * 128:j1 * 128], ALU.subtract), ct, t_re)
            tail.append((j0, j1, vt))
            return ct
        tail = []
        blocks(None, ROWE, t_rows, fin)
        for j0, j1, vt in tail:
            t_m = A(lambda e, j0=j0, j1=j1: e.activation(RA[:, j0 * 128:j1 * 128], RA[:, j0 * 128:j1 * 128], ACT.Exp),
                    vt)
        MM_ = RC[:, :].rearrange("p (j g h) -> p j g h", g=TG, h=8)

        AC1 = RB[:, :].rearrange("p (n f) -> p n f", f=145)
        z4 = VC(lambda e: e.memset(RB[:, :], 0.0), t_m)
        mmb, adb, ohx, gx = {}, {}, {}, {}
        f1, tokg1 = replay(SPB, 136, 17, 34, 145, [sp1, vv()], lambda: mmb, [s_m[22], s_m[23]])
        prep = {}

        def tile_b(t):
            rows, tok, gi, RG, base = f1(t)
            if t % 17 == 0:
                b = min(t + 17, NTL)
                for a_, b_ in ((t, b),):
                    tg, j = a_ // TJ, a_ % TJ
                    n = b_ - a_
                    A(lambda e: e.activation(RG[:, base:base + n, 128:136], EE[:, j:j + n, tg, :], ACT.Copy), tok, t_m)
                    prep[gi] = A(lambda e: e.activation(RG[:, base:base + n, 136:144], MM_[:, j:j + n, tg, :], ACT.Copy), t_m)
                    ones_t = P(lambda e: e.memset(RG[:, base:base + n, 144:145], 1.0), tok)
                    prep[gi] = [prep[gi], ones_t]
            ohx[t] = V(lambda e: e.tensor_scalar(OH[:, t % 4, :], IOTA[:, :], KEY1[:, t:t + 1], None, ALU.is_equal),
                       mmb.get(t - 4))
            gx[t] = V(lambda e: e.tensor_tensor(
                rows[:, 0:128].rearrange("p (h c) -> p h c", c=16), rows[:, 0:128].rearrange("p (h c) -> p h c", c=16),
                EE[:, t % TJ, t // TJ, :].unsqueeze(2).to_broadcast([128, 8, 16]), ALU.mult), tok, t_m)
            for h in range(2):
                mmb[t] = T(lambda e, h=h: e.matmul(PS[t % 4][:, h * 145:(h + 1) * 145], OH[:, t % 4, h * 128:(h + 1) * 128],
                                                   rows, start=True, stop=True), gx[t], prep[gi], adb.get(t - 4))

        def add_b(t):
            def go(e):
                w = window(e, "v", WTAB1, t)
                sl = RB[:, bass.ds(w * 290, 290)]
                return e.tensor_tensor(sl, sl, PS[t % 4][:, 0:290], ALU.add)
            adb[t] = V(go, mmb[t], adb.get(t - 1), z4)

        for t in range(NTL + 2):
            if t < NTL:
                tile_b(t)
            if t >= 2:
                add_b(t - 2)

        SN = [SC1[:, 0:392], SC1[:, 400:792], SC2[:, 0:392], SC2[:, 400:792], ST[:, 0:392], WE0[:, 0:392], WE0[:, 400:792]]
        n8 = [s.rearrange("p (t h) -> p t h", h=8) for s in SN]
        CT = WE0[:, 800:849]
        HA = WE0[:, 849:896]
        SUMS, DEN, SM, DEG = AC1[:, 0:NT, 0:128], AC1[:, 0:NT, 128:136], AC1[:, 0:NT, 136:144], AC1[:, 0:NT, 144]
        VC(lambda e: e.tensor_scalar(CT, DEG, 1.0, None, ALU.max))
        VC(lambda e: e.reciprocal(RDEG[:, :], CT))
        VC(lambda e: e.tensor_scalar(CT, DEG, 1.0, None, ALU.min))
        VC(lambda e: e.tensor_scalar(CT, CT, -1.0, BIG, ALU.add, ALU.mult))

        def b8(v):
            return v.unsqueeze(2).to_broadcast([128, NT, 8])
        VC(lambda e: e.tensor_tensor(n8[0], SM, b8(RDEG[:, :]), ALU.mult))
        VC(lambda e: e.tensor_tensor(n8[0], n8[0], b8(CT), ALU.add))
        VC(lambda e: e.tensor_tensor(n8[1], HN[:, :, 128:136], HN[:, :, 136:144], ALU.add))
        VC(lambda e: e.scalar_tensor_tensor(out=SN[1], in0=SN[1], scalar=0.2, in1=SN[1], op0=ALU.mult, op1=ALU.max))
        VC(lambda e: e.tensor_tensor(SN[2], SN[0], SN[1], ALU.max))
        VC(lambda e: e.tensor_tensor(SN[0], SN[0], SN[2], ALU.subtract))
        VC(lambda e: e.tensor_tensor(SN[1], SN[1], SN[2], ALU.subtract))
        A(lambda e: e.activation(SN[3], SN[0], ACT.Exp), vv())
        t_ = A(lambda e: e.activation(SN[4], SN[1], ACT.Exp))
        VC(lambda e: e.tensor_tensor(n8[5], DEN, n8[3], ALU.mult), t_)
        VC(lambda e: e.tensor_tensor(SN[5], SN[5], SN[4], ALU.add))
        VC(lambda e: e.reciprocal(SN[6], SN[5]))
        VC(lambda e: e.tensor_tensor(SN[3], SN[3], SN[6], ALU.mult))
        VC(lambda e: e.tensor_tensor(SN[4], SN[4], SN[6], ALU.mult))

        def h16(v):
            return v.unsqueeze(2).to_broadcast([128, NT * 8, 16])

        S4 = SUMS.rearrange("p t (h c) -> p t h c", c=16)
        H4 = HN[:, :, 0:128].rearrange("p t (h c) -> p t h c", c=16)
        for t in range(NT):
            V(lambda e, t=t: e.tensor_tensor(S4[:, t], S4[:, t], n8[3][:, t, :].unsqueeze(2).to_broadcast([128, 8, 16]),
                                             ALU.mult), *([vv()] if t == 0 else []))
            V(lambda e, t=t: e.tensor_tensor(H4[:, t], H4[:, t], n8[4][:, t, :].unsqueeze(2).to_broadcast([128, 8, 16]),
                                             ALU.mult), *([d_g] if t == 0 else []))
        VC(lambda e: e.tensor_tensor(XS[:, :, :], XS[:, :, :], SUMS, ALU.add))
        VC(lambda e: e.tensor_tensor(XS[:, :, :], XS[:, :, :], HN[:, :, 0:128], ALU.add))
        t_x2 = VC(lambda e: e.tensor_tensor(XS[:, :, :], XS[:, :, :],
                                            BIAS1[:, :].unsqueeze(1).to_broadcast([128, NT, 128]), ALU.add), l_gb)

        WTR = [RC[:, k * 128:(k + 1) * 128] for k in range(6)]
        for k, iw in enumerate((iSS, iNE, iED, iDA, iCO, iSE)):
            m = T(lambda e, k=k, iw=iw: e.transpose(PS[4 + k // 4][:, (k % 4) * 128:(k % 4 + 1) * 128], WT[:, iw, :],
                                                    IDENT[:, :]), l_w[iw], t_x2)
        V(lambda e: e.tensor_copy(RC[:, 0:512], PS[4][:, :]), m)
        t_wtr = V(lambda e: e.tensor_copy(RC[:, 512:768], PS[5][:, 0:256]))
        hn = layernorm(t_x2)
        HT = RA[:, 0:NP]
        ht = transposed(HT, hn, t_x2, t_wtr)
        for g in range(7):
            rl[g] = A(lambda e, g=g: e.activation(HF[:, 7 * g:7 * g + 7, :], HF[:, 7 * g:7 * g + 7, :], ACT.Relu),
                      q.now("t"))
        d_t2 = rows_out(TAB2, HF, lambda t: rl[t // 7], s_m[13])
        AG = RB[:, 0:NW * WN]
        z5 = V(lambda e: e.memset(AG, 0.0), vv())
        t_ag = run_gather(AG, WTAB1, TAB2, IDX1, KEY1, None, [d_t2, z5, t_wtr, ht])
        ATC = HN[:, :, :].rearrange("p a b -> p (a b)")[:, 0:NW * WN]
        l_at = q.dma("s", s_m[14], lambda e: e.dma_start(ATC, ATTD), d_att, d_t2)
        cst("t", c_ones, l_b1)
        evo = {}
        for t in range(NT):
            def node(t=t):
                bank = PS[t % 4]
                sl = slice(t * 128, (t + 1) * 128)
                T(lambda e: e.matmul(bank[:, 0:128], AG[:, sl], WTR[1], start=True, stop=False), t_ag, evo.get(t - 4))
                T(lambda e: e.matmul(bank[:, 0:128], ATC[:, sl], WTR[2], start=False, stop=True), l_at)
                T(lambda e: e.matmul(PS[4 + t % 3][:, 0:128], RA[:, sl], WTR[0], start=True, stop=False), evo.get(t - 3))
                m_ = T(lambda e: e.matmul(PS[4 + t % 3][:, 0:128], ONES[0:1, :], ROWS[0:1, 0:128], start=False, stop=True))
                tmp_ = OH[:, t % 2, 0:128]
                V(lambda e: e.tensor_scalar(tmp_, bank[:, 0:128], RDEG[:, t:t + 1], None, ALU.mult), m_, evo.get(t - 2))
                VC(lambda e: e.tensor_tensor(tmp_, tmp_, PS[4 + t % 3][:, 0:128], ALU.add))
                evo[t] = VC(lambda e: e.scalar_tensor_tensor(out=XS[:, t, :], in0=tmp_, scalar=0.0, in1=XS[:, t, :],
                                                             op0=ALU.max, op1=ALU.add))
            node()
        t_x3 = evo[NT - 1]

        hn = layernorm(t_x3)
        ht = transposed(HT, hn, t_x3)
        cst("t", l_b2, l_b3, l_b4)
        Y = HN[:, :, :].rearrange("p a b -> p (a b)")
        ev = {}
        T3v = TAB3.rearrange("(t p k) d -> p t (k d)", p=128, k=2)
        stage = [Y[:, 0:7 * 256], Y[:, 7 * 256:14 * 256]]
        stage = [RB[:, 0:7 * 256].rearrange("p (a b) -> p a b", b=256), RB[:, 7 * 256:14 * 256].rearrange("p (a b) -> p a b", b=256)]
        dg = {}
        for t in range(NT):
            def node3(t=t):
                bank = PS[t % 4]
                sl = slice(t * 128, (t + 1) * 128)
                T(lambda e: e.matmul(bank[:, 0:256], RA[:, sl], RC[:, 3 * 128:5 * 128], start=True, stop=False),
                  ht, evo.get(NT - 1), ev.get(t - 4))
                m_ = T(lambda e: e.matmul(bank[:, 0:256], ONES[0:1, :], ROWS[0:1, 128:384], start=False, stop=True))
                g = t // 7
                ev[t] = A(lambda e: e.activation(stage[g % 2][:, t % 7, :], bank[:, 0:256], ACT.Copy), m_, dg.get(g - 2))
                if t % 7 == 6:
                    dg[g] = q.dma("s", s_m[16 + g % 2], lambda e: e.dma_start(T3v[:, 7 * g:7 * g + 7, :], stage[g % 2]),
                                  ev[t])
            node3()
        z6 = V(lambda e: e.memset(AG, 0.0), dg[5], dg[6])
        l_i3 = q.dma("s", s_in[34], lambda e: e.dma_start(IDX0[:, :], I3D), d_i3, t_x3)
        t_ag = run_gather(AG, WTAB1, TAB3, IDX0, KEY1, None, [dg[5], dg[6], z6, l_i3])
        evo = {}
        outs = []
        for t in range(NT):
            def node4(t=t):
                bank = PS[t % 4]
                sl = slice(t * 128, (t + 1) * 128)
                T(lambda e: e.matmul(bank[:, 0:128], AG[:, sl], IDENT[:, :], start=True, stop=False), t_ag, evo.get(t - 4))
                T(lambda e: e.matmul(bank[:, 0:128], RA[:, sl], WTR[5], start=False, stop=False))
                m_ = T(lambda e: e.matmul(bank[:, 0:128], ONES[0:1, :], ROWS[0:1, 384:512], start=False, stop=True))
                evo[t] = V(lambda e: e.scalar_tensor_tensor(out=XS[:, t, :], in0=bank[:, 0:128], scalar=0.0,
                                                            in1=XS[:, t, :], op0=ALU.max, op1=ALU.add), m_)
            node4()
            if t % 8 == 7:
                a = t - 7
                outs.append(q.dma("s", s_fin, lambda e, a=a: e.dma_start(
                    out[a * 128:(a + 8) * 128, :].rearrange("(t p) d -> p t d", p=128), XS[:, a:a + 8, :]), evo[t]))
        outs.append(q.dma("s", s_fin, lambda e: e.dma_start(out[48 * 128:N, :], XS[0:N - 48 * 128, NT - 1, :]), evo[NT - 1]))
        q.wait("s", outs[-1])

        block = ctx.enter_context(nc.Block())

        @block.sync
        def _(e):
            for it in q.items["s"]:
                it(e)

        @block.gpsimd
        def _(e):
            for it in q.items["p"]:
                it(e)

        @block.scalar
        def _(e):
            for it in q.items["a"]:
                it(e)

        @block.tensor
        def _(e):
            for it in q.items["t"]:
                it(e)

        @block.vector
        def _(e):
            for it in q.items["v"]:
                it(e)


_INS = ['x', 'src', 'dst', 'edge_attr_128', 'edge_type_2', 'edge_type_200', 'L0_gnn_W1', 'L0_gnn_W2', 'L0_gnn_W3',
        'L0_gnn_re_attention_weight', 'L0_gnn_u', 'L0_gnn_en_weight', 'L0_gnn_re_weight',
        'L0_gnn_re_specific_attention', 'L1_gnn_W', 'L1_gnn_att_src', 'L1_gnn_att_dst', 'L1_gnn_bias',
        'L2_gnn_w_self_W', 'L2_gnn_w_self_b', 'L2_gnn_w_nei_W', 'L2_gnn_w_edge_W', 'L3_gnn_W_data', 'L3_gnn_b_data',
        'L3_gnn_W_control', 'L3_gnn_b_control', 'L3_gnn_W_self', 'L3_gnn_b_self']
_OUTS = [((6250, 128), 'float32')]


def kernel(**inputs):
    import numpy as _np
    import concourse.bacc as _bacc
    from concourse import mybir as _mybir
    from concourse.bass_utils import run_bass_kernel_spmd as _run

    nc = _bacc.Bacc("TRN2", target_bir_lowering=False, num_devices=1)
    arrays, args = {}, []
    for name in _INS:
        a = _np.ascontiguousarray(inputs[name])
        arrays[f"in_{name}_dram"] = a
        args.append(nc.dram_tensor(f"in_{name}_dram", a.shape, _mybir.dt.from_np(a.dtype), kind="ExternalInput").ap())
    for i, (shape, dtype) in enumerate(_OUTS):
        dt = _mybir.dt.from_np(_np.dtype(dtype))
        args.append(nc.dram_tensor(f"out_{i}_dram", shape, dt, kind="ExternalOutput").ap())
    program(nc, *args)
    r = _run(nc, [arrays], core_ids=[0])
    return r.results[0]["out_0_dram"]
```

```python
from contextlib import ExitStack

import concourse.bass as bass
from concourse import mybir

ALU = mybir.AluOpType
ACT = mybir.ActivationFunctionType
F32 = mybir.dt.float32
BF16 = mybir.dt.bfloat16
I32 = mybir.dt.int32
I16 = mybir.dt.int16
AX_X = mybir.AxisListType.X
RMAX = bass.bass_isa.ReduceOp.max
RADD = bass.bass_isa.ReduceOp.add

N = 6250
D = 128
E = 100000
NREL = 200
EP, EC = 125, 800
NT = 49
NP = NT * 128
NW = 25
WN = 256
NT0 = E // 128 + NW
NTL = (E + NW * 142) // 128
NTB = 7
TG, TJ = 16, 51
BIG = 1.0e30
PAD = 256 << 21
LAST = E - 128
SC_FIRST = 96


class Queues:

    def __init__(self, sems):
        self.names = ("v", "a", "t", "p", "s")
        self.items = {n: [] for n in self.names}
        self.sem = dict(sems)
        self.count = {n: 0 for n in self.names}
        self.seen = {n: {} for n in self.names}
        self.dcount = {}

    def wait(self, eng, *tokens):
        for tok in tokens:
            if tok is None:
                continue
            if isinstance(tok, list):
                self.wait(eng, *tok)
                continue
            sem, value = tok
            key = id(sem)
            if self.seen[eng].get(key, 0) >= value:
                continue
            self.seen[eng][key] = value
            self.items[eng].append(lambda e, s=sem, v=value: e.wait_ge(s, v))

    def op(self, eng, fn, *tokens):
        self.wait(eng, *tokens)
        self.count[eng] += 1
        sem = self.sem[eng]
        self.items[eng].append(lambda e: fn(e).then_inc(sem, 1))
        return (sem, self.count[eng])

    def quiet(self, eng, fn, *tokens):
        self.wait(eng, *tokens)
        self.items[eng].append(fn)

    def dma(self, eng, sem, fn, *tokens):
        self.wait(eng, *tokens)
        self.dcount[id(sem)] = self.dcount.get(id(sem), 0) + 16
        self.items[eng].append(lambda e: fn(e).then_inc(sem, 16))
        return (sem, self.dcount[id(sem)])

    def now(self, eng):
        return (self.sem[eng], self.count[eng])


def program(nc, x, src, dst, edge_attr_128, edge_type_2, edge_type_200,
            W1, W2, W3, relw, u, en_w, re_w, re_att,
            gW, att_src, att_dst, gbias,
            w_self_W, w_self_b, w_nei_W, w_edge_W,
            W_data, b_data, W_control, b_control, W_self, b_self, out, stop_at=99):
    ctx = ExitStack()
    with ctx:
        def sb(name, shape, dt=F32):
            return ctx.enter_context(nc.sbuf_tensor(name, shape, dt))

        def sem(name):
            return ctx.enter_context(nc.semaphore(name))

        def dram(name, shape, dt=F32):
            return nc.dram_tensor(name, shape, dt).ap()

        XS = sb("XS", [128, NT, D])
        HN = sb("HN", [128, NT, 144])
        RA = sb("RA", [128, 6528])
        RB = sb("RB", [128, NW * 290])
        RC = sb("RC", [128, 6528])
        RING = sb("RING", [128, 34, 145])
        GR = RING[:, :, :].rearrange("p a b -> p (a b)")
        IDX0 = sb("IDX0", [128, NTB * 128], I32)
        KEY0 = sb("KEY0", [128, NTB * 128])
        WE0 = sb("WE0", [128, NTB * 128])
        SC1 = sb("SC1", [128, NTB * 128])
        SC2 = sb("SC2", [128, NTB * 128])
        IDX1 = sb("IDX1", [128, NTB * 128], I32)
        KEY1 = sb("KEY1", [128, NTB * 128])
        OH = sb("OH", [128, 4, WN])
        OHB = sb("OHB", [128, 4, WN], BF16)
        OHT = sb("OHT", [128, 4, WN], BF16)
        WTAB0 = sb("WTAB0", [1, NTB * 128], I16)
        WTAB1 = sb("WTAB1", [1, NTB * 128], I16)
        IOTA = sb("IOTA", [128, WN])
        IOTAB = sb("IOTAB", [128, WN], BF16)
        IOI = sb("IOI", [128, WN], I32)
        IDENT = sb("IDENT", [128, 128])
        IDENTB = sb("IDENTB", [128, 128], BF16)
        TRI = sb("TRI", [128, 128])
        ONES = sb("ONES", [128, 128])
        BD = sb("BD", [128, 8])
        WT = sb("WT", [128, 12, 128])
        RHS1 = sb("RHS1", [128, 144])
        ADC = sb("ADC", [128, 16])
        COLS = sb("COLS", [128, 16])
        RELB = sb("RELB", [128, NREL])
        BIAS1 = sb("BIAS1", [128, D])
        ROWS = sb("ROWS", [1, 512])
        AD3 = sb("AD3", [128, 50, 24], BF16)
        ST = sb("ST", [128, 640])
        SI = sb("SI", [128, 64], I32)
        RDEG = sb("RDEG", [128, NT])
        CUM0 = sb("CUM0", [128, NW])

        PS = [ctx.enter_context(nc.psum_tensor(f"PS{i}", [128, 512], F32)) for i in range(8)]

        TAB = [dram(f"TAB{i}", (NP, D)) for i in range(3)]
        TABQ = dram("TABQ", (NP, 132))
        TABG = dram("TABG", (NP, 136))
        TAB2 = dram("TABN", (NP, D))
        TAB3 = dram("TABM", (2 * NP, D))
        SPB = dram("SPB", (128, NTL, 136))
        REC0 = dram("REC0", (NTB * 128 * 128, 1), I32)
        REC1 = dram("REC1", (E + 128, 1), I32)
        RECX = dram("RECX", (E // 16 + 1, 128), I32)
        RECA = dram("RECA", (E, 2), I32)
        RECB = dram("RECB", (E, 2), I32)
        EA = dram("EA", (E, D))
        TW0 = dram("TW0", (NTB, 128), I16)
        TW1 = dram("TW1", (NTB, 128), I16)
        TBT = dram("TBT", (NTB, 128), I32)
        KFD = dram("KFD", (128, NTB * 128))
        I3D = dram("I3D", (128, NTB * 128), I32)
        ATTD = dram("ATTD", (128, NW * WN))

        q = Queues({n: sem(f"e_{n}") for n in ("v", "a", "t", "p", "s")})
        s_in = [sem(f"in{i}") for i in range(40)]
        s_g = [sem(f"g{i}") for i in range(34)]
        s_h = [sem(f"h{i}") for i in range(16)]
        s_m = [sem(f"m{i}") for i in range(24)]
        s_r0, s_r1 = sem("r0"), sem("r1")
        s_fin = sem("fin")
        s_join = sem("join")

        def V(fn, *w):
            return q.op("v", fn, *w)

        def A(fn, *w):
            return q.op("a", fn, *w)

        def T(fn, *w):
            return q.op("t", fn, *w)

        def P(fn, *w):
            return q.op("p", fn, *w)

        def vv():
            return q.now("v")

        def VC(fn, *w):
            return q.op("v", fn, q.now("v"), *w)

        def load(i, dst_ap, src_ap, *w, eng="s"):
            return q.dma(eng, s_in[i], lambda e: e.dma_start(dst_ap, src_ap), *w)

        def affine(t_, op, fill, pattern, cm, base, *w):
            return P(lambda e: e.affine_select(out=t_, in_=t_, compare_op=op, fill=fill, base=base,
                                               pattern=pattern, channel_multiplier=cm), *w)

        c0 = P(lambda e: e.memset(IDENT[:, :], 0.0))
        c1 = P(lambda e: e.memset(TRI[:, :], 0.0))
        c_ones = P(lambda e: e.memset(ONES[:, :], 1.0))
        c2 = P(lambda e: e.memset(BD[:, :], 1.0))
        c_id = affine(IDENT[:, :], ALU.not_equal, 1.0, [[-1, 128]], 1, 0, c2)
        c_tri = affine(TRI[:, :], ALU.is_ge, 1.0, [[-1, 128]], 1, 0, c2)
        c3 = affine(BD[:, :], ALU.is_ge, 0.0, [[-16, 8]], 1, 0, c2)
        c_bd = affine(BD[:, :], ALU.is_ge, 0.0, [[16, 8]], -1, 15, c3)
        c4 = P(lambda e: e.iota(IOI[:, :], pattern=[[1, WN]], base=0, channel_multiplier=0))
        c_tt = P(lambda e: e.iota(SI[:, 0:NTB], pattern=[[128, NTB]], base=0, channel_multiplier=1))
        c5 = P(lambda e: e.tensor_copy(IOTA[:, :], IOI[:, :]), c4)
        c_io = P(lambda e: e.tensor_copy(IOTAB[:, :], IOI[:, :]), c4)
        c_idb = P(lambda e: e.tensor_copy(IDENTB[:, :], IDENT[:, :]), c_id)

        def edges(ap):
            return ap.rearrange("(p c) -> p c", c=EC)

        def slot(k, dt=I32):
            v = RA[0:EP, k * EC:(k + 1) * EC]
            return v if dt is F32 else v.bitcast(dt)

        def slotb(k, dt=I32):
            v = RC[0:EP, k * EC:(k + 1) * EC]
            return v if dt is F32 else v.bitcast(dt)

        l_src = load(0, slot(0), edges(src))
        l_dst = load(1, slot(1), edges(dst))
        l_nx = load(2, slotb(0)[0:124, :], dst[1:1 + 124 * EC].rearrange("(p c) -> p c", c=EC), eng="a")
        l_nx1 = load(3, slotb(0)[124:125, 0:EC - 1], dst[1 + 124 * EC:E].rearrange("(p c) -> p c", p=1), eng="a")
        l_nx2 = load(4, slotb(0)[124:125, EC - 1:EC], dst[E - 1:E].rearrange("(p c) -> p c", p=1), eng="a")
        l_t200 = load(5, slot(2), edges(edge_type_200))
        l_t2 = load(6, slot(3), edges(edge_type_2))
        m_x = P(lambda e: e.memset(XS[:, NT - 1, :], 0.0))
        l_x = load(7, XS[:, 0:NT - 1, :], x[0:48 * 128, :].rearrange("(t p) d -> p t d", p=128))
        l_x2 = load(8, XS[0:N - 48 * 128, NT - 1, :], x[48 * 128:N, :], m_x)

        names = [W1, W2, W3, en_w, re_w, gW, w_self_W, w_nei_W, w_edge_W, W_data, W_control, W_self]
        l_w = [load(9 + i, WT[:, i, :], a, eng="a") for i, a in enumerate(names)]
        (iW1, iW2, iW3, iEN, iRE, iGW, iSS, iNE, iED, iDA, iCO, iSE) = range(12)
        l_u = [load(i, COLS[:, k:k + 1], u[k * 128:(k + 1) * 128].rearrange("(p k) -> p k", k=1), eng="a")
               for k, i in enumerate((21, 35, 36))]
        l_ra = load(22, COLS[:, 3:4], re_att.rearrange("(p k) -> p k", k=1), eng="a")
        l_as = load(23, COLS[:, 4:5], att_src.rearrange("h (c k) -> (h c) k", k=1), eng="a")
        l_ad = load(24, COLS[:, 5:6], att_dst.rearrange("h (c k) -> (h c) k", k=1), eng="a")
        l_rel = load(25, RELB[:, :], relw.rearrange("(a n) -> a n", a=1).to_broadcast([128, NREL]), eng="a")
        l_gb = load(26, BIAS1[:, :], gbias.rearrange("(a n) -> a n", a=1).to_broadcast([128, D]), eng="a")
        l_b1 = load(27, ROWS[:, 0:128], w_self_b.rearrange("(a n) -> a n", a=1), eng="a")
        l_b2 = load(28, ROWS[:, 128:256], b_data.rearrange("(a n) -> a n", a=1), eng="a")
        l_b3 = load(29, ROWS[:, 256:384], b_control.rearrange("(a n) -> a n", a=1), eng="a")
        l_b4 = load(30, ROWS[:, 384:512], b_self.rearrange("(a n) -> a n", a=1), eng="a")

        m_pad = P(lambda e: e.memset(SC2[:, :].bitcast(I32), PAD))
        pads = []
        for b in range(NTB):
            def put(b=b):
                return q.dma("s", s_m[0], lambda e: e.dma_start(
                    REC0[b * 16384:(b + 1) * 16384, :].rearrange("(p l) o -> p (l o)", l=128),
                    SC2[:, 0:128].bitcast(I32)), m_pad)
            pads.append(put())
        d_pad = pads[-1]
        m_pad1 = P(lambda e: e.memset(SC2[0:1, 128:256].bitcast(I32), 8191 << 14), m_pad)
        d_pad1 = q.dma("s", s_m[1], lambda e: e.dma_start(
            REC1[E:E + 128, :].rearrange("(a l) o -> a (l o)", a=1), SC2[0:1, 128:256].bitcast(I32)), m_pad1)

        def cst(eng, *toks):
            q.wait(eng, *toks)

        def place(key, nb, padded, msk, scn, pos, posi, w0, tot_out, work, base_out=None):
            cnt, offs, tmp, tot = (work[:, 32 * k:32 * k + nb] for k in range(4))
            cum = work[:, 128:128 + nb]
            cols = []
            V(lambda e: e.memset(work[:, :], 0.0))
            for b in range(nb):
                def count(b=b):
                    return V(lambda e: e.tensor_scalar(msk[b % 2], key, float(b), None, ALU.is_equal, ALU.add,
                                                       accum_out=cnt[0:EP, b:b + 1]),
                             w0, q.now("v"))
                last = count()
            m1 = T(lambda e: e.matmul(PS[0][:, 0:nb], TRI[0:EP, :], cnt[0:EP, :], start=True, stop=True),
                   last, c_tri, c_idb)
            m2 = T(lambda e: e.matmul(PS[1][:, 0:nb], ONES[0:EP, :], cnt[0:EP, :], start=True, stop=True))
            V(lambda e: e.tensor_copy(tot, PS[1][:, 0:nb]), m2)
            VC(lambda e: e.tensor_copy(tmp, tot))
            if padded:
                ti = SI[:, 8:8 + nb]
                VC(lambda e: e.tensor_scalar(ti, tot, 127.0, None, ALU.add))
                VC(lambda e: e.tensor_scalar(ti, ti, 7, None, ALU.arith_shift_right))
                VC(lambda e: e.tensor_copy(tmp, ti))
            VC(lambda e: e.tensor_tensor_scan(cum, ONES[:, 0:nb], tmp, 0.0, ALU.mult, ALU.add))
            mul = 128.0 if padded else 1.0
            VC(lambda e: e.tensor_tensor(tmp, cum, tmp, ALU.subtract))
            VC(lambda e: e.tensor_scalar(tmp, tmp, mul, -1.0, ALU.mult, ALU.add))
            VC(lambda e: e.tensor_tensor(offs, tmp, PS[0][:, 0:nb], ALU.add), m1)
            for b in range(nb):
                def one(b=b):
                    k = b % 2
                    V(lambda e: e.tensor_scalar(msk[k].bitcast(I32), key, float(b), None, ALU.is_equal), q.now("v"))
                    VC(lambda e: e.tensor_tensor_scan(scn, work2[0:EP, :], msk[k].bitcast(I32),
                                                      offs[0:EP, b:b + 1], ALU.mult, ALU.add))
                    return VC(lambda e: e.copy_predicated(pos, msk[k].bitcast(I32), scn))
                one()
            return VC(lambda e: e.tensor_copy(posi, pos)), cum, tot

        work2 = RING[:, 0:6, :].rearrange("p a b -> p (a b)")[:, 0:EC]
        ringf = RING[:, 6:34, :].rearrange("p a b -> p (a b)")

        def rs(k):
            return ringf[0:EP, k * EC:(k + 1) * EC]

        V(lambda e: e.memset(work2, 1.0))
        wk, ws_, pos0 = rs(0), rs(1), rs(2)
        msk = [slotb(1, F32), slotb(2, F32)]
        wi = slotb(3)
        t_win = VC(lambda e: e.tensor_scalar(wi, slot(0), 8, None, ALU.arith_shift_right), l_src)
        t_key = VC(lambda e: e.tensor_copy(wk, wi))
        work0 = ST[:, 0:160]
        VC(lambda e: e.memset(pos0, 0.0))
        posi0 = slotb(4)
        t_pos0, cum0, tot0 = place(wk, NW, True, msk, ws_, pos0, posi0, [c_ones, t_key], None, work0)
        v0 = slotb(5)
        VC(lambda e: e.tensor_scalar(v0, slot(0), 255, 21, ALU.bitwise_and, ALU.logical_shift_left))
        VC(lambda e: e.tensor_scalar(wi, slot(1), 8, None, ALU.logical_shift_left), l_dst)
        VC(lambda e: e.tensor_tensor(v0, v0, wi, ALU.bitwise_or))
        t_v0 = VC(lambda e: e.tensor_tensor(v0, v0, slot(2), ALU.bitwise_or), l_t200)
        v1 = slot(4)
        VC(lambda e: e.tensor_scalar(wi, slot(3), 0.0, None, ALU.not_equal), l_t2)
        VC(lambda e: e.tensor_scalar(v1, slot(1), 14, None, ALU.logical_shift_left))
        VC(lambda e: e.tensor_tensor(v1, v1, wi, ALU.bitwise_or))
        VC(lambda e: e.tensor_scalar(wi, slot(0), 1, None, ALU.logical_shift_left))
        t_v1 = VC(lambda e: e.tensor_tensor(v1, v1, wi, ALU.bitwise_or))
        d_v1 = q.dma("s", s_m[2], lambda e: e.dma_start(
            REC1[0:E, :].rearrange("(p c) o -> p (c o)", c=EC), v1), t_v1)
        fl = SI[0:EP, 40:41]
        FLG = SI[:, 41:42]
        VC(lambda e: e.tensor_tensor(wi, slotb(0), slot(1), ALU.is_lt), l_nx, l_nx1, l_nx2)
        VC(lambda e: e.memset(ST[:, 620:621], 0.0))
        t_fl = VC(lambda e: e.tensor_reduce(ST[0:EP, 620:621], wi, AX_X, ALU.max))
        t_fa = P(lambda e: e.partition_all_reduce(ST[:, 621:622], ST[:, 620:621], 128, RMAX), t_fl)
        t_flag = VC(lambda e: e.tensor_copy(FLG, ST[:, 621:622]), t_fa)

        flag_regs = {}

        def general():
            outer_sem, outer_cnt = q.sem, q.count
            outer_seen = q.seen
            q.sem = {n: g_sem[n] for n in q.names}
            q.count = {n: 0 for n in q.names}
            q.seen = {n: {} for n in q.names}
            saved = q.items
            q.items = {n: [] for n in q.names}
            bufs = [RECA, RECB]
            eid = rs(4).bitcast(I32)
            vp = RB[0:EP, 0:2 * EC].bitcast(I32).rearrange("p (c k) -> p c k", k=2)
            kf, sc, ps_ = rs(0), rs(1), rs(2)
            ki = rs(3).bitcast(I32)
            mk = [RB[0:EP, 2 * EC:3 * EC], RB[0:EP, 3 * EC:4 * EC]]
            pi = RB[0:EP, 4 * EC:5 * EC].bitcast(I32)
            wrk = ST[:, 160:320]
            P(lambda e: e.iota(eid, pattern=[[1, EC]], base=0, channel_multiplier=EC), t_pos0)
            V(lambda e: e.tensor_copy(vp[:, :, 0], v1), q.now("p"))
            ld = VC(lambda e: e.tensor_copy(vp[:, :, 1], eid))
            done = None
            for r, (sh, nb) in enumerate(((14, 16), (18, 16), (22, NW))):
                if r:
                    ld = q.dma("s", g_m[0], lambda e, r=r: e.dma_start(
                        vp, bufs[(r - 1) % 2].rearrange("(p c) k -> p c k", c=EC)), done)
                VC(lambda e, sh=sh: e.tensor_scalar(ki, vp[:, :, 0], sh, None, ALU.arith_shift_right), ld)
                if nb == 16:
                    VC(lambda e: e.tensor_scalar(ki, ki, 15, None, ALU.bitwise_and))
                tk = VC(lambda e: e.tensor_copy(kf, ki))
                VC(lambda e: e.memset(ps_, 0.0))
                tp, _, _ = place(kf, nb, False, mk, sc, ps_, pi, [tk, ld], None, wrk)
                for c in range(EC):
                    done = q.dma("p", g_m[1], lambda e, c=c, r=r: e.indirect_dma_start(
                        bufs[r % 2], bass.IndirectOffsetOnAxis(ap=pi[:, c:c + 1], axis=0), vp[:, c, :], None), tp, ld)
            ld = q.dma("s", g_m[0], lambda e: e.dma_start(vp, bufs[0].rearrange("(p c) k -> p c k", c=EC)), done)
            VC(lambda e: e.tensor_copy(ki, vp[:, :, 0]), ld)
            t1 = VC(lambda e: e.tensor_copy(pi, vp[:, :, 1]))
            w1 = q.dma("s", g_m[2], lambda e: e.dma_start(
                REC1[0:E, :].rearrange("(p c) o -> p (c o)", c=EC), ki), t1, d_v1)
            G = RB[0:EP, 5 * EC:5 * EC + 16 * 128].rearrange("p (a d) -> p a d", d=128)
            EAV = EA.rearrange("(p c) d -> p c d", c=EC)
            prev = [None] * 2
            for b in range(EC // 8):
                h = b % 2
                for k in range(8):
                    c = b * 8 + k
                    ga = q.dma("p", g_g[h], lambda e, c=c, k=k, h=h: e.indirect_dma_start(
                        G[:, h * 8 + k, :], None, edge_attr_128,
                        bass.IndirectOffsetOnAxis(ap=pi[:, c:c + 1], axis=0)), prev[h], t1)
                prev[h] = q.dma("s", g_w[h], lambda e, b=b, h=h: e.dma_start(
                    EAV[:, b * 8:b * 8 + 8, :], G[:, h * 8:h * 8 + 8, :]), ga)
            q.wait("s", prev[0], prev[1], w1)
            ends = {n: q.now(n) for n in q.names if q.count[n]}
            for n in q.names:
                for m, tok in ends.items():
                    q.wait(n, tok)
            branch = q.items
            q.items, q.sem, q.count, q.seen = saved, outer_sem, outer_cnt, outer_seen
            return branch

        g_sem = {n: sem(f"ge_{n}") for n in ("v", "a", "t", "p", "s")}
        g_m = [sem(f"gm{i}") for i in range(3)]
        g_g = [sem(f"gg{i}") for i in range(2)]
        g_w = [sem(f"gw{i}") for i in range(2)]
        branch = general()
        for n in ("v", "t", "p", "s"):
            q.wait(n, t_flag, t_pos0, d_v1 if n == "s" else None)

            def enter(e, n=n):
                r = e.alloc_register(f"flag_{n}")
                e.load([r], FLG[0:1, 0:1])
                flag_regs[n] = r
                with e.If_ne(r, 0):
                    for it in branch[n]:
                        it(e)
                e.sem_inc(s_join, 1)
                e.wait_ge(s_join, 4)
            q.items[n].append(enter)

        d_x = q.dma("s", s_m[6], lambda e: e.dma_start(
            RECX, bass.AP(REC1.tensor, 0, [[16, E // 16 + 1], [1, 128]])), d_v1, d_pad1)

        sct = {}

        def scatter(c):
            def put(c=c):
                return q.dma("p", s_g[16 + c % 16], lambda e: e.indirect_dma_start(
                    REC0, bass.IndirectOffsetOnAxis(ap=posi0[:, c:c + 1], axis=0), v0[:, c:c + 1], None),
                    t_pos0, t_v0, d_pad, sct.get(c - 16))
            sct[c] = put()
        for c in range(SC_FIRST):
            scatter(c)

        tf = ST[:, 320:327]
        VC(lambda e: e.tensor_copy(tf, SI[:, 0:NTB]), c_tt, c_idb)

        def windows(cum, wout):
            VC(lambda e: e.memset(wout, 0.0))
            for b in range(1, NW):
                VC(lambda e, b=b: e.scalar_tensor_tensor(out=wout, in0=tf, scalar=cum[:, b - 1:b], in1=wout,
                                                         op0=ALU.is_ge, op1=ALU.add))

        W0F, W1F = ST[:, 328:335], ST[:, 336:343]
        windows(cum0, W0F)
        VC(lambda e: e.tensor_copy(CUM0[:, :], cum0))
        I16A = sb("I16A", [128, 16], I16)
        t_w0 = VC(lambda e: e.tensor_copy(I16A[:, 0:NTB], W0F))
        def ident_store(dst_ap, src_ap, s_, *w):
            return q.dma("s", s_, lambda e: e.dma_start(dst_ap.rearrange("b p -> p b"), src_ap,
                                                        allow_slow_non_contiguous=True), *w)
        d_w0 = ident_store(TW0, I16A[:, 0:NTB], s_m[3], t_w0)
        l_w0 = q.dma("s", s_m[4], lambda e: e.dma_start(WTAB0[0:1, :], TW0.rearrange("b p -> (b p)").rearrange("(a n) -> a n", a=1)), d_w0)

        cnt1 = ST[:, 352:352 + NW]
        tot1, nt1, cum1, st1, sh1 = (ST[:, 384 + 32 * k:384 + 32 * k + NW] for k in range(5))
        VC(lambda e: e.tensor_scalar(wi, slot(1), 8, None, ALU.arith_shift_right))
        VC(lambda e: e.tensor_copy(wk, wi))
        VC(lambda e: e.memset(cnt1, 0.0))
        for b in range(NW):
            t_c1 = VC(lambda e, b=b: e.tensor_scalar(msk[0], wk, float(b), None, ALU.is_equal, ALU.add,
                                                     accum_out=cnt1[0:EP, b:b + 1]))
        m3 = T(lambda e: e.matmul(PS[2][:, 0:NW], ONES[0:EP, :], cnt1[0:EP, :], start=True, stop=True), t_c1)
        VC(lambda e: e.tensor_copy(tot1, PS[2][:, 0:NW]), m3)
        ti = SI[:, 8:8 + NW]
        al1 = ST[:, 592:592 + NW]
        VC(lambda e: e.tensor_tensor_scan(st1, ONES[:, 0:NW], tot1, 0.0, ALU.mult, ALU.add))
        VC(lambda e: e.tensor_copy(ti, st1))
        VC(lambda e: e.tensor_scalar(ti, ti, 4, 4, ALU.arith_shift_right, ALU.logical_shift_left))
        VC(lambda e: e.tensor_copy(al1, ti))
        VC(lambda e: e.tensor_copy(nt1[:, 0:1], st1[:, 0:1]))
        VC(lambda e: e.tensor_tensor(nt1[:, 1:NW], st1[:, 1:NW], al1[:, 0:NW - 1], ALU.subtract))
        VC(lambda e: e.tensor_scalar(ti, nt1, 127.0, None, ALU.add))
        VC(lambda e: e.tensor_scalar(ti, ti, 7, None, ALU.arith_shift_right))
        VC(lambda e: e.tensor_copy(nt1, ti))
        VC(lambda e: e.tensor_tensor_scan(cum1, ONES[:, 0:NW], nt1, 0.0, ALU.mult, ALU.add))
        windows(cum1, W1F)
        VC(lambda e: e.scalar_tensor_tensor(out=sh1, in0=cum1, scalar=-128.0, in1=al1, op0=ALU.mult, op1=ALU.add))
        VC(lambda e: e.tensor_copy(nt1, sh1))
        VC(lambda e: e.tensor_tensor(nt1[:, 1:NW], sh1[:, 1:NW], sh1[:, 0:NW - 1], ALU.subtract))
        BTF, tm = ST[:, 544:551], ST[:, 552:559]
        VC(lambda e: e.tensor_scalar(BTF, tf, 128.0, None, ALU.mult))
        for b in range(1, NW):
            VC(lambda e, b=b: e.tensor_scalar(tm, tf, cum1[:, b - 1:b], nt1[:, b - 1:b], ALU.is_ge, ALU.mult))
            VC(lambda e: e.tensor_tensor(BTF, BTF, tm, ALU.add))
        BTA, DT, FT, W256 = ST[:, 560:567], ST[:, 568:575], ST[:, 576:583], ST[:, 584:591]
        VC(lambda e: e.tensor_scalar(BTF, BTF, float(E), None, ALU.min))
        VC(lambda e: e.tensor_scalar(BTA, BTF, float(LAST), None, ALU.min))
        VC(lambda e: e.tensor_tensor(DT, BTF, BTA, ALU.subtract))
        VC(lambda e: e.tensor_scalar(FT, DT, 0.0, None, ALU.is_gt))
        VC(lambda e: e.tensor_scalar(W256, W1F, 256.0, None, ALU.mult))
        VC(lambda e: e.tensor_copy(I16A[:, 8:8 + NTB], W1F))
        VC(lambda e: e.tensor_scalar(BTF, BTF, 0.0625, None, ALU.mult))
        VC(lambda e: e.tensor_copy(SI[:, 44:44 + NTB], BTF))
        t_tb = VC(lambda e: e.tensor_copy(SI[:, 52:52 + NTB], BTA))
        d1 = ident_store(TW1, I16A[:, 8:8 + NTB], s_m[5], t_tb)
        d3 = ident_store(TBT, SI[:, 52:52 + NTB], s_m[7], t_tb)
        l_w1 = q.dma("s", s_m[8], lambda e: e.dma_start(WTAB1[0:1, :], TW1.rearrange("b p -> (b p)").rearrange("(a n) -> a n", a=1)), d1)
        q.wait("s", d3)

        RR = RC[:, 0:NTB * 128].rearrange("p (b l) -> p b l", l=128)
        RRI = RR.bitcast(I32)
        t_rr = [q.dma("p", s_g[b], lambda e, b=b: e.indirect_dma_start(
            RRI[:, b, :], None, RECX, bass.IndirectOffsetOnAxis(ap=SI[:, 44 + b:45 + b], axis=0)), d_x, t_tb)
            for b in range(NTB)]
        for c in range(SC_FIRST, EC):
            scatter(c)
        t_sc = [sct[c] for c in range(EC - 16, EC)]
        RL = RC[:, NTB * 128:NTB * 128 + 128].bitcast(I32)
        RLF = RC[:, NTB * 128 + 128:NTB * 128 + 256]
        t_rl = q.dma("s", s_m[9], lambda e: e.dma_start(
            RL, REC1[LAST:E, :].rearrange("(a l) o -> a (l o)", a=1).to_broadcast([128, 128])), t_c1)

        KR = [HN[:, 0:49, :].rearrange("p a b -> p (a b)")[:, k * 896:(k + 1) * 896].rearrange("p (b l) -> p b l", l=128) for k in range(5)]
        DI1 = HN[:, :, :].rearrange("p a b -> p (a b)")[:, 5 * 896:6 * 896].bitcast(I32).rearrange("p (b l) -> p b l", l=128)

        def decode(DI, dst_f, srci, sh, mask, *w):
            if mask is None:
                VC(lambda e: e.tensor_scalar(DI, srci, sh, None, ALU.arith_shift_right), *w)
            else:
                VC(lambda e: e.tensor_scalar(DI, srci, sh, mask, ALU.arith_shift_right, ALU.bitwise_and), *w)
            return VC(lambda e: e.tensor_copy(dst_f, DI))

        def columns(dst_t, src_rows, tok, banks, prev_evac):
            last = prev_evac
            for half, (a, b) in enumerate(((0, 4), (4, NTB))):
                bank = PS[banks[half]]
                for k in range(a, b):
                    mt = T(lambda e, k=k, a=a, bank=bank: e.transpose(
                        bank[:, (k - a) * 128:(k - a + 1) * 128], src_rows[:, k, :], IDENT[:, :]),
                        tok, prev_evac, c_id)
                last = V(lambda e, a=a, b=b, bank=bank: e.tensor_copy(
                    dst_t[:, a * 128:b * 128], bank[:, 0:(b - a) * 128]), mt)
            return last

        decode(DI1, KR[0], RRI, 14, None, t_rr)
        decode(DI1, KR[1], RRI, 1, 8191)
        decode(DI1, KR[2], RRI, 0, 16383)
        KA = KR[3]
        VC(lambda e: e.tensor_copy(KR[4], KR[0]))
        for b in range(NTB):
            VC(lambda e, b=b: e.tensor_scalar(KR[4][:, b, :], KR[0][:, b, :], W256[:, b:b + 1], None, ALU.subtract))
        VC(lambda e: e.tensor_scalar(RL, RL, 14, None, ALU.arith_shift_right), t_rl)
        VC(lambda e: e.tensor_copy(RLF, RL))
        for b in range(NTB):
            lm = ST[:, 0:128]
            VC(lambda e, b=b: e.tensor_scalar(lm, IOTA[:, 0:128], DT[:, b:b + 1], -1.0e4, ALU.is_lt, ALU.mult), t_pos0, c_io)
            VC(lambda e: e.tensor_tensor(lm, lm, RLF, ALU.add))
            VC(lambda e, b=b: e.tensor_scalar(lm, lm, W256[:, b:b + 1], None, ALU.subtract))
            VC(lambda e, b=b: e.tensor_tensor(lm, lm, KR[4][:, b, :], ALU.subtract))
            VC(lambda e, b=b: e.scalar_tensor_tensor(out=KA[:, b, :], in0=lm, scalar=FT[:, b:b + 1],
                                                     in1=KR[4][:, b, :], op0=ALU.mult, op1=ALU.add))
        t_dec = vv()
        KEYA = SC1
        e1 = columns(KEYA, KA, t_dec, (0, 1), None)
        e1 = columns(KEY1, KR[4], t_dec, (2, 3), None)
        e1 = columns(WE0, KR[0], t_dec, (0, 1), e1)
        d_kf = q.dma("s", s_in[31], lambda e: e.dma_start(KFD, WE0[:, :]), e1)
        e1 = columns(IDX1, KR[1], t_dec, (2, 3), e1)
        t_i3 = columns(IDX0, KR[2], t_dec, (0, 1), e1)
        d_i3 = q.dma("s", s_in[32], lambda e: e.dma_start(I3D, IDX0[:, :]), t_i3)
        cst("v", c_io)

        wregs = {}

        def window(e, n, tab, t):
            key = n
            if key not in wregs:
                wregs[key] = [e.alloc_register(f"w_{n}_{i}") for i in range(8)]
            if t % 8 == 0:
                e.load(wregs[key], tab[0:1, t:t + 8])
            return e.snap(wregs[key][t % 8], min_val=0, max_val=NW - 1)

        GD = GR[:, 0:32 * 128].rearrange("p (a d) -> p a d", d=128)

        def run_gather(acc, tab, table, idx, key, wgt, ready, extra=None, n=NTL):
            mm = {}

            def fetch(t):
                s = t % 16
                tok = q.dma("p", s_g[s], lambda e: e.indirect_dma_start(
                    GD[:, s, :], None, table, bass.IndirectOffsetOnAxis(ap=idx[:, t:t + 1], axis=0)),
                    ready, mm.get(t - 16))
                return GD[:, s, :], tok
            return sum_pass(acc, tab, fetch, key, wgt, ready, extra, mm, n)

        def sum_pass(acc, tab, fetch, key, wgt, ready, extra, mm, n=NTL):
            ad, oh = {}, {}
            for t in range(n + 2):
                if t < n:
                    def tile(t=t):
                        wt = extra(t) if extra is not None else None
                        if wgt is None:
                            oh[t] = V(lambda e: e.tensor_scalar(OH[:, t % 4, :], IOTA[:, :], key[:, t:t + 1], None,
                                                                ALU.is_equal), mm.get(t - 4), ready)
                        else:
                            oh[t] = V(lambda e: e.tensor_scalar(OH[:, t % 4, :], IOTA[:, :], key[:, t:t + 1],
                                                                wgt[:, t:t + 1], ALU.is_equal, ALU.mult),
                                      mm.get(t - 4), ready, wt)
                        rows, tok = fetch(t)
                        mm[t] = T(lambda e: e.matmul(PS[t % 4][:, 0:WN], rows, OH[:, t % 4, :],
                                                     start=True, stop=True),
                                  oh[t], tok, ad.get(t - 4), ready)
                    tile()
                if t >= 2:
                    def add(t=t - 2):
                        def go(e):
                            w = window(e, "v", tab, t)
                            sl = acc[:, bass.ds(w * WN, WN)]
                            return e.tensor_tensor(sl, sl, PS[t % 4][:, 0:WN], ALU.add)
                        return V(go, mm[t], ad.get(t - 1), ready)
                    ad[t - 2] = add()
            return ad[n - 1]

        ATT = RB[:, 0:NW * WN]
        m_att = V(lambda e: e.memset(ATT, 0.0), vv())
        aregs = {}
        amm = {}
        toks_attr = {}
        AB = 8

        def attr_sp(e):
            r = e.alloc_register("flag_attr")
            e.load([r], FLG[0:1, 0:1])
            rr = [e.alloc_register(f"ba{i}") for i in range(8)]
            for which in (0, 1):
                with (e.If_eq(r, 0) if which == 0 else e.Else()):
                    table = edge_attr_128 if which == 0 else EA
                    for t in range(NTL):
                        s = t % 16
                        if t >= 16:
                            e.wait_ge(*amm[t - 16])
                        if t % 8 == 0:
                            e.load(rr, TBT.rearrange("b p -> (b p)").rearrange("(a n) -> a n", a=1)[0:1, t:t + 8])
                        v = e.snap(rr[t % 8], min_val=0, max_val=LAST)
                        e.dma_start(GD[:, s, :], table[bass.ds(v, 128), :]).then_inc(s_h[s], 16)

        q.wait("s", t_i3)
        q.items["s"].append(attr_sp)

        def attr_fetch(t):
            s = t % 16
            q.dcount[id(s_h[s])] = q.dcount.get(id(s_h[s]), 0) + 16
            return GD[:, s, :], (s_h[s], q.dcount[id(s_h[s])])

        t_att = sum_pass(ATT, WTAB1, attr_fetch, KEYA, None, [m_att, l_w1, t_i3, c_io], None, amm)
        d_att = q.dma("s", s_m[10], lambda e: e.dma_start(ATTD, ATT), t_att)

        def norm_pipe(pre, post, *w, pre_t=None):
            bs, mv, sd, rd = (ST[:, 0:6 * NT], ST[:, 6 * NT:8 * NT], ST[:, 8 * NT:9 * NT], ST[:, 9 * NT:10 * NT])
            mvv = mv.rearrange("p (t k) -> p t k", k=2)
            root = {}
            first = vv()

            def stats(g, k0, k1):
                if pre is not None:
                    pre(k0, k1)
                s0 = vv()
                for t in range(k0, k1):
                    V(lambda e, t=t: e.bn_stats(bs[:, 6 * t:6 * t + 6], XS[:, t, :]), first, s0, *w)
                s1 = vv()
                for t in range(k0, k1):
                    V(lambda e, t=t: e.bn_aggr(mv[:, 2 * t:2 * t + 2], bs[:, 6 * t:6 * t + 6]), s1)
                VC(lambda e: e.tensor_scalar(sd[:, k0:k1], mvv[:, k0:k1, 1], 1.0e-5, None, ALU.add))
                root[g] = A(lambda e: e.activation(sd[:, k0:k1], sd[:, k0:k1], ACT.Sqrt), vv())

            def norm(g, k0, k1):
                VC(lambda e: e.reciprocal(rd[:, k0:k1], sd[:, k0:k1]), root[g])
                s2 = vv()
                toks = {}
                for t in range(k0, k1):
                    toks[t] = V(lambda e, t=t: e.tensor_scalar(HN[:, t, 0:128], XS[:, t, :], mvv[:, t, 0:1],
                                                               rd[:, t:t + 1], ALU.subtract, ALU.mult), s2, *w)
                post(k0, k1, toks)

            if pre_t is not None:
                pre_t(0, 8)
            for g in range(8):
                if g < 7:
                    stats(g, 8 * g, min(8 * g + 8, NT))
                if g < 6 and pre_t is not None:
                    pre_t(8 * g + 8, min(8 * g + 16, NT))
                if g:
                    norm(g - 1, 8 * g - 8, min(8 * g, NT))

        def transposer(dst_t, *w):
            outs, ev = {}, {}

            def go(k0, k1, toks):
                for a in range(k0, k1, 4):
                    b = min(a + 4, k1)
                    bank = PS[6 + (a // 4) % 2]
                    for k in range(a, b):
                        mt = T(lambda e, k=k, a=a, bank=bank: e.transpose(
                            bank[:, (k - a) * 128:(k - a + 1) * 128], HN[:, k, 0:128], IDENT[:, :]),
                            toks[k], ev.get(a // 4 - 2))
                    ev[a // 4] = A(lambda e, a=a, b=b, bank=bank: e.activation(
                        dst_t[:, a * 128:b * 128], bank[:, 0:(b - a) * 128], ACT.Relu), mt, *w)
                    for k in range(a, b):
                        outs[k] = ev[a // 4]
            return go, outs

        def relu_rows(table, s_, k0, k1):
            r = A(lambda e: e.activation(HN[:, k0:k1, 0:128], HN[:, k0:k1, 0:128], ACT.Relu), q.now("t"))
            return store_rows(table, HN[:, :, 0:128], s_, k0, k1, r)

        def store_rows(table, src_v, s_, k0, k1, *w):
            tv = table.rearrange("(t p) d -> p t d", p=128)
            return q.dma("s", s_, lambda e: e.dma_start(tv[:, k0:k1, :], src_v[:, k0:k1, :]), *w)

        ACC = RA[:, 0:NW * WN]
        z0 = V(lambda e: e.memset(RA[:, NP:NW * WN], 0.0), t_c1)
        tr, ht = transposer(ACC, t_c1, t_v1, d_v1)
        HF = HN[:, :, 0:128]
        tab_tok = []

        def post0(k0, k1, toks):
            tr(k0, k1, toks)
            tab_tok.append(relu_rows(TAB[0], s_m[11], k0, k1))
        norm_pipe(None, post0, l_x, l_x2, t_i3)
        d_tab = tab_tok[-1]
        ht = list(ht.values())

        R0 = RC[:, 0:NTB * 128].rearrange("p (b l) -> p b l", l=128)
        l_r0 = q.dma("s", s_m[12], lambda e: e.dma_start(
            R0.bitcast(I32), REC0.rearrange("(b p l) o -> p b (l o)", p=128, l=128)), t_sc, t_dec)
        K0 = [RC[:, (k + 1) * 896:(k + 2) * 896].rearrange("p (b l) -> p b l", l=128) for k in range(3)]
        DI0 = RC[:, 4 * 896:5 * 896].bitcast(I32).rearrange("p (b l) -> p b l", l=128)
        decode(DI0, K0[0], R0.bitcast(I32), 21, None, l_r0, t_sc)
        decode(DI0, K0[1], R0.bitcast(I32), 8, 8191)
        decode(DI0, K0[2], R0.bitcast(I32), 0, 255)
        t_d0 = vv()
        TYP = SC1
        cst("v", d_kf, d_i3)
        e0 = columns(KEY0, K0[0], t_d0, (0, 1), t_att)
        e0 = columns(IDX0, K0[1], t_d0, (2, 3), t_att)
        e0 = columns(TYP, K0[2], t_d0, (0, 1), e0)
        t_e0 = e0

        wsel_s = RC[:, 5 * 896:5 * 896 + 2 * NREL]

        def wsel(t):
            return V(lambda e: e.scalar_tensor_tensor(
                out=wsel_s[:, (t % 2) * NREL:(t % 2 + 1) * NREL], in0=IOTA[:, 0:NREL], scalar=TYP[:, t:t + 1], in1=RELB[:, :],
                op0=ALU.is_equal, op1=ALU.mult, accum_out=WE0[:, t:t + 1]), l_rel, t_e0, ws_prev.get(t - 2))
        ws_prev = {}

        def wsel_first(t):
            if t == 0:
                ws_prev[0] = wsel(0)
            if t + 1 < NT0:
                ws_prev[t + 1] = wsel(t + 1)
            return ws_prev[t]

        V3R, U3B = RC[:, 5376 + 512:5376 + 640], RC[:, 5376 + 640:5376 + 768]
        t_ = V(lambda e: e.tensor_copy(U3B, COLS[:, 2:3].to_broadcast([128, 128])), l_u, t_e0)
        m = T(lambda e: e.matmul(PS[4][:, 0:128], U3B, WT[:, iEN, :], start=True, stop=True), t_, l_w[iEN], *ht)
        t_v3 = V(lambda e: e.tensor_copy(V3R, PS[4][:, 0:128]), m)
        t_q2 = V(lambda e: e.memset(HN[:, :, 129:132], 0.0), d_i3)

        acc_tok = [ht, z0]
        tabs = [TAB[0], TAB[1], TAB[2], TABQ]
        for layer, iw in enumerate((iW1, iW2, iW3)):
            done = run_gather(ACC, WTAB0, tabs[layer], IDX0, KEY0, WE0,
                              [d_tab, l_w0, t_e0, *([] if layer else [*ht, z0])],
                              extra=wsel_first if layer == 0 else None, n=NT0)
            ev, mt = {}, {}
            for g in range(13):
                k0, k1 = 4 * g, min(4 * g + 4, NT)
                bank = PS[4 + g % 3]
                for k in range(k0, k1):
                    mt[g] = T(lambda e, k=k, k0=k0, bank=bank, iw=iw: e.matmul(
                        bank[:, (k - k0) * 128:(k - k0 + 1) * 128], ACC[:, k * 128:(k + 1) * 128], WT[:, iw, :],
                        start=True, stop=True), done, ev.get(g - 3), l_w[iw])
                ev[g] = A(lambda e, k0=k0, k1=k1, bank=bank: e.activation(
                    HN[:, k0:k1, 0:128], bank[:, 0:(k1 - k0) * 128].rearrange("p (a b) -> p a b", b=128), ACT.Tanh),
                    mt[g], d_tab, t_v3)
                if layer < 2 and g % 2 == 1 or g == 12 and layer < 2:
                    a = 8 * (g // 2)
                    d_new = store_rows(tabs[layer + 1], HF, s_m[13 + layer], a, k1, ev[g])
                if layer == 2:
                    for k in range(k0, k1):
                        tq = V(lambda e, k=k: e.scalar_tensor_tensor(
                            out=OH[:, k % 2, 0:128], in0=HN[:, k, 0:128], scalar=1.0, in1=V3R, op0=ALU.mult,
                            op1=ALU.mult, accum_out=HN[:, k, 128:129]), ev[g], t_v3, t_q2, *([vv()] if k % 2 == 0 else []))
                    if g % 2 == 1 or g == 12:
                        a = 8 * (g // 2)
                        d_q = store_rows(TABQ, HN[:, :, 0:132], s_m[15], a, k1, tq)
            d_tab = d_new
            ev2 = {}
            for g in range(13):
                c0_, c1_ = 512 * g, min(512 * g + 512, NW * WN)
                bank = PS[g % 4]
                m = T(lambda e, c0_=c0_, c1_=c1_, bank=bank, iw=iw: e.matmul(
                    bank[:, 0:c1_ - c0_], WT[:, iw, :], ACC[:, c0_:c1_], start=True, stop=True), ev2.get(g - 4))
                ev2[g] = A(lambda e, c0_=c0_, c1_=c1_, bank=bank: e.activation(
                    ACC[:, c0_:c1_], bank[:, 0:c1_ - c0_], ACT.Tanh), m)
            acc_tok = [ev2[12]]
            cst("v", ev2[12])
            hn_ev = ev

        if stop_at == 0:
            pass

        m = T(lambda e: e.matmul(PS[4][:, 0:1], WT[:, iEN, :], COLS[:, 0:1], start=True, stop=True), l_u, l_w[iEN], hn_ev[12])
        m = T(lambda e: e.transpose(PS[4][:, 128:256], WT[:, iRE, :], IDENT[:, :]), l_w[iRE])
        V(lambda e: e.tensor_copy(COLS[:, 6:7], PS[4][:, 0:1]), m)
        RET = ST[:, 500:628]
        VC(lambda e: e.tensor_copy(RET, PS[4][:, 128:256]))
        m = T(lambda e: e.matmul(PS[5][:, 0:1], RET, COLS[:, 3:4], start=True, stop=True), vv(), l_ra)
        VC(lambda e: e.tensor_tensor(COLS[:, 8:9], PS[5][:, 0:1], COLS[:, 1:2], ALU.mult), m)
        m = T(lambda e: e.matmul(PS[5][:, 1:2], ONES[:, :], COLS[:, 8:9], start=True, stop=True), vv())
        VC(lambda e: e.tensor_copy(COLS[:, 9:10], PS[5][:, 1:2]), m)
        V1B = RC[:, 512:640]
        t_v1b = VC(lambda e: e.tensor_copy(V1B, COLS[:, 6:7].to_broadcast([128, 128])), done)
        PB = RB[:, 0:NW * WN]
        ev2 = {}
        for g in range(13):
            c0_, c1_ = 512 * g, min(512 * g + 512, NW * WN)
            bank = PS[g % 4]
            m = T(lambda e, c0_=c0_, c1_=c1_, bank=bank: e.matmul(
                bank[:, 0:c1_ - c0_], V1B, ACC[:, c0_:c1_], start=True, stop=True), ev2.get(g - 4), t_v1b, acc_tok)
            ev2[g] = A(lambda e, c0_=c0_, c1_=c1_, bank=bank: e.activation(
                PB[:, c0_:c1_], bank[:, 0:c1_ - c0_], ACT.Copy), m, d_att)
        t_pb = ev2[12]
        t_accfree = m

        GS = 11
        NG = -(-NT0 // GS)
        S0, QE = SC1, SC2
        MG, FG, ZG = ST[:, 0:80], ST[:, 80:160], ST[:, 160:240]
        GM, SW = ST[:, 240:320], ST[:, 320:352]
        MR = ST[0:1, 352:356]
        junk = RC[:, 0:2 * WN].rearrange("p (a b) -> p a b", b=WN)
        RG0 = GR[:, 0:3 * GS * 132].rearrange("p (a d) -> p a d", d=132)
        z1 = V(lambda e: e.memset(ACC, 0.0), t_accfree, d_q)
        V(lambda e: e.memset(ZG, 0.0))
        t_z0 = V(lambda e: e.tensor_scalar(WE0[:, 0:NT0], KEY0[:, 0:NT0], 255.5, -BIG, ALU.is_gt, ALU.mult), done)
        pe_t, gat, ohb, oh0, mm0, ad0, lasts0, exp_t, fac_t = {}, {}, {}, {}, {}, {}, {}, {}, {}
        tm0 = {}

        def gather0(t):
            s = t % (3 * GS)
            gat[t] = q.dma("p", s_g[s], lambda e: e.indirect_dma_start(
                RG0[:, s, :], None, TABQ, bass.IndirectOffsetOnAxis(ap=IDX0[:, t:t + 1], axis=0)),
                d_q, done, mm0.get(t - 3 * GS), tm0.get(t // GS - 3))

        def score(t):
            def go(e):
                w = window(e, "v", WTAB0, t)
                return e.scalar_tensor_tensor(out=junk[:, t % 2, :], in0=IOTA[:, :], scalar=KEY0[:, t:t + 1],
                                              in1=PB[:, bass.ds(w * WN, WN)], op0=ALU.is_equal, op1=ALU.mult,
                                              accum_out=S0[:, t:t + 1])
            pe_t[t] = V(go, t_pb, pe_t.get(t - 2), done)

        def group_of(g):
            return slice(g * GS, min(g * GS + GS, NT0))

        def stage1(g):
            sl = group_of(g)
            n = sl.stop - sl.start
            s = sl.start % (3 * GS)
            tm0[g] = V(lambda e: e.tensor_tensor(S0[:, sl], S0[:, sl], RG0[:, s:s + n, 128], ALU.add),
                       [gat[t] for t in range(sl.start, sl.stop)], vv())

        def stage2(g):
            sl = group_of(g)
            V(lambda e: e.tensor_scalar(S0[:, sl], S0[:, sl], COLS[:, 9:10], None, ALU.add), tm0[g])

        def stage3(g):
            sl = group_of(g)
            V(lambda e: e.scalar_tensor_tensor(out=QE[:, sl], in0=S0[:, sl], scalar=0.01, in1=S0[:, sl],
                                               op0=ALU.mult, op1=ALU.max), vv())

        def stage4(g):
            sl = group_of(g)
            V(lambda e: e.tensor_tensor(QE[:, sl], QE[:, sl], WE0[:, sl], ALU.add), vv(), t_z0)

        def stage5(g):
            sl = group_of(g)
            t_ = V(lambda e: e.tensor_reduce(GM[:, g:g + 1], QE[:, sl], AX_X, ALU.max), vv())
            st_m[g] = T(lambda e: e.matmul(PS[4 + g % 2][0:1, 0:128], GM[:, g:g + 1], IDENT[:, :],
                                           start=True, stop=True), t_, st_b.get(g - 2))

        def stage6(g):
            t_ = V(lambda e: e.tensor_reduce(MR[:, g % 4:g % 4 + 1], PS[4 + g % 2][0:1, 0:128], AX_X, ALU.max),
                   st_m[g], vv())
            st_m[g] = T(lambda e: e.matmul(PS[6 + g % 2][:, 0:1], ONES[0:1, :], MR[:, g % 4:g % 4 + 1],
                                           start=True, stop=True), t_)

        def stage7(g):
            sl = group_of(g)
            if g == 0:
                t_ = V(lambda e: e.tensor_copy(MG[:, 0:1], PS[6][:, 0:1]), st_m[0], vv())
            else:
                t_ = V(lambda e: e.tensor_tensor(MG[:, g:g + 1], MG[:, g - 1:g], PS[6 + g % 2][:, 0:1], ALU.max),
                       st_m[g], vv())
            st_b[g] = t_
            fac_t[g] = A(lambda e: e.activation(FG[:, g:g + 1], MG[:, g:g + 1], ACT.Exp,
                                                bias=MG[:, max(g - 1, 0):max(g - 1, 0) + 1], scale=-1.0), t_)

        def stage8(g):
            sl = group_of(g)
            t_ = V(lambda e: e.tensor_scalar(QE[:, sl], QE[:, sl], MG[:, g:g + 1], None, ALU.subtract), vv())
            exp_t[g] = A(lambda e: e.activation(S0[:, sl], QE[:, sl], ACT.Exp, accum_out=ZG[:, g:g + 1]), t_)

        def apply0(t):
            g = t // GS
            s = t % (3 * GS)
            ohb[t] = V(lambda e: e.tensor_scalar(OHB[:, t % 4, :], IOTAB[:, :], KEY0[:, t:t + 1], None, ALU.is_equal),
                       oh0.get(t - 4), done)
            oh0[t] = A(lambda e: e.activation(OH[:, t % 4, :], OHB[:, t % 4, :], ACT.Copy, scale=S0[:, t:t + 1]),
                       ohb[t], exp_t[g], mm0.get(t - 4))
            mm0[t] = T(lambda e: e.matmul(PS[t % 4][:, 0:WN], RG0[:, s, 0:128], OH[:, t % 4, :],
                                          start=True, stop=True), oh0[t], gat[t], ad0.get(t - 4), t_pb)

        def add0(t):
            g = t // GS
            first = t % GS == 0

            def go(e):
                w = window(e, "v2", WTAB0, t)
                sl = ACC[:, bass.ds(w * WN, WN)]
                if first:
                    return e.scalar_tensor_tensor(out=sl, in0=sl, scalar=FG[:, g:g + 1], in1=PS[t % 4][:, 0:WN],
                                                  op0=ALU.mult, op1=ALU.add)
                return e.tensor_tensor(sl, sl, PS[t % 4][:, 0:WN], ALU.add)
            ad0[t] = V(go, mm0[t], ad0.get(t - 1), z1, fac_t[g] if first else None)

        st_m, st_b = {}, {}
        stages = [stage1, stage2, stage3, stage4, stage5, stage6, stage7, stage8]
        at = [3, 3, 3, 4, 4, 6, 8, 8]
        LAG = GS + 10
        for t in range(NT0 + GS + LAG + 4):
            if t < NT0:
                gather0(t)
                score(t)
            for k, fn in enumerate(stages):
                g, r = divmod(t - GS - at[k], GS)
                if r == 0 and 0 <= g < NG:
                    fn(g)
            if 0 <= t - LAG < NT0:
                apply0(t - LAG)
            if 0 <= t - LAG - 3 < NT0:
                add0(t - LAG - 3)
        d_l0 = ad0[NT0 - 1]
        MX = MG[:, NG - 1:NG]
        VC(lambda e: e.tensor_scalar(GM[:, 0:NG], MG[:, 0:NG], MX, None, ALU.subtract), q.now("a"))
        t_ = A(lambda e: e.activation(GM[:, 0:NG], GM[:, 0:NG], ACT.Exp), vv())
        VC(lambda e: e.tensor_tensor(ZG[:, 0:NG], ZG[:, 0:NG], GM[:, 0:NG], ALU.mult), t_)
        VC(lambda e: e.tensor_reduce(COLS[:, 12:13], ZG[:, 0:NG], AX_X, ALU.add))
        t_z = P(lambda e: e.partition_all_reduce(COLS[:, 13:14], COLS[:, 12:13], 128, RADD), vv())
        VC(lambda e: e.tensor_scalar(RC[:, 0:NG], IOTA[:, 0:NG], float(GS), None, ALU.mult))
        for w in range(NW):
            VC(lambda e, w=w: e.tensor_scalar(RC[:, 128:128 + NG], RC[:, 0:NG], CUM0[:, w:w + 1], None, ALU.is_lt))
            VC(lambda e, w=w: e.tensor_tensor(RC[:, 256:256 + NG], RC[:, 128:128 + NG], GM[:, 0:NG], ALU.mult))
            VC(lambda e, w=w: e.tensor_reduce(SW[:, w:w + 1], RC[:, 256:256 + NG], AX_X, ALU.max))
        VC(lambda e: e.reciprocal(COLS[:, 14:15], COLS[:, 13:14]), t_z)
        t_sw = VC(lambda e: e.tensor_scalar(SW[:, 0:NW], SW[:, 0:NW], COLS[:, 14:15], None, ALU.mult))

        def two_phase_a(table, wd, idx, gs, nring, spill, ready, per_tile, per_group, s_sp):
            RG = GR[:, 0:nring * wd].rearrange("p (a d) -> p a d", d=wd)
            free = {}
            t0 = 0
            groups = []
            while t0 < NTL:
                t1 = min(t0 + gs, (t0 // TJ + 1) * TJ if gs == 17 else NTL, NTL)
                groups.append((t0, t1))
                t0 = t1
            ngr = nring // gs
            toks = {}
            lasts = []
            for gi, (a, b) in enumerate(groups):
                base = (gi % ngr) * gs
                for t in range(a, b):
                    s = base + t - a
                    toks[t] = q.dma("p", s_g[s], lambda e, s=s, t=t: e.indirect_dma_start(
                        RG[:, s, :], None, table, bass.IndirectOffsetOnAxis(ap=idx[:, t:t + 1], axis=0)),
                        ready, free.get(gi - ngr))
                    per_tile(t)
                gt = [toks[t] for t in range(a, b)]
                d = q.dma("s", s_sp[gi % ngr], lambda e, a=a, b=b, base=base: e.dma_start(
                    spill[:, a:b, :], RG[:, base:base + b - a, :]), gt)
                free[gi] = [d, per_group(gi, a, b, RG[:, base:base + b - a, :], gt)]
                lasts.append(d)
            return lasts[-ngr:]

        V(lambda e: e.tensor_scalar(ADC[:, 0:8], BD[:, :], COLS[:, 4:5], None, ALU.mult), l_as, c_bd, c_idb)
        t_adc = V(lambda e: e.tensor_scalar(ADC[:, 8:16], BD[:, :], COLS[:, 5:6], None, ALU.mult), l_ad)
        m = T(lambda e: e.transpose(PS[0][:, 0:128], WT[:, iGW, :], IDENT[:, :]), l_w[iGW], d_l0)
        t_ = VC(lambda e: e.tensor_copy(RET, PS[0][:, 0:128]), m)
        m = T(lambda e: e.matmul(PS[1][:, 0:16], RET, ADC[:, :], start=True, stop=True), t_, t_adc)
        V(lambda e: e.tensor_copy(RHS1[:, 128:144], PS[1][:, 0:16]), m)
        t_rhs = V(lambda e: e.tensor_copy(RHS1[:, 0:128], WT[:, iGW, :]))
        evt, mtt = {}, {}

        def pre1_t(k0, k1):
            for k in range(k0, k1):
                g = k // 4
                mtt[k] = T(lambda e, k=k, g=g: e.transpose(
                    PS[4 + g % 2][:, (k % 4) * 128:(k % 4 + 1) * 128], ACC[:, k * 128:(k + 1) * 128], IDENT[:, :]),
                    d_l0, evt.get(g - 2))

        def pre1(k0, k1):
            for k in range(k0, k1, 2):
                c = min(k + 2, k1)
                g = k // 4
                evt[g] = V(lambda e, k=k, c=c, g=g: e.scalar_tensor_tensor(
                    out=XS[:, k:c, :],
                    in0=PS[4 + g % 2][:, (k % 4) * 128:(k % 4 + c - k) * 128].rearrange("p (a b) -> p a b", b=128),
                    scalar=SW[:, k // 2:k // 2 + 1], in1=XS[:, k:c, :], op0=ALU.mult, op1=ALU.add), mtt[min(4 * g + 3, k1 - 1)], t_sw)

        tr, ht = transposer(ACC)
        ev, evk = {}, {}
        cnt_g = [0]
        tab_tok = []

        def post1(k0, k1, toks):
            tr(k0, k1, toks)
            for a in range(k0, k1, 3):
                b = min(a + 3, k1)
                g = cnt_g[0]
                cnt_g[0] += 1
                bank = PS[g % 4]
                for k in range(a, b):
                    mt_ = T(lambda e, k=k, a=a, bank=bank: e.matmul(
                        bank[:, (k - a) * 144:(k - a + 1) * 144], ACC[:, k * 128:(k + 1) * 128], RHS1[:, :],
                        start=True, stop=True), ht[k], t_rhs, ev.get(g - 4))
                ev[g] = A(lambda e, a=a, b=b, bank=bank: e.activation(
                    HN[:, a:b, :], bank[:, 0:(b - a) * 144].rearrange("p (a b) -> p a b", b=144), ACT.Copy), mt_)
            tab_tok.append(store_rows(TABG, HN[:, :, 0:136], s_m[11], k0, k1, ev[g]))
        norm_pipe(pre1, post1, pre_t=pre1_t)
        t_hw = ev[max(ev)]
        d_g = tab_tok[-1]
        t_x1 = evt[12]
        AR = ST[:, 0:NT * 8].rearrange("p (t h) -> p t h", h=8)
        AF = RC[:, 0:NT * 8].rearrange("p (t h) -> p t h", h=8)
        V(lambda e: e.memset(AD3[:, :, :], 0.0), t_rhs)
        VC(lambda e: e.tensor_copy(AR, HN[:, :, 136:144]), t_hw)
        for k in range(3):
            part = AD3[:, 0:NT, 8 * k:8 * k + 8]
            VC(lambda e, part=part: e.tensor_copy(part, AR))
            if k < 2:
                VC(lambda e, part=part: e.tensor_copy(AF, part))
                VC(lambda e: e.tensor_tensor(AR, AR, AF, ALU.subtract))
        t_ad3 = vv()
        EE = RA[:, :].rearrange("p (j g h) -> p j g h", g=TG, h=8)
        AE = RB[:, 0:6528].rearrange("p (j g h) -> p j g h", g=TG, h=8)
        z2 = VC(lambda e: e.memset(RA[:, :], 0.0), [ev[k] for k in ev])
        z3 = VC(lambda e: e.memset(RB[:, 0:6528], 0.0))
        ohb, tr, oht, lk, evd = {}, {}, {}, {}, {}
        pend = []

        def lk_tile(t):
            gi = t // 17
            j0 = t % TJ
            ohb[t] = V(lambda e: e.tensor_scalar(OHB[:, t % 4, :], IOTAB[:, :], KEY1[:, t:t + 1], None, ALU.is_equal),
                       tr.get(t - 4), z3)
            pb = PS[4 + t % 4][:, 0:128].bitcast(BF16)
            for h in range(2):
                tr[t] = T(lambda e, h=h: e.transpose(pb[:, h * 128:h * 128 + 128],
                                                     OHB[:, t % 4, h * 128:(h + 1) * 128], IDENTB[:, :]),
                          ohb[t], oht.get(t - 4), c_idb)
            oht[t] = A(lambda e: e.activation(OHT[:, t % 4, :], pb, ACT.Copy),
                       tr[t], lk.get(t - 4))
            pend.append(t)
            if len(pend) > 2 or t == NTL - 1:
                while len(pend) > (0 if t == NTL - 1 else 2):
                    look(pend.pop(0))

        def look(t):
            gi = grp_of[t]
            c = (t - grp_start[t]) * 24
            bank = PS[gi % 3]

            def go(e, h):
                w = window(e, "t", WTAB1, t) if h == 0 else wlast["v"]
                wlast["v"] = w
                return e.matmul(bank[:, c:c + 24], OHT[:, t % 4, h * 128:(h + 1) * 128],
                                AD3[:, bass.ds(w * 2 + h, 1), :].rearrange("p a b -> p (a b)"),
                                start=(h == 0), stop=(h == 1))
            T(lambda e: go(e, 0), oht[t], t_ad3, evd.get(gi - 3))
            lk[t] = T(lambda e: go(e, 1))
            if t == grp_end[t]:
                a, b = grp_start[t], t + 1
                tg, j = a // TJ, a % TJ
                pv = bank[:, 0:24 * (b - a)].rearrange("p (t k h) -> p t h k", k=3, h=8)
                evd[gi] = V(lambda e: e.tensor_reduce(AE[:, j:j + b - a, tg, :], pv, AX_X, ALU.add), lk[t], z3)

        wlast = {}
        grp_of, grp_start, grp_end = {}, {}, {}
        t0, gi = 0, 0
        while t0 < NTL:
            t1 = min(t0 + 17, (t0 // TJ + 1) * TJ, NTL)
            for t in range(t0, t1):
                grp_of[t], grp_start[t], grp_end[t] = gi, t0, t1 - 1
            t0, gi = t1, gi + 1

        def as_group(gi, a, b, rows, gt):
            tg, j = a // TJ, a % TJ
            return A(lambda e: e.activation(EE[:, j:j + b - a, tg, :], rows[:, :, 128:136], ACT.Copy), gt, z2)

        cst("v", t_x1)
        sp1 = two_phase_a(TABG, 136, IDX1, 17, 34, SPB, [d_g, t_i3, d_l0], lk_tile, as_group, [s_m[20], s_m[21]])
        VC(lambda e: e.tensor_tensor(RA[:, :], RA[:, :], RB[:, 0:6528], ALU.add), q.now("a"))
        VC(lambda e: e.scalar_tensor_tensor(out=RA[:, :], in0=RA[:, :], scalar=0.2, in1=RA[:, :],
                                            op0=ALU.mult, op1=ALU.max))
        IN = SC1[:, 0:TG * TJ]
        VC(lambda e: e.memset(SC1[:, NTL:TG * TJ], -BIG))
        VC(lambda e: e.tensor_scalar(IN[:, 0:NTL], KEY1[:, 0:NTL], 255.5, -BIG, ALU.is_gt, ALU.mult))
        VC(lambda e: e.tensor_scalar(SC2[:, 0:NTL], KEY1[:, 0:NTL], -0.5, -BIG, ALU.is_lt, ALU.mult))
        VC(lambda e: e.tensor_tensor(IN[:, 0:NTL], IN[:, 0:NTL], SC2[:, 0:NTL], ALU.add))
        for g in range(TG):
            V(lambda e, g=g: e.tensor_tensor(EE[:, :, g, :], EE[:, :, g, :],
                                             IN[:, g * TJ:(g + 1) * TJ].unsqueeze(2).to_broadcast([128, TJ, 8]),
                                             ALU.add), *( [vv()] if g == 0 else []))
        t_e = vv()
        RK8 = RC[:, :].rearrange("p (j g h) -> p j g h", g=TG, h=8)
        l_kf = q.dma("s", s_in[33], lambda e: e.dma_start(SC2[:, :], KFD), d_kf, vv())
        VC(lambda e: e.memset(SC2[:, NTL:TG * TJ], 8191.0), l_kf)
        s_ = vv()
        for g in range(TG):
            V(lambda e, g=g: e.tensor_copy(RK8[:, :, g, :],
                                           SC2[:, g * TJ:(g + 1) * TJ].unsqueeze(2).to_broadcast([128, TJ, 8])), s_)
        t_k8 = vv()
        ROWE = RB[:, 0:6528]

        def blocks(dst_t, src_t, tok, act, out_tok=None):
            evb, mb = {}, {}
            for g in range(13):
                j0, j1 = 4 * g, min(4 * g + 4, TJ)
                bank = PS[g % 4]
                for j in range(j0, j1):
                    mb[g] = T(lambda e, j=j, j0=j0, bank=bank: e.transpose(
                        bank[:, (j - j0) * 128:(j - j0 + 1) * 128], src_t[:, j * 128:(j + 1) * 128], IDENT[:, :]),
                        tok, evb.get(g - 4))
                evb[g] = act(g, j0, j1, bank, mb[g], mb)
            return evb[12]

        def copy_to(dst_t):
            def f(g, j0, j1, bank, mtok, _):
                return A(lambda e: e.activation(dst_t[:, j0 * 128:j1 * 128], bank[:, 0:(j1 - j0) * 128], ACT.Copy),
                         mtok)
            return f
        t_re = blocks(ROWE, RA, t_e, copy_to(ROWE))
        t_rk = blocks(RC, RC, [t_k8, t_re], copy_to(RC))
        VC(lambda e: e.tensor_copy(COLS[:, 0:1], RC[:, 0:1]), t_rk)
        VC(lambda e: e.tensor_copy(COLS[:, 1:2], RC[:, 6527:6528]))
        BN = HX = None
        BND = GR[:, 0:3264].bitcast(BF16)
        VC(lambda e: e.tensor_tensor(BND[:, 1:6528], RC[:, 1:6528], RC[:, 0:6527], ALU.not_equal), sp1)
        VC(lambda e: e.memset(BND[:, 0:1], 0.0))
        VC(lambda e: e.tensor_scalar(BND, BND, -BIG, None, ALU.mult))
        VC(lambda e: e.tensor_reduce(COLS[:, 2:3], BND, AX_X, ALU.min))
        VC(lambda e: e.tensor_tensor_scan(ROWE, BND, ROWE, -BIG, ALU.add, ALU.max), t_re)
        VC(lambda e: e.tensor_copy(COLS[:, 3:4], ROWE[:, 6527:6528]))

        L1R = ST[0:1, 0:512]

        def row_of(k, col, tok):
            return T(lambda e: e.matmul(PS[4][0:1, 128 * k:128 * k + 128], COLS[:, col:col + 1], IDENT[:, :],
                                        start=True, stop=True), tok)
        for k, col in enumerate((0, 1, 2, 3)):
            m = row_of(k, col, vv())
        VC(lambda e: e.tensor_copy(L1R.rearrange("p (k h g) -> p k g h", h=8, g=TG),
                                   PS[4][0:1, :].rearrange("p (k g h) -> p k g h", g=TG, h=8)), m)
        KF, KL, BR, FR = (L1R[:, 128 * k:128 * k + 128].rearrange("p (h g) -> p h g", g=TG) for k in range(4))
        XR = ST[0:1, 512:640]
        NE = XR.rearrange("p (h g) -> p h g", g=TG)
        CR = RC[0:1, 0:128]
        C3 = CR.rearrange("p (h g) -> p h g", g=TG)
        TR2 = RC[0:1, 128:256]
        T3 = TR2.rearrange("p (h g) -> p h g", g=TG)
        FC = RC[0:1, 256:384]
        FC3 = FC.rearrange("p (h g) -> p h g", g=TG)
        CO = RC[0:1, 384:512]

        VC(lambda e: e.memset(XR, -BIG))
        VC(lambda e: e.tensor_tensor(NE[:, :, 1:TG], KF[:, :, 1:TG], KL[:, :, 0:TG - 1], ALU.not_equal))
        VC(lambda e: e.tensor_scalar(NE[:, :, 1:TG], NE[:, :, 1:TG], -BIG, None, ALU.mult))

        def carry(forward, vals3):
            VC(lambda e: e.memset(TR2, -BIG))
            if forward:
                VC(lambda e: e.tensor_tensor(T3[:, :, 1:TG], NE[:, :, 1:TG], BR[:, :, 1:TG], ALU.add))
                VC(lambda e: e.tensor_tensor_scan(FC, TR2, vals3, -BIG, ALU.add, ALU.max))
                VC(lambda e: e.memset(CR, -BIG))
                VC(lambda e: e.tensor_tensor(C3[:, :, 1:TG], FC3[:, :, 0:TG - 1], NE[:, :, 1:TG], ALU.add))
            else:
                VC(lambda e: e.tensor_tensor(T3[:, :, 0:TG - 1], NE[:, :, 1:TG], BR[:, :, 0:TG - 1], ALU.add))
                VC(lambda e: e.tensor_tensor_scan(FC[:, ::-1], TR2[:, ::-1], vals3[:, ::-1], -BIG, ALU.add, ALU.max))
                VC(lambda e: e.memset(CR, -BIG))
                VC(lambda e: e.tensor_tensor(C3[:, :, 0:TG - 1], FC3[:, :, 1:TG], NE[:, :, 1:TG], ALU.add))
            VC(lambda e: e.tensor_copy(CO.rearrange("p (g h) -> p h g", h=8), C3))
            m_ = T(lambda e: e.matmul(PS[5][:, 0:1], CO, ONES[0:1, 0:1], start=True, stop=True), vv())
            return VC(lambda e: e.tensor_copy(COLS[:, 4:5], PS[5][:, 0:1]), m_)

        carry(True, L1R[:, 384:512])
        VC(lambda e: e.tensor_tensor_scan(ROWE, BND, ROWE, COLS[:, 4:5], ALU.add, ALU.max))
        B2 = BND
        VC(lambda e: e.tensor_tensor_scan(RC[:, 6527:0:-1] if False else RC[:, 512:513], BND[:, 0:1], ROWE[:, 6527:6528],
                                          -BIG, ALU.add, ALU.max))
        def back(init):
            VC(lambda e: e.tensor_tensor(ROWE[:, 6527:6528], ROWE[:, 6527:6528], init, ALU.max)
               if init is not None else e.tensor_copy(COLS[:, 5:6], ROWE[:, 6527:6528]))
            VC(lambda e: e.tensor_copy(COLS[:, 5:6], ROWE[:, 6527:6528]))
            VC(lambda e: e.tensor_tensor_scan(ROWE[:, 0:6527][:, ::-1], BND[:, 1:6528][:, ::-1],
                                              ROWE[:, 0:6527][:, ::-1], COLS[:, 5:6], ALU.add, ALU.max))
        back(None)
        m = T(lambda e: e.matmul(PS[4][0:1, 0:128], ROWE[:, 0:1], IDENT[:, :], start=True, stop=True), vv())
        VC(lambda e: e.tensor_copy(FR, PS[4][0:1, 0:128].rearrange("p (g h) -> p h g", h=8)), m)
        carry(False, L1R[:, 384:512])
        back(COLS[:, 4:5])
        t_rows = vv()
        def fin(g, j0, j1, bank, mtok, _):
            ct = A(lambda e: e.activation(RC[:, j0 * 128:j1 * 128], bank[:, 0:(j1 - j0) * 128], ACT.Copy), mtok, t_rows)
            vt = V(lambda e: e.tensor_tensor(RA[:, j0 * 128:j1 * 128], RA[:, j0 * 128:j1 * 128],
                                             RC[:, j0 * 128:j1 * 128], ALU.subtract), ct, t_re)
            tail.append((j0, j1, vt))
            return ct
        tail = []
        blocks(None, ROWE, t_rows, fin)
        for j0, j1, vt in tail:
            t_m = A(lambda e, j0=j0, j1=j1: e.activation(RA[:, j0 * 128:j1 * 128], RA[:, j0 * 128:j1 * 128], ACT.Exp),
                    vt)
        MM_ = RC[:, :].rearrange("p (j g h) -> p j g h", g=TG, h=8)

        t_xb = P(lambda e: e.tensor_tensor(XS[:, :, :], XS[:, :, :], BIAS1[:, :].unsqueeze(1).to_broadcast([128, NT, 128]),
                                           ALU.add), l_gb, vv())

        AC1 = RB[:, :].rearrange("p (n f) -> p n f", f=145)
        z4 = VC(lambda e: e.memset(RB[:, :], 0.0), t_m)
        mmb, adb, ohx, gx = {}, {}, {}, {}
        prep = {}
        RG = RING[:, :, :]
        grps, g_at = [], {}
        t0 = 0
        while t0 < NTL:
            gi = len(grps)
            t1 = min(t0 + 9 - gi % 2, NTL)
            grps.append((t0, t1, (0, 9, 17, 26)[gi % 4]))
            for t in range(t0, t1):
                g_at[t] = gi
            t0 = t1
        s_rp = [s_m[22], s_m[23], s_in[38], s_in[39]]
        tok_rp = {}
        rp_ready = [sp1, vv()]

        def tile_b(t):
            gi = g_at[t]
            a0, a1, base = grps[gi]
            if t == a0:
                tok_rp[gi] = q.dma("s", s_rp[gi % 4], lambda e: e.dma_start(
                    RG[:, base:base + a1 - a0, 0:136], SPB[:, a0:a1, :]), rp_ready,
                    mmb.get(grps[gi - 4][1] - 1) if gi >= 4 else None)
            rows, tok = RG[:, base + t - a0, :], tok_rp[gi]
            if t == a0:
                b = a1
                for a_, b_ in ((t, b),):
                    tg, j = a_ // TJ, a_ % TJ
                    n = b_ - a_
                    A(lambda e: e.activation(RG[:, base:base + n, 128:136], EE[:, j:j + n, tg, :], ACT.Copy), tok, t_m)
                    prep[gi] = A(lambda e: e.activation(RG[:, base:base + n, 136:144], MM_[:, j:j + n, tg, :], ACT.Copy), t_m)
                    ones_t = P(lambda e: e.memset(RG[:, base:base + n, 144:145], 1.0), tok)
                    prep[gi] = [prep[gi], ones_t]
            hb = V(lambda e: e.tensor_scalar(OHB[:, t % 4, :], IOTAB[:, :], KEY1[:, t:t + 1], None, ALU.is_equal),
                   ohx.get(t - 4))
            ohx[t] = A(lambda e: e.activation(OH[:, t % 4, :], OHB[:, t % 4, :], ACT.Copy), hb, mmb.get(t - 4))
            gx[t] = P(lambda e: e.tensor_tensor(
                rows[:, 0:128].rearrange("p (h c) -> p h c", c=16), rows[:, 0:128].rearrange("p (h c) -> p h c", c=16),
                EE[:, t % TJ, t // TJ, :].unsqueeze(2).to_broadcast([128, 8, 16]), ALU.mult), tok, t_m)
            for h in range(2):
                mmb[t] = T(lambda e, h=h: e.matmul(PS[t % 4][:, h * 145:(h + 1) * 145], OH[:, t % 4, h * 128:(h + 1) * 128],
                                                   rows, start=True, stop=True), gx[t], ohx[t], prep[gi], adb.get(t - 4))

        def add_b(t):
            for h in range(2):
                def go(e, h=h):
                    if h == 0:
                        wb["v"] = window(e, "v", WTAB1, t)
                    sl = RB[:, bass.ds(wb["v"] * 290 + 145 * h, 145)]
                    return e.tensor_tensor(sl, sl, PS[t % 4][:, 145 * h:145 * h + 145], ALU.add)
                adh[t, h] = V(go, mmb[t], adh.get((t - 1, h)), z4)
            adb[t] = adh[t, 1]

        wb, adh = {}, {}
        for t in range(NTL + 3):
            if t < NTL:
                tile_b(t)
            if t >= 3:
                add_b(t - 3)

        SN = [SC1[:, 0:392], SC1[:, 400:792], SC2[:, 0:392], SC2[:, 400:792], RC[:, 1024:1416], WE0[:, 0:392], WE0[:, 400:792]]
        n8 = [s.rearrange("p (t h) -> p t h", h=8) for s in SN]
        CT = WE0[:, 800:849]
        HA = WE0[:, 849:896]
        SUMS, DEN, SM, DEG = AC1[:, 0:NT, 0:128], AC1[:, 0:NT, 128:136], AC1[:, 0:NT, 136:144], AC1[:, 0:NT, 144]
        VC(lambda e: e.tensor_scalar(CT, DEG, 1.0, None, ALU.max), q.now("a"))
        VC(lambda e: e.reciprocal(RDEG[:, :], CT))
        VC(lambda e: e.tensor_scalar(CT, DEG, 1.0, None, ALU.min))
        VC(lambda e: e.tensor_scalar(CT, CT, -1.0, BIG, ALU.add, ALU.mult))

        def b8(v):
            return v.unsqueeze(2).to_broadcast([128, NT, 8])
        VC(lambda e: e.tensor_tensor(n8[0], SM, b8(RDEG[:, :]), ALU.mult))
        VC(lambda e: e.tensor_tensor(n8[0], n8[0], b8(CT), ALU.add))
        VC(lambda e: e.tensor_tensor(n8[1], HN[:, :, 128:136], HN[:, :, 136:144], ALU.add))
        VC(lambda e: e.scalar_tensor_tensor(out=SN[1], in0=SN[1], scalar=0.2, in1=SN[1], op0=ALU.mult, op1=ALU.max))
        VC(lambda e: e.tensor_tensor(SN[2], SN[0], SN[1], ALU.max))
        VC(lambda e: e.tensor_tensor(SN[0], SN[0], SN[2], ALU.subtract))
        VC(lambda e: e.tensor_tensor(SN[1], SN[1], SN[2], ALU.subtract))
        A(lambda e: e.activation(SN[3], SN[0], ACT.Exp), vv())
        t_ = A(lambda e: e.activation(SN[4], SN[1], ACT.Exp))
        VC(lambda e: e.tensor_tensor(n8[5], DEN, n8[3], ALU.mult), t_)
        VC(lambda e: e.tensor_tensor(SN[5], SN[5], SN[4], ALU.add))
        VC(lambda e: e.reciprocal(SN[6], SN[5]))
        VC(lambda e: e.tensor_tensor(SN[3], SN[3], SN[6], ALU.mult))
        VC(lambda e: e.tensor_tensor(SN[4], SN[4], SN[6], ALU.mult))

        def h16(v):
            return v.unsqueeze(2).to_broadcast([128, NT * 8, 16])

        S4 = SUMS.rearrange("p t (h c) -> p t h c", c=16)
        H4 = HN[:, :, 0:128].rearrange("p t (h c) -> p t h c", c=16)
        t_n = vv()

        def pre2(k0, k1):
            for t in range(k0, k1):
                hp = P(lambda e, t=t: e.tensor_tensor(
                    H4[:, t], H4[:, t], n8[4][:, t, :].unsqueeze(2).to_broadcast([128, 8, 16]), ALU.mult), t_n, d_g)
                V(lambda e, t=t: e.tensor_tensor(
                    S4[:, t], S4[:, t], n8[3][:, t, :].unsqueeze(2).to_broadcast([128, 8, 16]), ALU.mult), t_n)
            VC(lambda e: e.tensor_tensor(XS[:, k0:k1, :], XS[:, k0:k1, :], SUMS[:, k0:k1, :], ALU.add), t_xb)
            VC(lambda e: e.tensor_tensor(XS[:, k0:k1, :], XS[:, k0:k1, :], HN[:, k0:k1, 0:128], ALU.add), hp)

        WTR = [RC[:, k * 128:(k + 1) * 128] for k in range(6)]
        for k, iw in enumerate((iSS, iNE, iED, iDA, iCO, iSE)):
            m = T(lambda e, k=k, iw=iw: e.transpose(PS[4 + k // 4][:, (k % 4) * 128:(k % 4 + 1) * 128], WT[:, iw, :],
                                                    IDENT[:, :]), l_w[iw], t_n)
        V(lambda e: e.tensor_copy(RC[:, 0:512], PS[4][:, :]), m)
        t_wtr = V(lambda e: e.tensor_copy(RC[:, 512:768], PS[5][:, 0:256]))
        HT = RA[:, 0:NP]
        tr, ht = transposer(HT, t_wtr)
        tab_tok = []

        def post2(k0, k1, toks):
            tr(k0, k1, toks)
            tab_tok.append(relu_rows(TAB2, s_m[13], k0, k1))
        norm_pipe(pre2, post2)
        ht = list(ht.values())
        d_t2 = tab_tok[-1]
        AG = RB[:, 0:NW * WN]
        z5 = V(lambda e: e.memset(AG, 0.0), vv())
        ATC = HN[:, :, :].rearrange("p a b -> p (a b)")[:, 0:NW * WN]
        NM = ATC[:, 0:NP].rearrange("p (t d) -> p t d", d=128)
        l_at = q.dma("s", s_m[14], lambda e: e.dma_start(ATC, ATTD), d_att, d_t2)
        cst("t", c_ones, l_b1)
        RDG = RDEG
        evn = {}

        def own_term(t):
            if t % 16 != 8 or t // 16 >= NT:
                return None
            k = t // 16
            sl = slice(k * 128, (k + 1) * 128)
            m0 = T(lambda e: e.matmul(PS[4][:, 0:128], ATC[:, sl], WTR[2], start=True, stop=True), l_at, evn.get(k - 1))
            T(lambda e: e.matmul(PS[5][:, 0:128], RA[:, sl], WTR[0], start=True, stop=False))
            m1_ = T(lambda e: e.matmul(PS[5][:, 0:128], ONES[0:1, :], ROWS[0:1, 0:128], start=False, stop=True))
            V(lambda e: e.tensor_scalar(NM[:, k, :], PS[4][:, 0:128], RDG[:, k:k + 1], None, ALU.mult), m0, m1_)
            evn[k] = VC(lambda e: e.tensor_tensor(NM[:, k, :], NM[:, k, :], PS[5][:, 0:128], ALU.add))
            return None
        t_ag = run_gather(AG, WTAB1, TAB2, IDX1, KEY1, None, [d_t2, z5, t_wtr, ht], extra=own_term)

        evo = {}

        mt3 = {}

        def pre3_t(k0, k1):
            for k in range(k0, k1):
                g = k // 4
                mt3[k] = T(lambda e, k=k, g=g: e.matmul(PS[4 + g % 2][:, (k % 4) * 128:(k % 4 + 1) * 128],
                                                        AG[:, k * 128:(k + 1) * 128], WTR[1], start=True, stop=True),
                           t_ag, evn[NT - 1], evo.get(4 * (g - 2) + 3))

        def pre3(k0, k1):
            for k in range(k0, k1):
                g = k // 4
                tmp_ = OH[:, k % 4, 0:128]
                tm_[k] = V(lambda e, k=k, g=g, tmp_=tmp_: e.scalar_tensor_tensor(
                    out=tmp_, in0=PS[4 + g % 2][:, (k % 4) * 128:(k % 4 + 1) * 128], scalar=RDG[:, k:k + 1],
                    in1=NM[:, k, :], op0=ALU.mult, op1=ALU.add), mt3[min(4 * g + 3, k1 - 1)], evo.get(k - 4))
                if k > k0:
                    relu3(k - 1)
            relu3(k1 - 1)

        def relu3(k):
            tmp_ = OH[:, k % 4, 0:128]
            evo[k] = V(lambda e: e.scalar_tensor_tensor(
                out=XS[:, k, :], in0=tmp_, scalar=0.0, in1=XS[:, k, :], op0=ALU.max, op1=ALU.add), tm_[k])
        tm_ = {}

        tr, ht = transposer(HT)
        cst("t", l_b2, l_b3, l_b4)
        ev = {}
        T3v = TAB3.rearrange("(t p k) d -> p t (k d)", p=128, k=2)
        stage = [RC[:, 768 + 2048 * k:768 + 2048 * (k + 1)].rearrange("p (a b) -> p a b", b=256) for k in range(2)]
        dg = {}

        def post3(k0, k1, toks):
            tr(k0, k1, toks)
            g = k0 // 8
            for k in range(k0, k1):
                bank = PS[k % 4]
                T(lambda e, k=k, bank=bank: e.matmul(bank[:, 0:256], RA[:, k * 128:(k + 1) * 128], RC[:, 3 * 128:5 * 128],
                                                     start=True, stop=False), ht[k], ev.get(k - 4))
                m_ = T(lambda e, bank=bank: e.matmul(bank[:, 0:256], ONES[0:1, :], ROWS[0:1, 128:384],
                                                     start=False, stop=True))
                ev[k] = A(lambda e, k=k, bank=bank: e.activation(stage[g % 2][:, k - k0, :], bank[:, 0:256], ACT.Copy),
                          m_, dg.get(g - 2))
            dg[g] = q.dma("s", s_m[16 + g % 2], lambda e: e.dma_start(T3v[:, k0:k1, :], stage[g % 2][:, 0:k1 - k0, :]),
                          ev[k1 - 1])
        norm_pipe(pre3, post3, pre_t=pre3_t)
        t_x3 = evo[NT - 1]
        l_bs = q.dma("s", s_in[37], lambda e: e.dma_start(COLS[:, 15:16], b_self.rearrange("(p k) -> p k", k=1)), t_x3)
        z7 = V(lambda e: e.memset(RB[:, NP:NW * WN], 0.0), vv())
        ev2 = {}
        for g in range(13):
            c0_, c1_ = 512 * g, min(512 * g + 512, NP)
            bank = PS[4 + g % 4]
            m = T(lambda e, c0_=c0_, c1_=c1_, bank=bank: e.matmul(
                bank[:, 0:c1_ - c0_], WTR[5], RA[:, c0_:c1_], start=True, stop=True), ev2.get(g - 4), t_x3,
                ht[NT - 1], [ev[k] for k in range(NT - 8, NT)])
            ev2[g] = A(lambda e, c0_=c0_, c1_=c1_, bank=bank: e.activation(
                AG[:, c0_:c1_], bank[:, 0:c1_ - c0_], ACT.Identity, bias=COLS[:, 15:16]), m, l_bs)
        l_i3 = q.dma("s", s_in[34], lambda e: e.dma_start(IDX0[:, :], I3D), d_i3, t_x3)
        q.wait("v", z7, ev2[12])
        t_ag = run_gather(AG, WTAB1, TAB3, IDX0, KEY1, None, [dg[5], dg[6], l_i3])
        evo = {}
        outs = []
        for t in range(NT):
            def node4(t=t):
                bank = PS[t % 4]
                sl = slice(t * 128, (t + 1) * 128)
                m_ = T(lambda e: e.transpose(bank[:, 0:128], AG[:, sl], IDENT[:, :]), t_ag, evo.get(t - 4))
                evo[t] = V(lambda e: e.scalar_tensor_tensor(out=XS[:, t, :], in0=bank[:, 0:128], scalar=0.0,
                                                            in1=XS[:, t, :], op0=ALU.max, op1=ALU.add), m_)
            node4()
            if t % 8 == 7:
                a = t - 7
                outs.append(q.dma("s", s_fin, lambda e, a=a: e.dma_start(
                    out[a * 128:(a + 8) * 128, :].rearrange("(t p) d -> p t d", p=128), XS[:, a:a + 8, :]), evo[t]))
        outs.append(q.dma("s", s_fin, lambda e: e.dma_start(out[48 * 128:N, :], XS[0:N - 48 * 128, NT - 1, :]), evo[NT - 1]))
        q.wait("s", outs[-1])

        block = ctx.enter_context(nc.Block())

        @block.sync
        def _(e):
            for it in q.items["s"]:
                it(e)

        @block.gpsimd
        def _(e):
            for it in q.items["p"]:
                it(e)

        @block.scalar
        def _(e):
            for it in q.items["a"]:
                it(e)

        @block.tensor
        def _(e):
            for it in q.items["t"]:
                it(e)

        @block.vector
        def _(e):
            for it in q.items["v"]:
                it(e)


_INS = ['x', 'src', 'dst', 'edge_attr_128', 'edge_type_2', 'edge_type_200', 'L0_gnn_W1', 'L0_gnn_W2', 'L0_gnn_W3',
        'L0_gnn_re_attention_weight', 'L0_gnn_u', 'L0_gnn_en_weight', 'L0_gnn_re_weight',
        'L0_gnn_re_specific_attention', 'L1_gnn_W', 'L1_gnn_att_src', 'L1_gnn_att_dst', 'L1_gnn_bias',
        'L2_gnn_w_self_W', 'L2_gnn_w_self_b', 'L2_gnn_w_nei_W', 'L2_gnn_w_edge_W', 'L3_gnn_W_data', 'L3_gnn_b_data',
        'L3_gnn_W_control', 'L3_gnn_b_control', 'L3_gnn_W_self', 'L3_gnn_b_self']
_OUTS = [((6250, 128), 'float32')]


def kernel(**inputs):
    import numpy as _np
    import concourse.bacc as _bacc
    from concourse import mybir as _mybir
    from concourse.bass_utils import run_bass_kernel_spmd as _run

    nc = _bacc.Bacc("TRN2", target_bir_lowering=False, num_devices=1)
    arrays, args = {}, []
    for name in _INS:
        a = _np.ascontiguousarray(inputs[name])
        arrays[f"in_{name}_dram"] = a
        args.append(nc.dram_tensor(f"in_{name}_dram", a.shape, _mybir.dt.from_np(a.dtype), kind="ExternalInput").ap())
    for i, (shape, dtype) in enumerate(_OUTS):
        dt = _mybir.dt.from_np(_np.dtype(dtype))
        args.append(nc.dram_tensor(f"out_{i}_dram", shape, dt, kind="ExternalOutput").ap())
    program(nc, *args)
    r = _run(nc, [arrays], core_ids=[0])
    return r.results[0]["out_0_dram"]
```

```python
from contextlib import ExitStack

import concourse.bass as bass
from concourse import mybir

ALU = mybir.AluOpType
ACT = mybir.ActivationFunctionType
F32 = mybir.dt.float32
BF16 = mybir.dt.bfloat16
I32 = mybir.dt.int32
I16 = mybir.dt.int16
AX_X = mybir.AxisListType.X
RMAX = bass.bass_isa.ReduceOp.max
RADD = bass.bass_isa.ReduceOp.add

N = 6250
D = 128
E = 100000
NREL = 200
EP, EC = 125, 800
NT = 49
NP = NT * 128
NW = 25
WN = 256
NT0 = E // 128 + NW
NTL = (E + NW * 142) // 128
NTB = 7
BIG = 1.0e30
PAD = 256 << 21
LAST = E - 128
SC_FIRST = 96


class Queues:

    def __init__(self, sems):
        self.names = ("v", "a", "t", "p", "s")
        self.items = {n: [] for n in self.names}
        self.sem = dict(sems)
        self.count = {n: 0 for n in self.names}
        self.seen = {n: {} for n in self.names}
        self.dcount = {}
        self.waits = set()

    def add(self, name, sem):
        self.items[name], self.sem[name], self.count[name], self.seen[name] = [], sem, 0, {}

    def merge(self, eng, other, mark):
        def units(items):
            out, cur = [], []
            for it in items:
                cur.append(it)
                if id(it) not in self.waits:
                    out.append(cur)
                    cur = []
            return out, cur
        mine, rest = units(self.items[eng][mark:])
        theirs, rest2 = units(self.items[other])
        del self.items[eng][mark:]
        self.items[other] = []
        n, k = max(len(mine), 1), 0
        for i in range(n):
            if i < len(mine):
                self.items[eng].extend(mine[i])
            upto = len(theirs) * (i + 1) // n
            for u in theirs[k:upto]:
                self.items[eng].extend(u)
            k = upto
        self.items[eng].extend(rest + rest2)

    def wait(self, eng, *tokens):
        for tok in tokens:
            if tok is None:
                continue
            if isinstance(tok, list):
                self.wait(eng, *tok)
                continue
            sem, value = tok
            key = id(sem)
            if self.seen[eng].get(key, 0) >= value:
                continue
            self.seen[eng][key] = value
            self.items[eng].append(lambda e, s=sem, v=value: e.wait_ge(s, v))
            self.waits.add(id(self.items[eng][-1]))

    def op(self, eng, fn, *tokens):
        self.wait(eng, *tokens)
        self.count[eng] += 1
        sem = self.sem[eng]
        self.items[eng].append(lambda e: fn(e).then_inc(sem, 1))
        return (sem, self.count[eng])

    def quiet(self, eng, fn, *tokens):
        self.wait(eng, *tokens)
        self.items[eng].append(fn)

    def dma(self, eng, sem, fn, *tokens):
        self.wait(eng, *tokens)
        self.dcount[id(sem)] = self.dcount.get(id(sem), 0) + 16
        self.items[eng].append(lambda e: fn(e).then_inc(sem, 16))
        return (sem, self.dcount[id(sem)])

    def now(self, eng):
        return (self.sem[eng], self.count[eng])


def program(nc, x, src, dst, edge_attr_128, edge_type_2, edge_type_200,
            W1, W2, W3, relw, u, en_w, re_w, re_att,
            gW, att_src, att_dst, gbias,
            w_self_W, w_self_b, w_nei_W, w_edge_W,
            W_data, b_data, W_control, b_control, W_self, b_self, out):
    ctx = ExitStack()
    with ctx:
        def sb(name, shape, dt=F32):
            return ctx.enter_context(nc.sbuf_tensor(name, shape, dt))

        def sem(name):
            return ctx.enter_context(nc.semaphore(name))

        def dram(name, shape, dt=F32):
            return nc.dram_tensor(name, shape, dt).ap()

        XS = sb("XS", [128, NT, D])
        HN = sb("HN", [128, NT, 144])
        RA = sb("RA", [128, 6528])
        RB = sb("RB", [128, NW * 292])
        RC = sb("RC", [128, 6528])
        RING = sb("RING", [128, 34, 145])
        GR = RING[:, :, :].rearrange("p a b -> p (a b)")
        IDX0 = sb("IDX0", [128, NTB * 128], I32)
        KEY0 = sb("KEY0", [128, NTB * 128])
        WE0 = sb("WE0", [128, NTB * 128])
        SC1 = sb("SC1", [128, NTB * 128])
        SC2 = sb("SC2", [128, NTB * 128])
        IDX1 = sb("IDX1", [128, NTB * 128], I32)
        KEY1 = sb("KEY1", [128, NTB * 128])
        OH = sb("OH", [128, 4, WN])
        OHB = sb("OHB", [128, 4, WN], BF16)
        OHT = sb("OHT", [128, 4, WN], BF16)
        WTAB0 = sb("WTAB0", [1, NTB * 128], I16)
        WTAB1 = sb("WTAB1", [1, NTB * 128], I16)
        IOTA = sb("IOTA", [128, WN])
        IOTAB = sb("IOTAB", [128, WN], BF16)
        IOI = sb("IOI", [128, WN], I32)
        IDENT = sb("IDENT", [128, 128])
        IDENTB = sb("IDENTB", [128, 128], BF16)
        TRI = sb("TRI", [128, 128])
        ONES = sb("ONES", [128, 128])
        BD = sb("BD", [128, 8])
        WT = sb("WT", [128, 12, 128])
        RHS1 = sb("RHS1", [128, 144])
        ADC = sb("ADC", [128, 16])
        COLS = sb("COLS", [128, 16])
        RELB = sb("RELB", [128, NREL])
        BIAS1 = sb("BIAS1", [128, D])
        ROWS = sb("ROWS", [1, 512])
        AD3 = sb("AD3", [128, 50, 24], BF16)
        ST = sb("ST", [128, 640])
        SI = sb("SI", [128, 64], I32)
        RDEG = sb("RDEG", [128, NT])
        CUM0 = sb("CUM0", [128, NW])

        PS = [ctx.enter_context(nc.psum_tensor(f"PS{i}", [128, 512], F32)) for i in range(8)]

        TAB = [dram(f"TAB{i}", (NP, D)) for i in range(3)]
        TABQ = dram("TABQ", (NP, 132))
        TABG = dram("TABG", (NP, 136))
        TAB2 = dram("TABN", (NP, D))
        TAB3 = dram("TABM", (2 * NP, D))
        REC0 = dram("REC0", (NTB * 128 * 128, 1), I32)
        REC1 = dram("REC1", (E + 128, 1), I32)
        RECX = dram("RECX", (E // 16 + 1, 128), I32)
        RECA = dram("RECA", (E, 2), I32)
        RECB = dram("RECB", (E, 2), I32)
        EA = dram("EA", (E, D))
        TW0 = dram("TW0", (NTB, 128), I16)
        TW1 = dram("TW1", (NTB, 128), I16)
        TBT = dram("TBT", (NTB, 128), I32)
        KFD = dram("KFD", (128, NTB * 128))
        I3D = dram("I3D", (128, NTB * 128), I32)
        ATTD = dram("ATTD", (128, NW * WN))

        q = Queues({n: sem(f"e_{n}") for n in ("v", "a", "t", "p", "s")})
        s_in = [sem(f"in{i}") for i in range(40)]
        s_g = [sem(f"g{i}") for i in range(34)]
        s_h = [sem(f"h{i}") for i in range(16)]
        s_m = [sem(f"m{i}") for i in range(24)]
        s_fin = sem("fin")
        s_join = sem("join")

        def V(fn, *w):
            return q.op("v", fn, *w)

        def A(fn, *w):
            return q.op("a", fn, *w)

        def T(fn, *w):
            return q.op("t", fn, *w)

        def P(fn, *w):
            return q.op("p", fn, *w)

        def vv():
            return q.now("v")

        def VC(fn, *w):
            return q.op("v", fn, q.now("v"), *w)

        def load(i, dst_ap, src_ap, *w, eng="s"):
            return q.dma(eng, s_in[i], lambda e: e.dma_start(dst_ap, src_ap), *w)

        def affine(t_, op, fill, pattern, cm, base, *w):
            return P(lambda e: e.affine_select(out=t_, in_=t_, compare_op=op, fill=fill, base=base,
                                               pattern=pattern, channel_multiplier=cm), *w)

        c0 = P(lambda e: e.memset(IDENT[:, :], 0.0))
        c1 = P(lambda e: e.memset(TRI[:, :], 0.0))
        c_ones = P(lambda e: e.memset(ONES[:, :], 1.0))
        c2 = P(lambda e: e.memset(BD[:, :], 1.0))
        c_id = affine(IDENT[:, :], ALU.not_equal, 1.0, [[-1, 128]], 1, 0, c2)
        c_tri = affine(TRI[:, :], ALU.is_ge, 1.0, [[-1, 128]], 1, 0, c2)
        c3 = affine(BD[:, :], ALU.is_ge, 0.0, [[-16, 8]], 1, 0, c2)
        c_bd = affine(BD[:, :], ALU.is_ge, 0.0, [[16, 8]], -1, 15, c3)
        c4 = P(lambda e: e.iota(IOI[:, :], pattern=[[1, WN]], base=0, channel_multiplier=0))
        c_tt = P(lambda e: e.iota(SI[:, 0:NTB], pattern=[[128, NTB]], base=0, channel_multiplier=1))
        c5 = P(lambda e: e.tensor_copy(IOTA[:, :], IOI[:, :]), c4)
        c_io = P(lambda e: e.tensor_copy(IOTAB[:, :], IOI[:, :]), c4)
        c_idb = P(lambda e: e.tensor_copy(IDENTB[:, :], IDENT[:, :]), c_id)

        def edges(ap):
            return ap.rearrange("(p c) -> p c", c=EC)

        def slot(k, dt=I32):
            v = RA[0:EP, k * EC:(k + 1) * EC]
            return v if dt is F32 else v.bitcast(dt)

        def slotb(k, dt=I32):
            v = RC[0:EP, k * EC:(k + 1) * EC]
            return v if dt is F32 else v.bitcast(dt)

        l_src = load(0, slot(0), edges(src))
        l_dst = load(1, slot(1), edges(dst))
        l_nx = load(2, slotb(0)[0:124, :], dst[1:1 + 124 * EC].rearrange("(p c) -> p c", c=EC), eng="a")
        l_nx1 = load(3, slotb(0)[124:125, 0:EC - 1], dst[1 + 124 * EC:E].rearrange("(p c) -> p c", p=1), eng="a")
        l_nx2 = load(4, slotb(0)[124:125, EC - 1:EC], dst[E - 1:E].rearrange("(p c) -> p c", p=1), eng="a")
        l_t200 = load(5, slot(2), edges(edge_type_200))
        l_t2 = load(6, slot(3), edges(edge_type_2))
        m_x = P(lambda e: e.memset(XS[:, NT - 1, :], 0.0))
        l_x = load(7, XS[:, 0:NT - 1, :], x[0:48 * 128, :].rearrange("(t p) d -> p t d", p=128))
        l_x2 = load(8, XS[0:N - 48 * 128, NT - 1, :], x[48 * 128:N, :], m_x)

        names = [W1, W2, W3, en_w, re_w, gW, w_self_W, w_nei_W, w_edge_W, W_data, W_control, W_self]
        l_w = [load(9 + i, WT[:, i, :], a, eng="a") for i, a in enumerate(names)]
        (iW1, iW2, iW3, iEN, iRE, iGW, iSS, iNE, iED, iDA, iCO, iSE) = range(12)
        l_u = [load(i, COLS[:, k:k + 1], u[k * 128:(k + 1) * 128].rearrange("(p k) -> p k", k=1), eng="a")
               for k, i in enumerate((21, 35, 36))]
        l_ra = load(22, COLS[:, 3:4], re_att.rearrange("(p k) -> p k", k=1), eng="a")
        l_as = load(23, COLS[:, 4:5], att_src.rearrange("h (c k) -> (h c) k", k=1), eng="a")
        l_ad = load(24, COLS[:, 5:6], att_dst.rearrange("h (c k) -> (h c) k", k=1), eng="a")
        l_rel = load(25, RELB[:, :], relw.rearrange("(a n) -> a n", a=1).to_broadcast([128, NREL]), eng="a")
        l_gb = load(26, BIAS1[:, :], gbias.rearrange("(a n) -> a n", a=1).to_broadcast([128, D]), eng="a")
        l_b1 = load(27, ROWS[:, 0:128], w_self_b.rearrange("(a n) -> a n", a=1), eng="a")
        l_b2 = load(28, ROWS[:, 128:256], b_data.rearrange("(a n) -> a n", a=1), eng="a")
        l_b3 = load(29, ROWS[:, 256:384], b_control.rearrange("(a n) -> a n", a=1), eng="a")
        l_b4 = load(30, ROWS[:, 384:512], b_self.rearrange("(a n) -> a n", a=1), eng="a")

        m_pad = P(lambda e: e.memset(SC2[:, :].bitcast(I32), PAD))
        pads = []
        for b in range(NTB):
            def put(b=b):
                return q.dma("s", s_m[0], lambda e: e.dma_start(
                    REC0[b * 16384:(b + 1) * 16384, :].rearrange("(p l) o -> p (l o)", l=128),
                    SC2[:, 0:128].bitcast(I32)), m_pad)
            pads.append(put())
        d_pad = pads[-1]
        m_pad1 = P(lambda e: e.memset(SC2[0:1, 128:256].bitcast(I32), 8191 << 14), m_pad)
        d_pad1 = q.dma("s", s_m[1], lambda e: e.dma_start(
            REC1[E:E + 128, :].rearrange("(a l) o -> a (l o)", a=1), SC2[0:1, 128:256].bitcast(I32)), m_pad1)

        def cst(eng, *toks):
            q.wait(eng, *toks)

        def place(key, nb, padded, msk, scn, pos, posi, w0, work):
            cnt, offs, tmp, tot = (work[:, 32 * k:32 * k + nb] for k in range(4))
            cum = work[:, 128:128 + nb]
            cols = []
            V(lambda e: e.memset(work[:, :], 0.0))
            for b in range(nb):
                def count(b=b):
                    return V(lambda e: e.tensor_scalar(msk[b % 2], key, float(b), None, ALU.is_equal, ALU.add,
                                                       accum_out=cnt[0:EP, b:b + 1]),
                             w0, q.now("v"))
                last = count()
            m1 = T(lambda e: e.matmul(PS[0][:, 0:nb], TRI[0:EP, :], cnt[0:EP, :], start=True, stop=True),
                   last, c_tri, c_idb)
            m2 = T(lambda e: e.matmul(PS[1][:, 0:nb], ONES[0:EP, :], cnt[0:EP, :], start=True, stop=True))
            V(lambda e: e.tensor_copy(tot, PS[1][:, 0:nb]), m2)
            VC(lambda e: e.tensor_copy(tmp, tot))
            if padded:
                ti = SI[:, 8:8 + nb]
                VC(lambda e: e.tensor_scalar(ti, tot, 127.0, None, ALU.add))
                VC(lambda e: e.tensor_scalar(ti, ti, 7, None, ALU.arith_shift_right))
                VC(lambda e: e.tensor_copy(tmp, ti))
            VC(lambda e: e.tensor_tensor_scan(cum, ONES[:, 0:nb], tmp, 0.0, ALU.mult, ALU.add))
            mul = 128.0 if padded else 1.0
            VC(lambda e: e.tensor_tensor(tmp, cum, tmp, ALU.subtract))
            VC(lambda e: e.tensor_scalar(tmp, tmp, mul, -1.0, ALU.mult, ALU.add))
            VC(lambda e: e.tensor_tensor(offs, tmp, PS[0][:, 0:nb], ALU.add), m1)
            for b in range(nb):
                def one(b=b):
                    k = b % 2
                    V(lambda e: e.tensor_scalar(msk[k].bitcast(I32), key, float(b), None, ALU.is_equal), q.now("v"))
                    VC(lambda e: e.tensor_tensor_scan(scn, work2[0:EP, :], msk[k].bitcast(I32),
                                                      offs[0:EP, b:b + 1], ALU.mult, ALU.add))
                    return VC(lambda e: e.copy_predicated(pos, msk[k].bitcast(I32), scn))
                one()
            return VC(lambda e: e.tensor_copy(posi, pos)), cum, tot

        work2 = RING[:, 0:6, :].rearrange("p a b -> p (a b)")[:, 0:EC]
        ringf = RING[:, 6:34, :].rearrange("p a b -> p (a b)")

        def rs(k):
            return ringf[0:EP, k * EC:(k + 1) * EC]

        V(lambda e: e.memset(work2, 1.0))
        wk, ws_, pos0 = rs(0), rs(1), rs(2)
        msk = [slotb(1, F32), slotb(2, F32)]
        wi = slotb(3)
        t_win = VC(lambda e: e.tensor_scalar(wi, slot(0), 8, None, ALU.arith_shift_right), l_src)
        t_key = VC(lambda e: e.tensor_copy(wk, wi))
        work0 = ST[:, 0:160]
        VC(lambda e: e.memset(pos0, 0.0))
        posi0 = slotb(4)
        t_pos0, cum0, tot0 = place(wk, NW, True, msk, ws_, pos0, posi0, [c_ones, t_key], work0)
        v0 = slotb(5)
        VC(lambda e: e.tensor_scalar(v0, slot(0), 255, 21, ALU.bitwise_and, ALU.logical_shift_left))
        VC(lambda e: e.tensor_scalar(wi, slot(1), 8, None, ALU.logical_shift_left), l_dst)
        VC(lambda e: e.tensor_tensor(v0, v0, wi, ALU.bitwise_or))
        t_v0 = VC(lambda e: e.tensor_tensor(v0, v0, slot(2), ALU.bitwise_or), l_t200)
        v1 = slot(4)
        VC(lambda e: e.tensor_scalar(wi, slot(3), 0.0, None, ALU.not_equal), l_t2)
        VC(lambda e: e.tensor_scalar(v1, slot(1), 14, None, ALU.logical_shift_left))
        VC(lambda e: e.tensor_tensor(v1, v1, wi, ALU.bitwise_or))
        VC(lambda e: e.tensor_scalar(wi, slot(0), 1, None, ALU.logical_shift_left))
        t_v1 = VC(lambda e: e.tensor_tensor(v1, v1, wi, ALU.bitwise_or))
        d_v1 = q.dma("s", s_m[2], lambda e: e.dma_start(
            REC1[0:E, :].rearrange("(p c) o -> p (c o)", c=EC), v1), t_v1)
        fl = SI[0:EP, 40:41]
        FLG = SI[:, 41:42]
        VC(lambda e: e.tensor_tensor(wi, slotb(0), slot(1), ALU.is_lt), l_nx, l_nx1, l_nx2)
        VC(lambda e: e.memset(ST[:, 620:621], 0.0))
        t_fl = VC(lambda e: e.tensor_reduce(ST[0:EP, 620:621], wi, AX_X, ALU.max))
        t_fa = P(lambda e: e.partition_all_reduce(ST[:, 621:622], ST[:, 620:621], 128, RMAX), t_fl)
        t_flag = VC(lambda e: e.tensor_copy(FLG, ST[:, 621:622]), t_fa)

        flag_regs = {}

        def general():
            outer_sem, outer_cnt = q.sem, q.count
            outer_seen = q.seen
            q.sem = {n: g_sem[n] for n in q.names}
            q.count = {n: 0 for n in q.names}
            q.seen = {n: {} for n in q.names}
            saved = q.items
            q.items = {n: [] for n in q.names}
            bufs = [RECA, RECB]
            eid = rs(4).bitcast(I32)
            vp = RB[0:EP, 0:2 * EC].bitcast(I32).rearrange("p (c k) -> p c k", k=2)
            kf, sc, ps_ = rs(0), rs(1), rs(2)
            ki = rs(3).bitcast(I32)
            mk = [RB[0:EP, 2 * EC:3 * EC], RB[0:EP, 3 * EC:4 * EC]]
            pi = RB[0:EP, 4 * EC:5 * EC].bitcast(I32)
            wrk = ST[:, 160:320]
            P(lambda e: e.iota(eid, pattern=[[1, EC]], base=0, channel_multiplier=EC), t_pos0)
            V(lambda e: e.tensor_copy(vp[:, :, 0], v1), q.now("p"))
            ld = VC(lambda e: e.tensor_copy(vp[:, :, 1], eid))
            done = None
            for r, (sh, nb) in enumerate(((14, 16), (18, 16), (22, NW))):
                if r:
                    ld = q.dma("s", g_m[0], lambda e, r=r: e.dma_start(
                        vp, bufs[(r - 1) % 2].rearrange("(p c) k -> p c k", c=EC)), done)
                VC(lambda e, sh=sh: e.tensor_scalar(ki, vp[:, :, 0], sh, None, ALU.arith_shift_right), ld)
                if nb == 16:
                    VC(lambda e: e.tensor_scalar(ki, ki, 15, None, ALU.bitwise_and))
                tk = VC(lambda e: e.tensor_copy(kf, ki))
                VC(lambda e: e.memset(ps_, 0.0))
                tp, _, _ = place(kf, nb, False, mk, sc, ps_, pi, [tk, ld], wrk)
                for c in range(EC):
                    done = q.dma("p", g_m[1], lambda e, c=c, r=r: e.indirect_dma_start(
                        bufs[r % 2], bass.IndirectOffsetOnAxis(ap=pi[:, c:c + 1], axis=0), vp[:, c, :], None), tp, ld)
            ld = q.dma("s", g_m[0], lambda e: e.dma_start(vp, bufs[0].rearrange("(p c) k -> p c k", c=EC)), done)
            VC(lambda e: e.tensor_copy(ki, vp[:, :, 0]), ld)
            t1 = VC(lambda e: e.tensor_copy(pi, vp[:, :, 1]))
            w1 = q.dma("s", g_m[2], lambda e: e.dma_start(
                REC1[0:E, :].rearrange("(p c) o -> p (c o)", c=EC), ki), t1, d_v1)
            G = RB[0:EP, 5 * EC:5 * EC + 16 * 128].rearrange("p (a d) -> p a d", d=128)
            EAV = EA.rearrange("(p c) d -> p c d", c=EC)
            prev = [None] * 2
            for b in range(EC // 8):
                h = b % 2
                for k in range(8):
                    c = b * 8 + k
                    ga = q.dma("p", g_g[h], lambda e, c=c, k=k, h=h: e.indirect_dma_start(
                        G[:, h * 8 + k, :], None, edge_attr_128,
                        bass.IndirectOffsetOnAxis(ap=pi[:, c:c + 1], axis=0)), prev[h], t1)
                prev[h] = q.dma("s", g_w[h], lambda e, b=b, h=h: e.dma_start(
                    EAV[:, b * 8:b * 8 + 8, :], G[:, h * 8:h * 8 + 8, :]), ga)
            q.wait("s", prev[0], prev[1], w1)
            ends = {n: q.now(n) for n in q.names if q.count[n]}
            for n in q.names:
                for m, tok in ends.items():
                    q.wait(n, tok)
            branch = q.items
            q.items, q.sem, q.count, q.seen = saved, outer_sem, outer_cnt, outer_seen
            return branch

        g_sem = {n: sem(f"ge_{n}") for n in ("v", "a", "t", "p", "s")}
        g_m = [sem(f"gm{i}") for i in range(3)]
        g_g = [sem(f"gg{i}") for i in range(2)]
        g_w = [sem(f"gw{i}") for i in range(2)]
        branch = general()
        for n in ("v", "t", "p", "s"):
            q.wait(n, t_flag, t_pos0, d_v1 if n == "s" else None)

            def enter(e, n=n):
                r = e.alloc_register(f"flag_{n}")
                e.load([r], FLG[0:1, 0:1])
                flag_regs[n] = r
                with e.If_ne(r, 0):
                    for it in branch[n]:
                        it(e)
                e.sem_inc(s_join, 1)
                e.wait_ge(s_join, 4)
            q.items[n].append(enter)

        d_x = q.dma("s", s_m[6], lambda e: e.dma_start(
            RECX, bass.AP(REC1.tensor, 0, [[16, E // 16 + 1], [1, 128]])), d_v1, d_pad1)

        sct = {}

        def scatter(c):
            def put(c=c):
                return q.dma("p", s_g[16 + c % 16], lambda e: e.indirect_dma_start(
                    REC0, bass.IndirectOffsetOnAxis(ap=posi0[:, c:c + 1], axis=0), v0[:, c:c + 1], None),
                    t_pos0, t_v0, d_pad, sct.get(c - 16))
            sct[c] = put()
        for c in range(SC_FIRST):
            scatter(c)

        tf = ST[:, 320:327]
        VC(lambda e: e.tensor_copy(tf, SI[:, 0:NTB]), c_tt, c_idb)

        def windows(cum, wout):
            VC(lambda e: e.memset(wout, 0.0))
            for b in range(1, NW):
                VC(lambda e, b=b: e.scalar_tensor_tensor(out=wout, in0=tf, scalar=cum[:, b - 1:b], in1=wout,
                                                         op0=ALU.is_ge, op1=ALU.add))

        W0F, W1F = ST[:, 328:335], ST[:, 336:343]
        windows(cum0, W0F)
        VC(lambda e: e.tensor_copy(CUM0[:, :], cum0))
        I16A = sb("I16A", [128, 16], I16)
        t_w0 = VC(lambda e: e.tensor_copy(I16A[:, 0:NTB], W0F))
        def ident_store(dst_ap, src_ap, s_, *w):
            return q.dma("s", s_, lambda e: e.dma_start(dst_ap.rearrange("b p -> p b"), src_ap,
                                                        allow_slow_non_contiguous=True), *w)
        d_w0 = ident_store(TW0, I16A[:, 0:NTB], s_m[3], t_w0)
        l_w0 = q.dma("s", s_m[4], lambda e: e.dma_start(WTAB0[0:1, :], TW0.rearrange("b p -> (b p)").rearrange("(a n) -> a n", a=1)), d_w0)

        cnt1 = ST[:, 352:352 + NW]
        tot1, nt1, cum1, st1, sh1 = (ST[:, 384 + 32 * k:384 + 32 * k + NW] for k in range(5))
        VC(lambda e: e.tensor_scalar(wi, slot(1), 8, None, ALU.arith_shift_right))
        VC(lambda e: e.tensor_copy(wk, wi))
        VC(lambda e: e.memset(cnt1, 0.0))
        for b in range(NW):
            t_c1 = VC(lambda e, b=b: e.tensor_scalar(msk[0], wk, float(b), None, ALU.is_equal, ALU.add,
                                                     accum_out=cnt1[0:EP, b:b + 1]))
        m3 = T(lambda e: e.matmul(PS[2][:, 0:NW], ONES[0:EP, :], cnt1[0:EP, :], start=True, stop=True), t_c1)
        VC(lambda e: e.tensor_copy(tot1, PS[2][:, 0:NW]), m3)
        ti = SI[:, 8:8 + NW]
        al1 = ST[:, 592:592 + NW]
        VC(lambda e: e.tensor_tensor_scan(st1, ONES[:, 0:NW], tot1, 0.0, ALU.mult, ALU.add))
        VC(lambda e: e.tensor_copy(ti, st1))
        VC(lambda e: e.tensor_scalar(ti, ti, 4, 4, ALU.arith_shift_right, ALU.logical_shift_left))
        VC(lambda e: e.tensor_copy(al1, ti))
        VC(lambda e: e.tensor_copy(nt1[:, 0:1], st1[:, 0:1]))
        VC(lambda e: e.tensor_tensor(nt1[:, 1:NW], st1[:, 1:NW], al1[:, 0:NW - 1], ALU.subtract))
        VC(lambda e: e.tensor_scalar(ti, nt1, 127.0, None, ALU.add))
        VC(lambda e: e.tensor_scalar(ti, ti, 7, None, ALU.arith_shift_right))
        VC(lambda e: e.tensor_copy(nt1, ti))
        VC(lambda e: e.tensor_tensor_scan(cum1, ONES[:, 0:NW], nt1, 0.0, ALU.mult, ALU.add))
        windows(cum1, W1F)
        VC(lambda e: e.scalar_tensor_tensor(out=sh1, in0=cum1, scalar=-128.0, in1=al1, op0=ALU.mult, op1=ALU.add))
        VC(lambda e: e.tensor_copy(nt1, sh1))
        VC(lambda e: e.tensor_tensor(nt1[:, 1:NW], sh1[:, 1:NW], sh1[:, 0:NW - 1], ALU.subtract))
        BTF, tm = ST[:, 544:551], ST[:, 552:559]
        VC(lambda e: e.tensor_scalar(BTF, tf, 128.0, None, ALU.mult))
        for b in range(1, NW):
            VC(lambda e, b=b: e.tensor_scalar(tm, tf, cum1[:, b - 1:b], nt1[:, b - 1:b], ALU.is_ge, ALU.mult))
            VC(lambda e: e.tensor_tensor(BTF, BTF, tm, ALU.add))
        BTA, DT, FT, W256 = ST[:, 560:567], ST[:, 568:575], ST[:, 576:583], ST[:, 584:591]
        VC(lambda e: e.tensor_scalar(BTF, BTF, float(E), None, ALU.min))
        VC(lambda e: e.tensor_scalar(BTA, BTF, float(LAST), None, ALU.min))
        VC(lambda e: e.tensor_tensor(DT, BTF, BTA, ALU.subtract))
        VC(lambda e: e.tensor_scalar(FT, DT, 0.0, None, ALU.is_gt))
        VC(lambda e: e.tensor_scalar(W256, W1F, 256.0, None, ALU.mult))
        VC(lambda e: e.tensor_copy(I16A[:, 8:8 + NTB], W1F))
        VC(lambda e: e.tensor_scalar(BTF, BTF, 0.0625, None, ALU.mult))
        VC(lambda e: e.tensor_copy(SI[:, 44:44 + NTB], BTF))
        t_tb = VC(lambda e: e.tensor_copy(SI[:, 52:52 + NTB], BTA))
        d1 = ident_store(TW1, I16A[:, 8:8 + NTB], s_m[5], t_tb)
        d3 = ident_store(TBT, SI[:, 52:52 + NTB], s_m[7], t_tb)
        l_w1 = q.dma("s", s_m[8], lambda e: e.dma_start(WTAB1[0:1, :], TW1.rearrange("b p -> (b p)").rearrange("(a n) -> a n", a=1)), d1)
        q.wait("s", d3)

        RR = RC[:, 0:NTB * 128].rearrange("p (b l) -> p b l", l=128)
        RRI = RR.bitcast(I32)
        t_rr = [q.dma("p", s_g[b], lambda e, b=b: e.indirect_dma_start(
            RRI[:, b, :], None, RECX, bass.IndirectOffsetOnAxis(ap=SI[:, 44 + b:45 + b], axis=0)), d_x, t_tb)
            for b in range(NTB)]
        for c in range(SC_FIRST, EC):
            scatter(c)
        t_sc = [sct[c] for c in range(EC - 16, EC)]
        RL = RC[:, NTB * 128:NTB * 128 + 128].bitcast(I32)
        RLF = RC[:, NTB * 128 + 128:NTB * 128 + 256]
        t_rl = q.dma("s", s_m[9], lambda e: e.dma_start(
            RL, REC1[LAST:E, :].rearrange("(a l) o -> a (l o)", a=1).to_broadcast([128, 128])), t_c1)

        KR = [HN[:, 0:49, :].rearrange("p a b -> p (a b)")[:, k * 896:(k + 1) * 896].rearrange("p (b l) -> p b l", l=128) for k in range(5)]
        DI1 = HN[:, :, :].rearrange("p a b -> p (a b)")[:, 5 * 896:6 * 896].bitcast(I32).rearrange("p (b l) -> p b l", l=128)

        def decode(DI, dst_f, srci, sh, mask, *w):
            if mask is None:
                VC(lambda e: e.tensor_scalar(DI, srci, sh, None, ALU.arith_shift_right), *w)
            else:
                VC(lambda e: e.tensor_scalar(DI, srci, sh, mask, ALU.arith_shift_right, ALU.bitwise_and), *w)
            return VC(lambda e: e.tensor_copy(dst_f, DI))

        def columns(dst_t, src_rows, tok, banks, prev_evac):
            last = prev_evac
            for half, (a, b) in enumerate(((0, 4), (4, NTB))):
                bank = PS[banks[half]]
                for k in range(a, b):
                    mt = T(lambda e, k=k, a=a, bank=bank: e.transpose(
                        bank[:, (k - a) * 128:(k - a + 1) * 128], src_rows[:, k, :], IDENT[:, :]),
                        tok, prev_evac, c_id)
                last = V(lambda e, a=a, b=b, bank=bank: e.tensor_copy(
                    dst_t[:, a * 128:b * 128], bank[:, 0:(b - a) * 128]), mt)
            return last

        decode(DI1, KR[0], RRI, 14, None, t_rr)
        decode(DI1, KR[1], RRI, 1, 8191)
        decode(DI1, KR[2], RRI, 0, 16383)
        KA = KR[3]
        VC(lambda e: e.tensor_copy(KR[4], KR[0]))
        for b in range(NTB):
            VC(lambda e, b=b: e.tensor_scalar(KR[4][:, b, :], KR[0][:, b, :], W256[:, b:b + 1], None, ALU.subtract))
        VC(lambda e: e.tensor_scalar(RL, RL, 14, None, ALU.arith_shift_right), t_rl)
        VC(lambda e: e.tensor_copy(RLF, RL))
        for b in range(NTB):
            lm = ST[:, 0:128]
            VC(lambda e, b=b: e.tensor_scalar(lm, IOTA[:, 0:128], DT[:, b:b + 1], -1.0e4, ALU.is_lt, ALU.mult), t_pos0, c_io)
            VC(lambda e: e.tensor_tensor(lm, lm, RLF, ALU.add))
            VC(lambda e, b=b: e.tensor_scalar(lm, lm, W256[:, b:b + 1], None, ALU.subtract))
            VC(lambda e, b=b: e.tensor_tensor(lm, lm, KR[4][:, b, :], ALU.subtract))
            VC(lambda e, b=b: e.scalar_tensor_tensor(out=KA[:, b, :], in0=lm, scalar=FT[:, b:b + 1],
                                                     in1=KR[4][:, b, :], op0=ALU.mult, op1=ALU.add))
        t_dec = vv()
        KEYA = SC1
        e1 = columns(KEYA, KA, t_dec, (0, 1), None)
        e1 = columns(KEY1, KR[4], t_dec, (2, 3), None)
        e1 = columns(WE0, KR[0], t_dec, (0, 1), e1)
        d_kf = q.dma("s", s_in[31], lambda e: e.dma_start(KFD, WE0[:, :]), e1)
        e1 = columns(IDX1, KR[1], t_dec, (2, 3), e1)
        t_i3 = columns(IDX0, KR[2], t_dec, (0, 1), e1)
        d_i3 = q.dma("s", s_in[32], lambda e: e.dma_start(I3D, IDX0[:, :]), t_i3)
        cst("v", c_io)

        wregs = {}

        def window(e, n, tab, t):
            key = n
            if key not in wregs:
                wregs[key] = [e.alloc_register(f"w_{n}_{i}") for i in range(16)]
            if t % 16 == 0:
                e.load(wregs[key], tab[0:1, t:t + 16])
            return e.snap(wregs[key][t % 16], min_val=0, max_val=NW - 1)

        GD = GR[:, 0:32 * 128].rearrange("p (a d) -> p a d", d=128)

        def run_gather(acc, tab, table, idx, key, wgt, ready, extra=None, n=NTL):
            mm = {}

            def fetch(t):
                s = t % 16
                tok = q.dma("p", s_g[s], lambda e: e.indirect_dma_start(
                    GD[:, s, :], None, table, bass.IndirectOffsetOnAxis(ap=idx[:, t:t + 1], axis=0)),
                    ready, mm.get(t - 16))
                return GD[:, s, :], tok
            return sum_pass(acc, tab, fetch, key, wgt, ready, extra, mm, n)

        def sum_pass(acc, tab, fetch, key, wgt, ready, extra, mm, n=NTL):
            ad, oh = {}, {}
            for t in range(n + 2):
                if t < n:
                    def tile(t=t):
                        wt = extra(t) if extra is not None else None
                        if wgt is None:
                            oh[t] = V(lambda e: e.tensor_scalar(OH[:, t % 4, :], IOTA[:, :], key[:, t:t + 1], None,
                                                                ALU.is_equal), mm.get(t - 4), ready)
                        else:
                            oh[t] = V(lambda e: e.tensor_scalar(OH[:, t % 4, :], IOTA[:, :], key[:, t:t + 1],
                                                                wgt[:, t:t + 1], ALU.is_equal, ALU.mult),
                                      mm.get(t - 4), ready, wt)
                        rows, tok = fetch(t)
                        mm[t] = T(lambda e: e.matmul(PS[t % 4][:, 0:WN], rows, OH[:, t % 4, :],
                                                     start=True, stop=True),
                                  oh[t], tok, ad.get(t - 4), ready)
                    tile()
                if t >= 2:
                    def add(t=t - 2):
                        def go(e):
                            w = window(e, "v", tab, t)
                            sl = acc[:, bass.ds(w * WN, WN)]
                            return e.tensor_tensor(sl, sl, PS[t % 4][:, 0:WN], ALU.add)
                        return V(go, mm[t], ad.get(t - 1), ready)
                    ad[t - 2] = add()
            return ad[n - 1]

        ATT = RB[:, 0:NW * WN]
        m_att = V(lambda e: e.memset(ATT, 0.0), vv())
        aregs = {}
        amm = {}

        def attr_sp(e):
            r = e.alloc_register("flag_attr")
            e.load([r], FLG[0:1, 0:1])
            rr = [e.alloc_register(f"ba{i}") for i in range(8)]
            for which in (0, 1):
                with (e.If_eq(r, 0) if which == 0 else e.Else()):
                    table = edge_attr_128 if which == 0 else EA
                    for t in range(NTL):
                        s = t % 16
                        if t >= 16:
                            e.wait_ge(*amm[t - 16])
                        if t % 8 == 0:
                            e.load(rr, TBT.rearrange("b p -> (b p)").rearrange("(a n) -> a n", a=1)[0:1, t:t + 8])
                        v = e.snap(rr[t % 8], min_val=0, max_val=LAST)
                        e.dma_start(GD[:, s, :], table[bass.ds(v, 128), :]).then_inc(s_h[s], 16)

        q.wait("s", t_i3)
        q.items["s"].append(attr_sp)

        def attr_fetch(t):
            s = t % 16
            q.dcount[id(s_h[s])] = q.dcount.get(id(s_h[s]), 0) + 16
            return GD[:, s, :], (s_h[s], q.dcount[id(s_h[s])])

        t_att = sum_pass(ATT, WTAB1, attr_fetch, KEYA, None, [m_att, l_w1, t_i3, c_io], None, amm)
        d_att = q.dma("s", s_m[10], lambda e: e.dma_start(ATTD, ATT), t_att)

        def norm_pipe(pre, post, *w, pre_t=None):
            bs, mv, sd, rd = (ST[:, 0:6 * NT], ST[:, 6 * NT:8 * NT], ST[:, 8 * NT:9 * NT], ST[:, 9 * NT:10 * NT])
            mvv = mv.rearrange("p (t k) -> p t k", k=2)
            root = {}
            first = vv()

            def stats(g, k0, k1):
                if pre is not None:
                    pre(k0, k1)
                s0 = vv()
                for t in range(k0, k1):
                    V(lambda e, t=t: e.bn_stats(bs[:, 6 * t:6 * t + 6], XS[:, t, :]), first, s0, *w)
                s1 = vv()
                for t in range(k0, k1):
                    V(lambda e, t=t: e.bn_aggr(mv[:, 2 * t:2 * t + 2], bs[:, 6 * t:6 * t + 6]), s1)
                VC(lambda e: e.tensor_scalar(sd[:, k0:k1], mvv[:, k0:k1, 1], 1.0e-5, None, ALU.add))
                root[g] = A(lambda e: e.activation(sd[:, k0:k1], sd[:, k0:k1], ACT.Sqrt), vv())

            def norm(g, k0, k1):
                VC(lambda e: e.reciprocal(rd[:, k0:k1], sd[:, k0:k1]), root[g])
                s2 = vv()
                toks = {}
                for t in range(k0, k1):
                    toks[t] = V(lambda e, t=t: e.tensor_scalar(HN[:, t, 0:128], XS[:, t, :], mvv[:, t, 0:1],
                                                               rd[:, t:t + 1], ALU.subtract, ALU.mult), s2, *w)
                post(k0, k1, toks)

            if pre_t is not None:
                pre_t(0, 8)
            for g in range(8):
                if g < 7:
                    stats(g, 8 * g, min(8 * g + 8, NT))
                if g < 6 and pre_t is not None:
                    pre_t(8 * g + 8, min(8 * g + 16, NT))
                if g:
                    norm(g - 1, 8 * g - 8, min(8 * g, NT))

        def transposer(dst_t, *w):
            outs, ev = {}, {}

            def go(k0, k1, toks):
                for a in range(k0, k1, 4):
                    b = min(a + 4, k1)
                    bank = PS[6 + (a // 4) % 2]
                    for k in range(a, b):
                        mt = T(lambda e, k=k, a=a, bank=bank: e.transpose(
                            bank[:, (k - a) * 128:(k - a + 1) * 128], HN[:, k, 0:128], IDENT[:, :]),
                            toks[k], ev.get(a // 4 - 2))
                    ev[a // 4] = A(lambda e, a=a, b=b, bank=bank: e.activation(
                        dst_t[:, a * 128:b * 128], bank[:, 0:(b - a) * 128], ACT.Relu), mt, *w)
                    for k in range(a, b):
                        outs[k] = ev[a // 4]
            return go, outs

        def relu_rows(table, s_, k0, k1):
            r = A(lambda e: e.activation(HN[:, k0:k1, 0:128], HN[:, k0:k1, 0:128], ACT.Relu), q.now("t"))
            return store_rows(table, HN[:, :, 0:128], s_, k0, k1, r)

        def store_rows(table, src_v, s_, k0, k1, *w):
            tv = table.rearrange("(t p) d -> p t d", p=128)
            return q.dma("s", s_, lambda e: e.dma_start(tv[:, k0:k1, :], src_v[:, k0:k1, :]), *w)

        ACC = RA[:, 0:NW * WN]
        z0 = V(lambda e: e.memset(RA[:, NP:NW * WN], 0.0), t_c1)
        tr, ht = transposer(ACC, t_c1, t_v1, d_v1)
        HF = HN[:, :, 0:128]
        tab_tok = []

        def post0(k0, k1, toks):
            tr(k0, k1, toks)
            tab_tok.append(relu_rows(TAB[0], s_m[11], k0, k1))
        norm_pipe(None, post0, l_x, l_x2, t_i3)
        d_tab = tab_tok[-1]
        ht = list(ht.values())

        R0 = RC[:, 0:NTB * 128].rearrange("p (b l) -> p b l", l=128)
        l_r0 = q.dma("s", s_m[12], lambda e: e.dma_start(
            R0.bitcast(I32), REC0.rearrange("(b p l) o -> p b (l o)", p=128, l=128)), t_sc, t_dec)
        K0 = [RC[:, (k + 1) * 896:(k + 2) * 896].rearrange("p (b l) -> p b l", l=128) for k in range(3)]
        DI0 = RC[:, 4 * 896:5 * 896].bitcast(I32).rearrange("p (b l) -> p b l", l=128)
        decode(DI0, K0[0], R0.bitcast(I32), 21, None, l_r0, t_sc)
        decode(DI0, K0[1], R0.bitcast(I32), 8, 8191)
        decode(DI0, K0[2], R0.bitcast(I32), 0, 255)
        t_d0 = vv()
        TYP = SC1
        cst("v", d_kf, d_i3)
        e0 = columns(KEY0, K0[0], t_d0, (0, 1), t_att)
        e0 = columns(IDX0, K0[1], t_d0, (2, 3), t_att)
        e0 = columns(TYP, K0[2], t_d0, (0, 1), e0)
        t_e0 = e0

        wsel_s = RC[:, 5 * 896:5 * 896 + 2 * NREL]

        def wsel(t):
            return V(lambda e: e.scalar_tensor_tensor(
                out=wsel_s[:, (t % 2) * NREL:(t % 2 + 1) * NREL], in0=IOTA[:, 0:NREL], scalar=TYP[:, t:t + 1], in1=RELB[:, :],
                op0=ALU.is_equal, op1=ALU.mult, accum_out=WE0[:, t:t + 1]), l_rel, t_e0, ws_prev.get(t - 2))
        ws_prev = {}

        def wsel_first(t):
            if t == 0:
                ws_prev[0] = wsel(0)
            if t + 1 < NT0:
                ws_prev[t + 1] = wsel(t + 1)
            return ws_prev[t]

        V3R, U3B = RC[:, 5376 + 512:5376 + 640], RC[:, 5376 + 640:5376 + 768]
        t_ = V(lambda e: e.tensor_copy(U3B, COLS[:, 2:3].to_broadcast([128, 128])), l_u, t_e0)
        m = T(lambda e: e.matmul(PS[4][:, 0:128], U3B, WT[:, iEN, :], start=True, stop=True), t_, l_w[iEN], *ht)
        t_v3 = V(lambda e: e.tensor_copy(V3R, PS[4][:, 0:128]), m)
        t_q2 = V(lambda e: e.memset(HN[:, :, 129:132], 0.0), d_i3)

        acc_tok = [ht, z0]
        tabs = TAB
        for layer, iw in enumerate((iW1, iW2, iW3)):
            done = run_gather(ACC, WTAB0, tabs[layer], IDX0, KEY0, WE0,
                              [d_tab, l_w0, t_e0, *([] if layer else [*ht, z0])],
                              extra=wsel_first if layer == 0 else None, n=NT0)
            ev, mt = {}, {}
            for g in range(13):
                k0, k1 = 4 * g, min(4 * g + 4, NT)
                bank = PS[4 + g % 3]
                for k in range(k0, k1):
                    mt[g] = T(lambda e, k=k, k0=k0, bank=bank, iw=iw: e.matmul(
                        bank[:, (k - k0) * 128:(k - k0 + 1) * 128], ACC[:, k * 128:(k + 1) * 128], WT[:, iw, :],
                        start=True, stop=True), done, ev.get(g - 3), l_w[iw])
                ev[g] = A(lambda e, k0=k0, k1=k1, bank=bank: e.activation(
                    HN[:, k0:k1, 0:128], bank[:, 0:(k1 - k0) * 128].rearrange("p (a b) -> p a b", b=128), ACT.Tanh),
                    mt[g], d_tab, t_v3)
                if layer < 2 and g % 2 == 1 or g == 12 and layer < 2:
                    a = 8 * (g // 2)
                    d_new = store_rows(tabs[layer + 1], HF, s_m[13 + layer], a, k1, ev[g])
                if layer == 2:
                    for k in range(k0, k1):
                        tq = V(lambda e, k=k: e.scalar_tensor_tensor(
                            out=OH[:, k % 2, 0:128], in0=HN[:, k, 0:128], scalar=1.0, in1=V3R, op0=ALU.mult,
                            op1=ALU.mult, accum_out=HN[:, k, 128:129]), ev[g], t_v3, t_q2, *([vv()] if k % 2 == 0 else []))
                    if g % 2 == 1 or g == 12:
                        a = 8 * (g // 2)
                        d_q = store_rows(TABQ, HN[:, :, 0:132], s_m[15], a, k1, tq)
            d_tab = d_new
            ev2 = {}
            for g in range(13):
                c0_, c1_ = 512 * g, min(512 * g + 512, NW * WN)
                bank = PS[g % 4]
                m = T(lambda e, c0_=c0_, c1_=c1_, bank=bank, iw=iw: e.matmul(
                    bank[:, 0:c1_ - c0_], WT[:, iw, :], ACC[:, c0_:c1_], start=True, stop=True), ev2.get(g - 4))
                ev2[g] = A(lambda e, c0_=c0_, c1_=c1_, bank=bank: e.activation(
                    ACC[:, c0_:c1_], bank[:, 0:c1_ - c0_], ACT.Tanh), m)
            acc_tok = [ev2[12]]
            cst("v", ev2[12])
            hn_ev = ev

        m = T(lambda e: e.matmul(PS[4][:, 0:1], WT[:, iEN, :], COLS[:, 0:1], start=True, stop=True), l_u, l_w[iEN], hn_ev[12])
        m = T(lambda e: e.transpose(PS[4][:, 128:256], WT[:, iRE, :], IDENT[:, :]), l_w[iRE])
        V(lambda e: e.tensor_copy(COLS[:, 6:7], PS[4][:, 0:1]), m)
        RET = ST[:, 500:628]
        VC(lambda e: e.tensor_copy(RET, PS[4][:, 128:256]))
        m = T(lambda e: e.matmul(PS[5][:, 0:1], RET, COLS[:, 3:4], start=True, stop=True), vv(), l_ra)
        VC(lambda e: e.tensor_tensor(COLS[:, 8:9], PS[5][:, 0:1], COLS[:, 1:2], ALU.mult), m)
        m = T(lambda e: e.matmul(PS[5][:, 1:2], ONES[:, :], COLS[:, 8:9], start=True, stop=True), vv())
        VC(lambda e: e.tensor_copy(COLS[:, 9:10], PS[5][:, 1:2]), m)
        V1B = RC[:, 512:640]
        t_v1b = VC(lambda e: e.tensor_copy(V1B, COLS[:, 6:7].to_broadcast([128, 128])), done)
        PB = RB[:, 0:NW * WN]
        ev2 = {}
        for g in range(13):
            c0_, c1_ = 512 * g, min(512 * g + 512, NW * WN)
            bank = PS[g % 4]
            m = T(lambda e, c0_=c0_, c1_=c1_, bank=bank: e.matmul(
                bank[:, 0:c1_ - c0_], V1B, ACC[:, c0_:c1_], start=True, stop=True), ev2.get(g - 4), t_v1b, acc_tok)
            ev2[g] = A(lambda e, c0_=c0_, c1_=c1_, bank=bank: e.activation(
                PB[:, c0_:c1_], bank[:, 0:c1_ - c0_], ACT.Copy), m, d_att)
        t_pb = ev2[12]
        t_accfree = m

        GS = 11
        NG = -(-NT0 // GS)
        S0, QE = SC1, SC2
        MG, FG, ZG = ST[:, 0:80], ST[:, 80:160], ST[:, 160:240]
        GM, SW = ST[:, 240:320], ST[:, 320:352]
        MR = ST[0:1, 352:356]
        junk = RC[:, 0:2 * WN].rearrange("p (a b) -> p a b", b=WN)
        RG0 = GR[:, 0:3 * GS * 132].rearrange("p (a d) -> p a d", d=132)
        z1 = V(lambda e: e.memset(ACC, 0.0), t_accfree, d_q)
        V(lambda e: e.memset(ZG, 0.0))
        t_z0 = V(lambda e: e.tensor_scalar(WE0[:, 0:NT0], KEY0[:, 0:NT0], 255.5, -BIG, ALU.is_gt, ALU.mult), done)
        pe_t, gat, ohb, oh0, mm0, ad0, lasts0, exp_t, fac_t = {}, {}, {}, {}, {}, {}, {}, {}, {}
        tm0 = {}

        def gather0(t):
            s = t % (3 * GS)
            gat[t] = q.dma("p", s_g[s], lambda e: e.indirect_dma_start(
                RG0[:, s, :], None, TABQ, bass.IndirectOffsetOnAxis(ap=IDX0[:, t:t + 1], axis=0)),
                d_q, done, mm0.get(t - 3 * GS), tm0.get(t // GS - 3))

        def score(t):
            def go(e):
                w = window(e, "v", WTAB0, t)
                return e.scalar_tensor_tensor(out=junk[:, t % 2, :], in0=IOTA[:, :], scalar=KEY0[:, t:t + 1],
                                              in1=PB[:, bass.ds(w * WN, WN)], op0=ALU.is_equal, op1=ALU.mult,
                                              accum_out=S0[:, t:t + 1])
            pe_t[t] = V(go, t_pb, pe_t.get(t - 2), done)

        def group_of(g):
            return slice(g * GS, min(g * GS + GS, NT0))

        def stage1(g):
            sl = group_of(g)
            n = sl.stop - sl.start
            s = sl.start % (3 * GS)
            tm0[g] = V(lambda e: e.tensor_tensor(S0[:, sl], S0[:, sl], RG0[:, s:s + n, 128], ALU.add),
                       [gat[t] for t in range(sl.start, sl.stop)], vv())

        def stage2(g):
            sl = group_of(g)
            V(lambda e: e.tensor_scalar(S0[:, sl], S0[:, sl], COLS[:, 9:10], None, ALU.add), tm0[g])

        def stage3(g):
            sl = group_of(g)
            V(lambda e: e.scalar_tensor_tensor(out=QE[:, sl], in0=S0[:, sl], scalar=0.01, in1=S0[:, sl],
                                               op0=ALU.mult, op1=ALU.max), vv())

        def stage4(g):
            sl = group_of(g)
            V(lambda e: e.tensor_tensor(QE[:, sl], QE[:, sl], WE0[:, sl], ALU.add), vv(), t_z0)

        def stage5(g):
            sl = group_of(g)
            t_ = V(lambda e: e.tensor_reduce(GM[:, g:g + 1], QE[:, sl], AX_X, ALU.max), vv())
            st_m[g] = T(lambda e: e.matmul(PS[4 + g % 2][0:1, 0:128], GM[:, g:g + 1], IDENT[:, :],
                                           start=True, stop=True), t_, st_b.get(g - 2))

        def stage6(g):
            t_ = V(lambda e: e.tensor_reduce(MR[:, g % 4:g % 4 + 1], PS[4 + g % 2][0:1, 0:128], AX_X, ALU.max),
                   st_m[g], vv())
            st_m[g] = T(lambda e: e.matmul(PS[6 + g % 2][:, 0:1], ONES[0:1, :], MR[:, g % 4:g % 4 + 1],
                                           start=True, stop=True), t_)

        def stage7(g):
            sl = group_of(g)
            if g == 0:
                t_ = V(lambda e: e.tensor_copy(MG[:, 0:1], PS[6][:, 0:1]), st_m[0], vv())
            else:
                t_ = V(lambda e: e.tensor_tensor(MG[:, g:g + 1], MG[:, g - 1:g], PS[6 + g % 2][:, 0:1], ALU.max),
                       st_m[g], vv())
            st_b[g] = t_
            fac_t[g] = A(lambda e: e.activation(FG[:, g:g + 1], MG[:, g:g + 1], ACT.Exp,
                                                bias=MG[:, max(g - 1, 0):max(g - 1, 0) + 1], scale=-1.0), t_)

        def stage8(g):
            sl = group_of(g)
            t_ = V(lambda e: e.tensor_scalar(QE[:, sl], QE[:, sl], MG[:, g:g + 1], None, ALU.subtract), vv())
            exp_t[g] = A(lambda e: e.activation(S0[:, sl], QE[:, sl], ACT.Exp, accum_out=ZG[:, g:g + 1]), t_)

        def apply0(t):
            g = t // GS
            s = t % (3 * GS)
            ohb[t] = V(lambda e: e.tensor_scalar(OHB[:, t % 4, :], IOTAB[:, :], KEY0[:, t:t + 1], None, ALU.is_equal),
                       oh0.get(t - 4), done)
            oh0[t] = A(lambda e: e.activation(OH[:, t % 4, :], OHB[:, t % 4, :], ACT.Copy, scale=S0[:, t:t + 1]),
                       ohb[t], exp_t[g], mm0.get(t - 4))
            mm0[t] = T(lambda e: e.matmul(PS[t % 4][:, 0:WN], RG0[:, s, 0:128], OH[:, t % 4, :],
                                          start=True, stop=True), oh0[t], gat[t], ad0.get(t - 4), t_pb)

        def add0(t):
            g = t // GS
            first = t % GS == 0

            def go(e):
                w = window(e, "v2", WTAB0, t)
                sl = ACC[:, bass.ds(w * WN, WN)]
                if first:
                    return e.scalar_tensor_tensor(out=sl, in0=sl, scalar=FG[:, g:g + 1], in1=PS[t % 4][:, 0:WN],
                                                  op0=ALU.mult, op1=ALU.add)
                return e.tensor_tensor(sl, sl, PS[t % 4][:, 0:WN], ALU.add)
            ad0[t] = V(go, mm0[t], ad0.get(t - 1), z1, fac_t[g] if first else None)

        st_m, st_b = {}, {}
        stages = [stage1, stage2, stage3, stage4, stage5, stage6, stage7, stage8]
        at = [3, 3, 3, 4, 4, 6, 8, 8]
        LAG = GS + 10
        for t in range(NT0 + GS + LAG + 4):
            if t < NT0:
                gather0(t)
                score(t)
            for k, fn in enumerate(stages):
                g, r = divmod(t - GS - at[k], GS)
                if r == 0 and 0 <= g < NG:
                    fn(g)
            if 0 <= t - LAG < NT0:
                apply0(t - LAG)
            if 0 <= t - LAG - 3 < NT0:
                add0(t - LAG - 3)
        d_l0 = ad0[NT0 - 1]
        MX = MG[:, NG - 1:NG]
        VC(lambda e: e.tensor_scalar(GM[:, 0:NG], MG[:, 0:NG], MX, None, ALU.subtract), q.now("a"))
        t_ = A(lambda e: e.activation(GM[:, 0:NG], GM[:, 0:NG], ACT.Exp), vv())
        VC(lambda e: e.tensor_tensor(ZG[:, 0:NG], ZG[:, 0:NG], GM[:, 0:NG], ALU.mult), t_)
        VC(lambda e: e.tensor_reduce(COLS[:, 12:13], ZG[:, 0:NG], AX_X, ALU.add))
        t_z = P(lambda e: e.partition_all_reduce(COLS[:, 13:14], COLS[:, 12:13], 128, RADD), vv())
        VC(lambda e: e.tensor_scalar(RC[:, 0:NG], IOTA[:, 0:NG], float(GS), None, ALU.mult))
        for w in range(NW):
            VC(lambda e, w=w: e.tensor_scalar(RC[:, 128:128 + NG], RC[:, 0:NG], CUM0[:, w:w + 1], None, ALU.is_lt))
            VC(lambda e, w=w: e.tensor_tensor(RC[:, 256:256 + NG], RC[:, 128:128 + NG], GM[:, 0:NG], ALU.mult))
            VC(lambda e, w=w: e.tensor_reduce(SW[:, w:w + 1], RC[:, 256:256 + NG], AX_X, ALU.max))
        VC(lambda e: e.reciprocal(COLS[:, 14:15], COLS[:, 13:14]), t_z)
        t_sw = VC(lambda e: e.tensor_scalar(SW[:, 0:NW], SW[:, 0:NW], COLS[:, 14:15], None, ALU.mult))

        V(lambda e: e.tensor_scalar(ADC[:, 0:8], BD[:, :], COLS[:, 4:5], None, ALU.mult), l_as, c_bd, c_idb)
        t_adc = V(lambda e: e.tensor_scalar(ADC[:, 8:16], BD[:, :], COLS[:, 5:6], None, ALU.mult), l_ad)
        m = T(lambda e: e.transpose(PS[0][:, 0:128], WT[:, iGW, :], IDENT[:, :]), l_w[iGW], d_l0)
        t_ = VC(lambda e: e.tensor_copy(RET, PS[0][:, 0:128]), m)
        m = T(lambda e: e.matmul(PS[1][:, 0:16], RET, ADC[:, :], start=True, stop=True), t_, t_adc)
        V(lambda e: e.tensor_copy(RHS1[:, 128:144], PS[1][:, 0:16]), m)
        t_rhs = V(lambda e: e.tensor_copy(RHS1[:, 0:128], WT[:, iGW, :]))
        evt, mtt = {}, {}

        def pre1_t(k0, k1):
            for k in range(k0, k1):
                g = k // 4
                mtt[k] = T(lambda e, k=k, g=g: e.transpose(
                    PS[4 + g % 2][:, (k % 4) * 128:(k % 4 + 1) * 128], ACC[:, k * 128:(k + 1) * 128], IDENT[:, :]),
                    d_l0, evt.get(g - 2))

        def pre1(k0, k1):
            for k in range(k0, k1, 2):
                c = min(k + 2, k1)
                g = k // 4
                evt[g] = V(lambda e, k=k, c=c, g=g: e.scalar_tensor_tensor(
                    out=XS[:, k:c, :],
                    in0=PS[4 + g % 2][:, (k % 4) * 128:(k % 4 + c - k) * 128].rearrange("p (a b) -> p a b", b=128),
                    scalar=SW[:, k // 2:k // 2 + 1], in1=XS[:, k:c, :], op0=ALU.mult, op1=ALU.add), mtt[min(4 * g + 3, k1 - 1)], t_sw)

        tr, ht = transposer(ACC)
        ev, evk = {}, {}
        cnt_g = [0]
        tab_tok = []

        def post1(k0, k1, toks):
            tr(k0, k1, toks)
            for a in range(k0, k1, 3):
                b = min(a + 3, k1)
                g = cnt_g[0]
                cnt_g[0] += 1
                bank = PS[g % 4]
                for k in range(a, b):
                    mt_ = T(lambda e, k=k, a=a, bank=bank: e.matmul(
                        bank[:, (k - a) * 144:(k - a + 1) * 144], ACC[:, k * 128:(k + 1) * 128], RHS1[:, :],
                        start=True, stop=True), ht[k], t_rhs, ev.get(g - 4))
                ev[g] = A(lambda e, a=a, b=b, bank=bank: e.activation(
                    HN[:, a:b, :], bank[:, 0:(b - a) * 144].rearrange("p (a b) -> p a b", b=144), ACT.Copy), mt_)
            tab_tok.append(store_rows(TABG, HN[:, :, 0:136], s_m[11], k0, k1, ev[g]))
        norm_pipe(pre1, post1, pre_t=pre1_t)
        t_hw = ev[max(ev)]
        d_g = tab_tok[-1]
        t_x1 = evt[12]
        AR = ST[:, 0:NT * 8].rearrange("p (t h) -> p t h", h=8)
        AF = RC[:, 0:NT * 8].rearrange("p (t h) -> p t h", h=8)
        V(lambda e: e.memset(AD3[:, :, :], 0.0), t_rhs)
        VC(lambda e: e.tensor_copy(AR, HN[:, :, 136:144]), t_hw)
        for k in range(3):
            part = AD3[:, 0:NT, 8 * k:8 * k + 8]
            VC(lambda e, part=part: e.tensor_copy(part, AR))
            if k < 2:
                VC(lambda e, part=part: e.tensor_copy(AF, part))
                VC(lambda e: e.tensor_tensor(AR, AR, AF, ALU.subtract))
        t_ad3 = vv()
        NL1 = 816
        NC1 = NL1 // 16
        OBR = RA[:, :].bitcast(BF16).rearrange("p (a b) -> p a b", b=WN)
        AC1 = RB[:, :].rearrange("p (n f) -> p n f", f=146)
        GRP = [GR[:, 0:2336], GR[:, 2336:4672], RC[:, 4192:6528]]
        GRP = [g.rearrange("p (a f) -> p a f", f=146) for g in GRP]
        ECH = [RC[:, 0:128], RC[:, 128:256]]
        K8, KT = RC[:, 256:384], RC[:, 384:512]
        BN = RC[:, 512:640]
        FW, FV, RV, RW = (RC[:, 640 + 128 * k:768 + 128 * k] for k in range(4))
        AEC, DCH = RC[:, 1152:1280], RC[:, 1280:1408]
        NER, NBR, NBB, KLR = RC[0:1, 1408:2224], RC[0:1, 2224:3040], RC[0:1, 3040:3856], WE0[0:1, 0:816]
        TR17, V17 = ST[0:1, 0:136], ST[0:1, 136:272]
        F17 = [ST[0:1, 272:408], ST[0:1, 408:544]]
        CFR = RC[0:1, 3856:3984]
        TRB, VBR = OH[0:1, 3, 0:128], OH[0:1, 3, 128:256]
        FBR, CBR = WE0[0:1, 0:128], WE0[0:1, 128:256]
        OHR, OHN = WE0[0:1, 256:512], WE0[0:1, 512:768]
        R18, DR = ST[0:1, 544:562], ST[0:1, 562:570]
        F18 = ST[:, 576:612].rearrange("p (a k) -> p a k", k=18)
        all_hw = [ev[k] for k in ev]
        VC(lambda e: e.memset(RB[:, :], 0.0), all_hw, t_x1)
        z4 = vv()
        VC(lambda e: e.memset(BN, 0.0), all_hw)
        for g in GRP:
            VC(lambda e, g=g: e.memset(g[:, :, 144:146], 1.0), d_l0)
        VC(lambda e: e.memset(TR17, -BIG))
        VC(lambda e: e.memset(F17[1], -BIG))
        VC(lambda e: e.memset(CBR, -BIG), d_l0)
        VC(lambda e: e.memset(R18[:, 8:18], 0.0))
        VC(lambda e: e.memset(R18[:, 16:17], 1.0))
        VC(lambda e: e.tensor_scalar(SC1[:, 0:NL1], KEY1[:, 0:NL1], 255.5, -BIG, ALU.is_gt, ALU.mult), t_i3)
        VC(lambda e: e.tensor_scalar(SC2[:, 0:NL1], KEY1[:, 0:NL1], -0.5, -BIG, ALU.is_lt, ALU.mult))
        VC(lambda e: e.tensor_tensor(SC1[:, 0:NL1], SC1[:, 0:NL1], SC2[:, 0:NL1], ALU.add))
        l_kf = q.dma("s", s_in[33], lambda e: e.dma_start(SC2[:, :], KFD), d_kf, vv())
        for a, b in ((0, 512), (512, NL1)):
            m = T(lambda e, a=a, b=b: e.matmul(PS[4 + a // 512][0:1, 0:b - a], IDENT[:, 127:128], SC2[:, a:b],
                                               start=True, stop=True), l_kf, all_hw, evt[12], [ht[k] for k in ht])
        VC(lambda e: e.tensor_copy(KLR[:, 0:512], PS[4][0:1, 0:512]), m)
        VC(lambda e: e.tensor_copy(KLR[:, 512:NL1], PS[5][0:1, 0:NL1 - 512]))
        KFR = SC2[0:1, 0:NL1]
        VC(lambda e: e.memset(NER[:, 0:1], 1.0), l_kf, all_hw)
        VC(lambda e: e.tensor_tensor(NER[:, 1:NL1], KFR[:, 1:NL1], KLR[:, 0:NL1 - 1], ALU.not_equal))
        VC(lambda e: e.tensor_scalar(NER, NER, -BIG, None, ALU.mult))
        VC(lambda e: e.tensor_tensor(KLR, KFR, KLR, ALU.not_equal))
        VC(lambda e: e.tensor_scalar(KLR, KLR, -BIG, None, ALU.mult))
        VC(lambda e: e.tensor_tensor(NBR, NER, KLR, ALU.add))
        VC(lambda e: e.memset(NBB, -BIG))
        VC(lambda e: e.tensor_tensor(NBB[:, 0:NL1 - 1], NER[:, 1:NL1], KLR[:, 0:NL1 - 1], ALU.add))
        VC(lambda e: e.memset(NBB.rearrange("p (c g) -> p c g", g=16)[:, :, 15:16], -BIG))
        t_pre = VC(lambda e: e.memset(CBR, -BIG))

        ohb1, tr1, oht1, lk1, gt1, mmb, adb, adh, ohx, gx = {}, {}, {}, {}, {}, {}, {}, {}, {}, {}
        red, e_t, f_t, ex_t, fac, scw = {}, {}, {}, {}, {}, {}
        small, big_v, big_a, dr_t = {}, {}, {}, {}
        wlast, wb = {}, {}

        def rows_of(t):
            return GRP[(t // 16) % 3][:, t % 16, :]

        def gather1(t):
            gt1[t] = q.dma("p", s_g[t % 34], lambda e: e.indirect_dma_start(
                rows_of(t)[:, 0:136], None, TABG, bass.IndirectOffsetOnAxis(ap=IDX1[:, t:t + 1], axis=0)),
                [d_g, t_i3, d_l0, z4], all_hw, mmb.get(t - 48), gt1.get(t - 34))

        def onehot1(t):
            ohb1[t] = V(lambda e: e.tensor_scalar(OBR[:, t % 51, :], IOTAB[:, :], KEY1[:, t:t + 1], None, ALU.is_equal),
                        tr1.get(t - 51), ohx.get(t - 51), all_hw)
            pb = PS[3 + t % 2][:, 0:128].bitcast(BF16)
            for h in range(2):
                tr1[t] = T(lambda e, h=h: e.transpose(pb[:, h * 128:h * 128 + 128],
                                                      OBR[:, t % 51, h * 128:(h + 1) * 128], IDENTB[:, :]),
                           ohb1[t], oht1.get(t - 2), c_idb, t_pre)
            oht1[t] = A(lambda e: e.activation(OHT[:, t % 4, :], pb, ACT.Copy), tr1[t], lk1.get(t - 4))

        def look(t):
            c = (t % 16) * 24

            def go(e, h):
                if h == 0:
                    wlast["v"] = window(e, "t", WTAB1, t)
                w = wlast["v"]
                return e.matmul(PS[5][:, c:c + 24], OHT[:, t % 4, h * 128:(h + 1) * 128],
                                AD3[:, bass.ds(w * 2 + h, 1), :].rearrange("p a b -> p (a b)"),
                                start=(h == 0), stop=(h == 1))
            T(lambda e: go(e, 0), oht1[t], t_ad3, red.get(t // 16 - 1), t_pre)
            lk1[t] = T(lambda e: go(e, 1))

        def v8(ap):
            return ap.rearrange("p (g h) -> p g h", h=8)

        q.add("w", sem("e_w"))
        q.wait("w", t_pre, t_ad3)
        ohr, ka, sc3, sc5, tr_t, tb_t = {}, {}, {}, {}, {}, {}

        def W(fn, *w):
            return q.op("w", fn, q.now("w"), *w)

        def c0(c):
            red[c] = W(lambda e: e.tensor_reduce(v8(AEC), PS[5][:, 0:384].rearrange("p (t k h) -> p t h k", k=3, h=8),
                                                 AX_X, ALU.add), lk1[16 * c + 15])
            ka[c] = A(lambda e: e.activation(v8(K8), SC2[:, 16 * c:16 * c + 16].unsqueeze(2).to_broadcast([128, 16, 8]),
                                             ACT.Copy), big_v.get(c - 1), l_kf, t_pre)

        def c1(c):
            E_ = ECH[c % 2]
            W(lambda e: e.tensor_tensor(v8(E_), v8(AEC), GRP[c % 3][:, :, 128:136], ALU.add), red[c],
              [gt1[t] for t in range(16 * c, 16 * c + 16)])
            W(lambda e: e.scalar_tensor_tensor(out=E_, in0=E_, scalar=0.2, in1=E_, op0=ALU.mult, op1=ALU.max))
            e_t[c] = W(lambda e: e.tensor_tensor(
                v8(E_), v8(E_), SC1[:, 16 * c:16 * c + 16].unsqueeze(2).to_broadcast([128, 16, 8]), ALU.add))
            T(lambda e: e.transpose(PS[6][:, 0:128], E_, IDENT[:, :]), e_t[c], ex_t.get(c - 1), t_pre)
            big_v[c] = T(lambda e: e.transpose(PS[6][:, 128:256], K8, IDENT[:, :]), ka[c])
            big_a[c] = A(lambda e: e.activation(KT, PS[6][:, 128:256], ACT.Copy), big_v[c], f_t.get(c - 1))

        def c2(c):
            W(lambda e: e.tensor_tensor(BN[:, 1:128], KT[:, 1:128], KT[:, 0:127], ALU.not_equal), big_a[c])
            f_t[c] = W(lambda e: e.tensor_scalar(BN[:, 1:128], BN[:, 1:128], -BIG, None, ALU.mult))
            t_ = W(lambda e: e.tensor_tensor_scan(FW, BN, PS[6][:, 0:128], -BIG, ALU.add, ALU.max))
            small[c] = T(lambda e: e.matmul(PS[7][0:1, 0:128], FW[:, 127:128], IDENT[:, :], start=True, stop=True),
                         t_, fac.get(c - 1))
            A(lambda e: e.activation(
                TR17.rearrange("p (h g) -> p h g", g=17)[:, :, 1:17],
                NBR[:, 16 * c:16 * c + 16].unsqueeze(1).to_broadcast([1, 8, 16]), ACT.Copy), t_pre, sc3.get(c - 1))
            tr_t[c] = A(lambda e: e.activation(V17.rearrange("p (h g) -> p h g", g=17)[:, :, 0:1],
                                     F17[(c - 1) % 2].rearrange("p (h g) -> p h g", g=17)[:, :, 16:17], ACT.Copy))

        def c3(c):
            W(lambda e: e.tensor_copy(V17.rearrange("p (h g) -> p g h", g=17)[:, 1:17, :],
                                      PS[7][0:1, 0:128].rearrange("p (g h) -> p g h", h=8)), small[c], tr_t[c])
            sc3[c] = W(lambda e: e.tensor_tensor_scan(F17[c % 2], TR17, V17, -BIG, ALU.add, ALU.max), dr_t.get(c - 1))
            t_ = W(lambda e: e.tensor_tensor(
                v8(CFR), F17[c % 2].rearrange("p (h g) -> p g h", g=17)[:, 0:16, :],
                NER[:, 16 * c:16 * c + 16].unsqueeze(2).to_broadcast([1, 16, 8]), ALU.add))
            small[c] = T(lambda e: e.matmul(PS[7][:, 128:129], CFR, ONES[0:1, 0:1], start=True, stop=True), t_)

        def c4(c):
            W(lambda e: e.tensor_copy(COLS[:, 0:1], PS[7][:, 128:129]), small[c])
            W(lambda e: e.tensor_tensor_scan(FV, BN, FW, COLS[:, 0:1], ALU.add, ALU.max))
            W(lambda e: e.tensor_copy(COLS[:, 1:2], FV[:, 127:128]))
            t_ = W(lambda e: e.tensor_tensor_scan(RV[:, 0:127][:, ::-1], BN[:, 1:128][:, ::-1], FV[:, 0:127][:, ::-1],
                                                   COLS[:, 1:2], ALU.add, ALU.max))
            small[c] = T(lambda e: e.matmul(PS[7][0:1, 256:384], RV[:, 0:1], IDENT[:, :], start=True, stop=True), t_)
            tb_t[c] = A(lambda e: e.activation(
                TRB.rearrange("p (h g) -> p h g", g=16),
                NBB[:, 16 * c:16 * c + 16].unsqueeze(1).to_broadcast([1, 8, 16]), ACT.Copy), sc5.get(c - 1))

        def c5(c):
            W(lambda e: e.tensor_copy(VBR.rearrange("p (h g) -> p g h", g=16),
                                      PS[7][0:1, 256:384].rearrange("p (g h) -> p g h", h=8)), small[c])
            sc5[c] = W(lambda e: e.tensor_tensor_scan(FBR[:, ::-1], TRB[:, ::-1], VBR[:, ::-1], -BIG, ALU.add, ALU.max), tb_t[c])
            t_ = W(lambda e: e.tensor_tensor(
                v8(CBR)[:, 0:15, :], FBR.rearrange("p (h g) -> p g h", g=16)[:, 1:16, :],
                NER[:, 16 * c + 1:16 * c + 16].unsqueeze(2).to_broadcast([1, 15, 8]), ALU.add))
            small[c] = T(lambda e: e.matmul(PS[7][:, 384:385], CBR, ONES[0:1, 0:1], start=True, stop=True), t_)
            key = KEY1[0:1, 16 * c:16 * c + 1]
            W(lambda e: e.tensor_scalar(OHR, IOTA[0:1, :], key, None, ALU.is_equal))
            ohr[c] = W(lambda e: e.tensor_scalar(OHN, IOTA[0:1, :], key, None, ALU.not_equal))

        def c6(c):
            W(lambda e: e.tensor_tensor(RW[:, 127:128], FV[:, 127:128], PS[7][:, 384:385], ALU.max), small[c])
            W(lambda e: e.tensor_copy(COLS[:, 2:3], RW[:, 127:128]))
            t_ = W(lambda e: e.tensor_tensor_scan(RW[:, 0:127][:, ::-1], BN[:, 1:128][:, ::-1], FV[:, 0:127][:, ::-1],
                                                   COLS[:, 2:3], ALU.add, ALU.max))
            big_v[c] = T(lambda e: e.transpose(PS[6][:, 256:384], RW, IDENT[:, :]), t_)
            small[c] = T(lambda e: e.matmul(PS[7][0:1, 392:400], RW[:, 0:1], IDENT[:, 0:8], start=True, stop=True))

        def c7(c):
            G_ = GRP[c % 3]
            t_ = W(lambda e: e.tensor_tensor(DCH, ECH[c % 2], PS[6][:, 256:384], ALU.subtract), small[c],
                   ex_t.get(c - 1))
            A(lambda e: e.activation(G_[:, :, 136:144], v8(PS[6][:, 256:384]), ACT.Copy), t_)
            ex_t[c] = A(lambda e: e.activation(G_[:, :, 128:136], v8(DCH), ACT.Exp))
            W(lambda e: e.tensor_tensor(DR, F17[(c - 1) % 2].rearrange("p (h g) -> p g h", g=17)[:, 16, :],
                                        PS[7][0:1, 392:400], ALU.subtract))
            dr_t[c] = W(lambda e: e.tensor_scalar(DR, DR, 0.0, None, ALU.min))
            ta = A(lambda e: e.activation(R18[:, 0:8], DR, ACT.Exp), dr_t[c])
            for h in range(2):
                T(lambda e, h=h: e.matmul(PS[7][:, 416 + 18 * h:434 + 18 * h], OHN[:, 128 * h:128 * h + 128],
                                          ONES[0:1, 0:18], start=True, stop=False), ta, ohr[c], dr_t[c])
                small[c] = T(lambda e, h=h: e.matmul(PS[7][:, 416 + 18 * h:434 + 18 * h], OHR[:, 128 * h:128 * h + 128],
                                                     R18, start=False, stop=True))

        def c8(c):
            fac[c] = W(lambda e: e.tensor_copy(ST[:, 576:612], PS[7][:, 416:452]), small[c], scw.get(c - 1))

        def rescale(c):
            t = 16 * c
            q.wait("v", vv())

            def go(e):
                wb["s"] = window(e, "v", WTAB1, t)
                a = RB[:, bass.ds(wb["s"] * 292, 292)].rearrange("p (b f) -> p b f", f=146)[:, :, 0:128]
                a = a.rearrange("p b (h k) -> p b h k", k=16)
                return e.tensor_tensor(a, a, F18[:, :, 0:8].unsqueeze(3).to_broadcast([128, 2, 8, 16]), ALU.mult)

            def go2(e):
                a = RB[:, bass.ds(wb["s"] * 292, 292)].rearrange("p (b f) -> p b f", f=146)[:, :, 128:146]
                return e.tensor_tensor(a, a, F18, ALU.mult)
            V(go, fac[c], adb.get(t - 1), z4)
            scw[c] = V(go2)

        def weigh(t):
            rows = rows_of(t)
            c = t // 16
            ohx[t] = A(lambda e: e.activation(OH[:, t % 3, :], OBR[:, t % 51, :], ACT.Copy), ohb1[t], mmb.get(t - 3))
            gx[t] = V(lambda e: e.tensor_tensor(
                rows[:, 0:128].rearrange("p (h c) -> p h c", c=16), rows[:, 0:128].rearrange("p (h c) -> p h c", c=16),
                rows[:, 128:136].unsqueeze(2).to_broadcast([128, 8, 16]), ALU.mult), gt1[t], ex_t[c])

        def apply1(t):
            rows = rows_of(t)
            for h in range(2):
                mmb[t] = T(lambda e, h=h: e.matmul(PS[t % 3][:, h * 146:(h + 1) * 146], OH[:, t % 3, h * 128:(h + 1) * 128],
                                                   rows, start=True, stop=True), gx[t], ohx[t], adb.get(t - 3), t_pre)

        def add_b(t):
            def go(e):
                w = wb["s"] if t % 16 == 0 else window(e, "v", WTAB1, t)
                sl = RB[:, bass.ds(w * 292, 292)]
                return e.tensor_tensor(sl, sl, PS[t % 3][:, 0:292], ALU.add)
            adb[t] = V(go, mmb[t], adb.get(t - 1), scw[t // 16] if t % 16 == 0 else None)

        steps = [(c0, 3), (c1, 4), (c2, 6), (c3, 8), (c4, 10), (c5, 12), (c6, 14), (c7, 16), (c8, 18)]
        LAG1 = 33
        for t in range(NL1 + LAG1 + 3):
            mark = len(q.items["v"])
            if t < NL1:
                gather1(t)
                onehot1(t)
            for fn, at_ in steps:
                c, r = divmod(t - 15 - at_, 16)
                if r == 0 and 0 <= c < NC1:
                    fn(c)
            if 0 <= t - 2 < NL1:
                look(t - 2)
            if 0 <= t - LAG1 - 2 < NL1 and (t - LAG1 - 2) % 16 == 0:
                rescale((t - LAG1 - 2) // 16)
            if 0 <= t - LAG1 + 1 < NL1:
                weigh(t - LAG1 + 1)
            if 0 <= t - LAG1 - 2 < NL1:
                add_b(t - LAG1 - 2)
            if 0 <= t - LAG1 < NL1:
                apply1(t - LAG1)
            q.merge("v", "w", mark)
        q.wait("v", q.now("w"))
        t_m = adb[NL1 - 1]
        t_xb = P(lambda e: e.tensor_tensor(XS[:, :, :], XS[:, :, :], BIAS1[:, :].unsqueeze(1).to_broadcast([128, NT, 128]),
                                           ALU.add), l_gb, t_m)

        SN = [SC1[:, 0:392], SC1[:, 400:792], SC2[:, 0:392], SC2[:, 400:792], RC[:, 1024:1416], WE0[:, 0:392], WE0[:, 400:792]]
        n8 = [s.rearrange("p (t h) -> p t h", h=8) for s in SN]
        CT = WE0[:, 800:849]
        HA = WE0[:, 849:896]
        SUMS, DEN, SM, DEG = AC1[:, 0:NT, 0:128], AC1[:, 0:NT, 128:136], AC1[:, 0:NT, 136:144], AC1[:, 0:NT, 144]
        CT2 = RC[:, 1416:1416 + NT]
        VC(lambda e: e.tensor_scalar(CT, DEG, 1.0, None, ALU.max), q.now("a"))
        VC(lambda e: e.reciprocal(RDEG[:, :], CT))
        VC(lambda e: e.tensor_scalar(CT, DEG, 1.0, None, ALU.min))
        VC(lambda e: e.tensor_scalar(CT, CT, -1.0, BIG, ALU.add, ALU.mult))

        def b8(v):
            return v.unsqueeze(2).to_broadcast([128, NT, 8])
        VC(lambda e: e.tensor_scalar(CT2, AC1[:, 0:NT, 145], 1.0, None, ALU.max))
        VC(lambda e: e.reciprocal(CT2, CT2))
        VC(lambda e: e.tensor_tensor(n8[0], SM, b8(CT2), ALU.mult))
        VC(lambda e: e.tensor_tensor(n8[0], n8[0], b8(CT), ALU.add))
        VC(lambda e: e.tensor_tensor(n8[1], HN[:, :, 128:136], HN[:, :, 136:144], ALU.add))
        VC(lambda e: e.scalar_tensor_tensor(out=SN[1], in0=SN[1], scalar=0.2, in1=SN[1], op0=ALU.mult, op1=ALU.max))
        VC(lambda e: e.tensor_tensor(SN[2], SN[0], SN[1], ALU.max))
        VC(lambda e: e.tensor_tensor(SN[0], SN[0], SN[2], ALU.subtract))
        VC(lambda e: e.tensor_tensor(SN[1], SN[1], SN[2], ALU.subtract))
        A(lambda e: e.activation(SN[3], SN[0], ACT.Exp), vv())
        t_ = A(lambda e: e.activation(SN[4], SN[1], ACT.Exp))
        VC(lambda e: e.tensor_tensor(n8[5], DEN, n8[3], ALU.mult), t_)
        VC(lambda e: e.tensor_tensor(SN[5], SN[5], SN[4], ALU.add))
        VC(lambda e: e.reciprocal(SN[6], SN[5]))
        VC(lambda e: e.tensor_tensor(SN[3], SN[3], SN[6], ALU.mult))
        VC(lambda e: e.tensor_tensor(SN[4], SN[4], SN[6], ALU.mult))

        def h16(v):
            return v.unsqueeze(2).to_broadcast([128, NT * 8, 16])

        S4 = SUMS.rearrange("p t (h c) -> p t h c", c=16)
        H4 = HN[:, :, 0:128].rearrange("p t (h c) -> p t h c", c=16)
        t_n = vv()

        def pre2(k0, k1):
            for t in range(k0, k1):
                hp = P(lambda e, t=t: e.tensor_tensor(
                    H4[:, t], H4[:, t], n8[4][:, t, :].unsqueeze(2).to_broadcast([128, 8, 16]), ALU.mult), t_n, d_g)
                V(lambda e, t=t: e.tensor_tensor(
                    S4[:, t], S4[:, t], n8[3][:, t, :].unsqueeze(2).to_broadcast([128, 8, 16]), ALU.mult), t_n)
            VC(lambda e: e.tensor_tensor(XS[:, k0:k1, :], XS[:, k0:k1, :], SUMS[:, k0:k1, :], ALU.add), t_xb)
            VC(lambda e: e.tensor_tensor(XS[:, k0:k1, :], XS[:, k0:k1, :], HN[:, k0:k1, 0:128], ALU.add), hp)

        WTR = [RC[:, k * 128:(k + 1) * 128] for k in range(6)]
        for k, iw in enumerate((iSS, iNE, iED, iDA, iCO, iSE)):
            m = T(lambda e, k=k, iw=iw: e.transpose(PS[4 + k // 4][:, (k % 4) * 128:(k % 4 + 1) * 128], WT[:, iw, :],
                                                    IDENT[:, :]), l_w[iw], t_n)
        V(lambda e: e.tensor_copy(RC[:, 0:512], PS[4][:, :]), m)
        t_wtr = V(lambda e: e.tensor_copy(RC[:, 512:768], PS[5][:, 0:256]))
        HT = RA[:, 0:NP]
        tr, ht = transposer(HT, t_wtr)
        tab_tok = []

        def post2(k0, k1, toks):
            tr(k0, k1, toks)
            tab_tok.append(relu_rows(TAB2, s_m[13], k0, k1))
        norm_pipe(pre2, post2)
        ht = list(ht.values())
        d_t2 = tab_tok[-1]
        AG = RB[:, 0:NW * WN]
        z5 = V(lambda e: e.memset(AG, 0.0), vv())
        ATC = HN[:, :, :].rearrange("p a b -> p (a b)")[:, 0:NW * WN]
        NM = ATC[:, 0:NP].rearrange("p (t d) -> p t d", d=128)
        l_at = q.dma("s", s_m[14], lambda e: e.dma_start(ATC, ATTD), d_att, d_t2)
        cst("t", c_ones, l_b1)
        evn = {}

        def own_term(t):
            if t % 16 != 8 or t // 16 >= NT:
                return None
            k = t // 16
            sl = slice(k * 128, (k + 1) * 128)
            m0 = T(lambda e: e.matmul(PS[4][:, 0:128], ATC[:, sl], WTR[2], start=True, stop=True), l_at, evn.get(k - 1))
            T(lambda e: e.matmul(PS[5][:, 0:128], RA[:, sl], WTR[0], start=True, stop=False))
            m1_ = T(lambda e: e.matmul(PS[5][:, 0:128], ONES[0:1, :], ROWS[0:1, 0:128], start=False, stop=True))
            V(lambda e: e.tensor_scalar(NM[:, k, :], PS[4][:, 0:128], RDEG[:, k:k + 1], None, ALU.mult), m0, m1_)
            evn[k] = VC(lambda e: e.tensor_tensor(NM[:, k, :], NM[:, k, :], PS[5][:, 0:128], ALU.add))
            return None
        t_ag = run_gather(AG, WTAB1, TAB2, IDX1, KEY1, None, [d_t2, z5, t_wtr, ht], extra=own_term)

        evo = {}

        mt3 = {}

        def pre3_t(k0, k1):
            for k in range(k0, k1):
                g = k // 4
                mt3[k] = T(lambda e, k=k, g=g: e.matmul(PS[4 + g % 2][:, (k % 4) * 128:(k % 4 + 1) * 128],
                                                        AG[:, k * 128:(k + 1) * 128], WTR[1], start=True, stop=True),
                           t_ag, evn[NT - 1], evo.get(4 * (g - 2) + 3))

        def pre3(k0, k1):
            for k in range(k0, k1):
                g = k // 4
                tmp_ = OH[:, k % 4, 0:128]
                tm_[k] = V(lambda e, k=k, g=g, tmp_=tmp_: e.scalar_tensor_tensor(
                    out=tmp_, in0=PS[4 + g % 2][:, (k % 4) * 128:(k % 4 + 1) * 128], scalar=RDEG[:, k:k + 1],
                    in1=NM[:, k, :], op0=ALU.mult, op1=ALU.add), mt3[min(4 * g + 3, k1 - 1)], evo.get(k - 4))
                if k > k0:
                    relu3(k - 1)
            relu3(k1 - 1)

        def relu3(k):
            tmp_ = OH[:, k % 4, 0:128]
            evo[k] = V(lambda e: e.scalar_tensor_tensor(
                out=XS[:, k, :], in0=tmp_, scalar=0.0, in1=XS[:, k, :], op0=ALU.max, op1=ALU.add), tm_[k])
        tm_ = {}

        tr, ht = transposer(HT)
        cst("t", l_b2, l_b3, l_b4)
        ev = {}
        T3v = TAB3.rearrange("(t p k) d -> p t (k d)", p=128, k=2)
        stage = [RC[:, 768 + 2048 * k:768 + 2048 * (k + 1)].rearrange("p (a b) -> p a b", b=256) for k in range(2)]
        dg = {}

        def post3(k0, k1, toks):
            tr(k0, k1, toks)
            g = k0 // 8
            for k in range(k0, k1):
                bank = PS[k % 4]
                T(lambda e, k=k, bank=bank: e.matmul(bank[:, 0:256], RA[:, k * 128:(k + 1) * 128], RC[:, 3 * 128:5 * 128],
                                                     start=True, stop=False), ht[k], ev.get(k - 4))
                m_ = T(lambda e, bank=bank: e.matmul(bank[:, 0:256], ONES[0:1, :], ROWS[0:1, 128:384],
                                                     start=False, stop=True))
                ev[k] = A(lambda e, k=k, bank=bank: e.activation(stage[g % 2][:, k - k0, :], bank[:, 0:256], ACT.Copy),
                          m_, dg.get(g - 2))
            dg[g] = q.dma("s", s_m[16 + g % 2], lambda e: e.dma_start(T3v[:, k0:k1, :], stage[g % 2][:, 0:k1 - k0, :]),
                          ev[k1 - 1])
        norm_pipe(pre3, post3, pre_t=pre3_t)
        t_x3 = evo[NT - 1]
        l_bs = q.dma("s", s_in[37], lambda e: e.dma_start(COLS[:, 15:16], b_self.rearrange("(p k) -> p k", k=1)), t_x3)
        z7 = V(lambda e: e.memset(RB[:, NP:NW * WN], 0.0), vv())
        ev2 = {}
        for g in range(13):
            c0_, c1_ = 512 * g, min(512 * g + 512, NP)
            bank = PS[4 + g % 4]
            m = T(lambda e, c0_=c0_, c1_=c1_, bank=bank: e.matmul(
                bank[:, 0:c1_ - c0_], WTR[5], RA[:, c0_:c1_], start=True, stop=True), ev2.get(g - 4), t_x3,
                ht[NT - 1], [ev[k] for k in range(NT - 8, NT)])
            ev2[g] = A(lambda e, c0_=c0_, c1_=c1_, bank=bank: e.activation(
                AG[:, c0_:c1_], bank[:, 0:c1_ - c0_], ACT.Identity, bias=COLS[:, 15:16]), m, l_bs)
        l_i3 = q.dma("s", s_in[34], lambda e: e.dma_start(IDX0[:, :], I3D), d_i3, t_x3)
        q.wait("v", z7, ev2[12])
        t_ag = run_gather(AG, WTAB1, TAB3, IDX0, KEY1, None, [dg[5], dg[6], l_i3])
        evo = {}
        outs = []
        for t in range(NT):
            def node4(t=t):
                bank = PS[t % 4]
                sl = slice(t * 128, (t + 1) * 128)
                m_ = T(lambda e: e.transpose(bank[:, 0:128], AG[:, sl], IDENT[:, :]), t_ag, evo.get(t - 4))
                evo[t] = V(lambda e: e.scalar_tensor_tensor(out=XS[:, t, :], in0=bank[:, 0:128], scalar=0.0,
                                                            in1=XS[:, t, :], op0=ALU.max, op1=ALU.add), m_)
            node4()
            if t % 8 == 7:
                a = t - 7
                outs.append(q.dma("s", s_fin, lambda e, a=a: e.dma_start(
                    out[a * 128:(a + 8) * 128, :].rearrange("(t p) d -> p t d", p=128), XS[:, a:a + 8, :]), evo[t]))
        outs.append(q.dma("s", s_fin, lambda e: e.dma_start(out[48 * 128:N, :], XS[0:N - 48 * 128, NT - 1, :]), evo[NT - 1]))
        q.wait("s", outs[-1])

        block = ctx.enter_context(nc.Block())

        @block.sync
        def _(e):
            for it in q.items["s"]:
                it(e)

        @block.gpsimd
        def _(e):
            for it in q.items["p"]:
                it(e)

        @block.scalar
        def _(e):
            for it in q.items["a"]:
                it(e)

        @block.tensor
        def _(e):
            for it in q.items["t"]:
                it(e)

        @block.vector
        def _(e):
            for it in q.items["v"]:
                it(e)


_INS = ['x', 'src', 'dst', 'edge_attr_128', 'edge_type_2', 'edge_type_200', 'L0_gnn_W1', 'L0_gnn_W2', 'L0_gnn_W3',
        'L0_gnn_re_attention_weight', 'L0_gnn_u', 'L0_gnn_en_weight', 'L0_gnn_re_weight',
        'L0_gnn_re_specific_attention', 'L1_gnn_W', 'L1_gnn_att_src', 'L1_gnn_att_dst', 'L1_gnn_bias',
        'L2_gnn_w_self_W', 'L2_gnn_w_self_b', 'L2_gnn_w_nei_W', 'L2_gnn_w_edge_W', 'L3_gnn_W_data', 'L3_gnn_b_data',
        'L3_gnn_W_control', 'L3_gnn_b_control', 'L3_gnn_W_self', 'L3_gnn_b_self']
_OUTS = [((6250, 128), 'float32')]


def kernel(**inputs):
    import numpy as _np
    import concourse.bacc as _bacc
    from concourse import mybir as _mybir
    from concourse.bass_utils import run_bass_kernel_spmd as _run

    nc = _bacc.Bacc("TRN2", target_bir_lowering=False, num_devices=1)
    arrays, args = {}, []
    for name in _INS:
        a = _np.ascontiguousarray(inputs[name])
        arrays[f"in_{name}_dram"] = a
        args.append(nc.dram_tensor(f"in_{name}_dram", a.shape, _mybir.dt.from_np(a.dtype), kind="ExternalInput").ap())
    for i, (shape, dtype) in enumerate(_OUTS):
        dt = _mybir.dt.from_np(_np.dtype(dtype))
        args.append(nc.dram_tensor(f"out_{i}_dram", shape, dt, kind="ExternalOutput").ap())
    program(nc, *args)
    r = _run(nc, [arrays], core_ids=[0])
    return r.results[0]["out_0_dram"]
```
